# Optimizing a Trainium2 kernel written in Bass

```python
import numpy as np
import jax
import jax.numpy as jnp

def _softmax(x, axis=-1):
    return jax.nn.softmax(x, axis=axis)

def _gelu(x):
    return jax.nn.gelu(x, approximate=True)

def _silu(x):
    return jax.nn.silu(x)

def _sigmoid(x):
    return jax.nn.sigmoid(x)

def _layernorm(x, axis=-1, eps=1e-05):
    m = jnp.mean(x, axis=axis, keepdims=True)
    v = jnp.var(x, axis=axis, keepdims=True)
    return (x - m) / jnp.sqrt(v + eps)

def _scatter_add(tgt, idx, src, axis=0):
    return tgt.at[idx].add(src)

def _segment_sum(src, seg, n):
    return jax.ops.segment_sum(src, seg, n)
kernel_name = 'mk_gnn_preln_d4_gnn_r8_b00188'

def setup_inputs(seed: int=0):
    np.random.seed(seed)
    _w = jnp.asarray

    def _rec_inputs():
        import jax
        import jax.numpy as jnp
        _gk = jax.random.key(seed)
        x = -0.0005121 + 1.001 * jax.random.normal(jax.random.fold_in(_gk, 1), (6250, 64), jnp.float32)
        src = jax.random.randint(jax.random.fold_in(_gk, 2), (200000,), 0, 6250, jnp.int32)
        dst = jnp.minimum((6250 * jax.random.uniform(jax.random.fold_in(_gk, 3), (200000,)) ** 2.0).astype(jnp.int32), 49999)
        _o = jnp.argsort(dst, stable=True)
        src = src[_o]
        dst = dst[_o]
        edge_attr_64 = -5.3897e-05 + 0.999841 * jax.random.normal(jax.random.fold_in(_gk, 13), (200000, 64), jnp.float32)
        edge_type_24 = jax.random.randint(jax.random.fold_in(_gk, 15), (200000,), 0, 24, jnp.int32)
        return (x, src, dst, edge_attr_64, edge_type_24)
    x, src, dst, edge_attr_64, edge_type_24 = _rec_inputs()

    def _L0_gnn_setup():
        import jax, jax.numpy as jnp
        import numpy as np
        N_NODES = 6250
        N_EDGES = 50000
        DIM = 64
        HEADS = 4
        BN_EPS = 1e-05

        def glorot(key, shape, fan_in, fan_out):
            std = np.sqrt(6.0 / (fan_in + fan_out))
            return jax.random.uniform(key, shape, jnp.float32, -std, std)

        def segment_softmax(a, seg, num_segments):
            m = jax.ops.segment_max(a, seg, num_segments=num_segments)
            e = jnp.exp(a - m[seg])
            s = jax.ops.segment_sum(e, seg, num_segments=num_segments)
            return e / (s[seg] + 1e-16)
        key = jax.random.key(seed)
        ks = jax.random.split(key, 6)
        x = jax.random.normal(ks[0], (N_NODES, DIM), jnp.float32)
        edge_attr = jax.random.normal(ks[1], (N_EDGES, DIM), jnp.float32)
        edge_index = jax.random.randint(ks[2], (2, N_EDGES), 0, N_NODES, jnp.int64)
        W = glorot(ks[3], (2 * DIM, HEADS * DIM), 2 * DIM, HEADS * DIM)
        att = glorot(ks[4], (1, HEADS, 2 * DIM), 2 * DIM, 1)
        bias = jnp.zeros((DIM,), jnp.float32)
        bn_gamma = jnp.ones((HEADS,), jnp.float32)
        bn_beta = jnp.zeros((HEADS,), jnp.float32)
        return {'x': x, 'edge_attr': edge_attr, 'W': W, 'att': att, 'bias': bias, 'bn_gamma': bn_gamma, 'bn_beta': bn_beta, 'edge_index': edge_index}
    _L0_gnn_all = _L0_gnn_setup()
    _L0_gnn_in = {k: v for k, v in _L0_gnn_all.items() if k in ('W', 'att', 'bias', 'bn_gamma', 'bn_beta')}
    del _L0_gnn_all

    def _L1_gnn_setup():
        import jax, jax.numpy as jnp
        import numpy as np
        N_NODES = 12500
        key = jax.random.key(seed)
        k1, k2 = jax.random.split(key)
        x = jax.random.normal(k1, (N_NODES, 64), dtype=jnp.float32)
        edge_index = jax.random.randint(k2, (2, 200000), 0, N_NODES, dtype=jnp.int64)
        return {'x': x, 'edge_index': edge_index}
    _L1_gnn_all = _L1_gnn_setup()
    _L1_gnn_in = {k: v for k, v in _L1_gnn_all.items() if k in ()}
    del _L1_gnn_all

    def _L2_gnn_setup():
        import jax, jax.numpy as jnp
        import numpy as np
        N_NODES = 12500
        N_EDGES = 150000
        HDIM = 64
        NUM_RELS = 24

        def _rel_graph_conv(h, src, dst, rel, W):
            n = h.shape[0]
            hw = jnp.einsum('nd,rdh->nrh', h, W)
            msgs = hw[src, rel]
            agg = jax.ops.segment_sum(msgs, dst, num_segments=n)
            deg = jax.ops.segment_sum(jnp.ones((src.shape[0],), h.dtype), dst, num_segments=n)
            agg = agg / jnp.maximum(deg, 1.0)[:, None]
            return jax.nn.relu(agg)
        key = jax.random.key(seed)
        k1, k2, k3, k4, k5, k6 = jax.random.split(key, 6)
        scale = 1.0 / np.sqrt(HDIM)
        return {'h': jax.random.normal(k1, (N_NODES, HDIM), dtype=jnp.float32), 'src': jax.random.randint(k2, (N_EDGES,), 0, N_NODES, dtype=jnp.int64) if jax.config.jax_enable_x64 else jax.random.randint(k2, (N_EDGES,), 0, N_NODES, dtype=jnp.int32), 'dst': jax.random.randint(k3, (N_EDGES,), 0, N_NODES, dtype=jnp.int32), 'rel': jax.random.randint(k4, (N_EDGES,), 0, NUM_RELS, dtype=jnp.int32), 'W1': jax.random.normal(k5, (NUM_RELS, HDIM, HDIM), dtype=jnp.float32) * scale, 'W2': jax.random.normal(k6, (NUM_RELS, HDIM, HDIM), dtype=jnp.float32) * scale}
    _L2_gnn_all = _L2_gnn_setup()
    _L2_gnn_in = {k: v for k, v in _L2_gnn_all.items() if k in ('W1', 'W2')}
    del _L2_gnn_all

    def _L3_gnn_setup():
        import jax, jax.numpy as jnp
        import numpy as np
        N = 8192
        E = 131072
        DIN = 64
        DOUT = 64

        def _linear(x, W, b):
            return x @ W.T + b

        def _mean_agg(h, norm, src, dst, n_nodes):
            msg = (h * norm)[src]
            summed = jax.ops.segment_sum(msg, dst, num_segments=n_nodes)
            deg = jax.ops.segment_sum(jnp.ones((dst.shape[0],), h.dtype), dst, num_segments=n_nodes)
            return summed / jnp.maximum(deg, 1.0)[:, None]
        key = jax.random.key(seed)
        ks = jax.random.split(key, 16)
        inp = {'feat': jax.random.normal(ks[0], (N, DIN), dtype=jnp.float32), 'norm': jax.random.uniform(ks[1], (N, 1), dtype=jnp.float32), 'src': jax.random.randint(ks[2], (E,), 0, N, dtype=jnp.int32), 'dst': jax.random.randint(ks[3], (E,), 0, N, dtype=jnp.int32)}
        s = 0.05
        inp['W_self'] = jax.random.normal(ks[4], (DOUT, DIN)) * s
        inp['b_self'] = jnp.zeros((DOUT,), jnp.float32)
        inp['W_self_high'] = jax.random.normal(ks[5], (DOUT, DIN)) * s
        inp['b_self_high'] = jnp.zeros((DOUT,), jnp.float32)
        inp['W_neigh'] = jax.random.normal(ks[6], (DOUT, DIN)) * s
        inp['b_neigh'] = jnp.zeros((DOUT,), jnp.float32)
        inp['W_neigh_high'] = jax.random.normal(ks[7], (DOUT, DIN)) * s
        inp['b_neigh_high'] = jnp.zeros((DOUT,), jnp.float32)
        inp['W_id'] = jax.random.normal(ks[8], (DOUT, DIN)) * s
        inp['b_id'] = jnp.zeros((DOUT,), jnp.float32)
        inp['w_att_low'] = jax.random.normal(ks[9], (1, DOUT)) * s
        inp['w_att_high'] = jax.random.normal(ks[10], (1, DOUT)) * s
        inp['w_att_mlp'] = jax.random.normal(ks[11], (1, DOUT)) * s
        inp['W_att'] = jax.random.normal(ks[12], (3, 3)) * s
        return inp
    _L3_gnn_all = _L3_gnn_setup()
    _L3_gnn_in = {k: v for k, v in _L3_gnn_all.items() if k in ('W_self', 'b_self', 'W_self_high', 'b_self_high', 'W_neigh', 'b_neigh', 'W_neigh_high', 'b_neigh_high', 'W_id', 'b_id', 'w_att_low', 'w_att_high', 'w_att_mlp', 'W_att')}
    del _L3_gnn_all
    return {'x': x, 'src': src, 'dst': dst, 'edge_attr_64': edge_attr_64, 'edge_type_24': edge_type_24, 'L0_gnn_W': _L0_gnn_in['W'], 'L0_gnn_att': _L0_gnn_in['att'], 'L0_gnn_bias': _L0_gnn_in['bias'], 'L0_gnn_bn_gamma': _L0_gnn_in['bn_gamma'], 'L0_gnn_bn_beta': _L0_gnn_in['bn_beta'], 'L2_gnn_W1': _L2_gnn_in['W1'], 'L2_gnn_W2': _L2_gnn_in['W2'], 'L3_gnn_W_self': _L3_gnn_in['W_self'], 'L3_gnn_b_self': _L3_gnn_in['b_self'], 'L3_gnn_W_self_high': _L3_gnn_in['W_self_high'], 'L3_gnn_b_self_high': _L3_gnn_in['b_self_high'], 'L3_gnn_W_neigh': _L3_gnn_in['W_neigh'], 'L3_gnn_b_neigh': _L3_gnn_in['b_neigh'], 'L3_gnn_W_neigh_high': _L3_gnn_in['W_neigh_high'], 'L3_gnn_b_neigh_high': _L3_gnn_in['b_neigh_high'], 'L3_gnn_W_id': _L3_gnn_in['W_id'], 'L3_gnn_b_id': _L3_gnn_in['b_id'], 'L3_gnn_w_att_low': _L3_gnn_in['w_att_low'], 'L3_gnn_w_att_high': _L3_gnn_in['w_att_high'], 'L3_gnn_w_att_mlp': _L3_gnn_in['w_att_mlp'], 'L3_gnn_W_att': _L3_gnn_in['W_att']}

def reference(x, src, dst, edge_attr_64, edge_type_24, L0_gnn_W, L0_gnn_att, L0_gnn_bias, L0_gnn_bn_gamma, L0_gnn_bn_beta, L2_gnn_W1, L2_gnn_W2, L3_gnn_W_self, L3_gnn_b_self, L3_gnn_W_self_high, L3_gnn_b_self_high, L3_gnn_W_neigh, L3_gnn_b_neigh, L3_gnn_W_neigh_high, L3_gnn_b_neigh_high, L3_gnn_W_id, L3_gnn_b_id, L3_gnn_w_att_low, L3_gnn_w_att_high, L3_gnn_w_att_mlp, L3_gnn_W_att):
    import jax
    import jax.numpy as jnp

    def _L0_gnn_ref(x, edge_attr, W, att, bias, bn_gamma, bn_beta, edge_index):
        import jax, jax.numpy as jnp
        import numpy as np
        N_NODES = 6250
        N_EDGES = 50000
        DIM = 64
        HEADS = 4
        BN_EPS = 1e-05

        def glorot(key, shape, fan_in, fan_out):
            std = np.sqrt(6.0 / (fan_in + fan_out))
            return jax.random.uniform(key, shape, jnp.float32, -std, std)

        def segment_softmax(a, seg, num_segments):
            m = jax.ops.segment_max(a, seg, num_segments=num_segments)
            e = jnp.exp(a - m[seg])
            s = jax.ops.segment_sum(e, seg, num_segments=num_segments)
            return e / (s[seg] + 1e-16)
        act = jax.nn.softplus
        i, j = (edge_index[0], edge_index[1])
        x_i = x[i]
        x_j = x[j]
        out_i = act(jnp.concatenate([x_i, edge_attr], -1) @ W).reshape(-1, HEADS, DIM)
        out_j = act(jnp.concatenate([x_j, edge_attr], -1) @ W).reshape(-1, HEADS, DIM)
        alpha = act((jnp.concatenate([out_i, out_j], -1) * att).sum(-1))
        mu = alpha.mean(0)
        var = alpha.var(0)
        alpha = (alpha - mu) * jax.lax.rsqrt(var + BN_EPS) * bn_gamma + bn_beta
        alpha = act(alpha)
        alpha = segment_softmax(alpha, i, N_NODES)
        msg = out_j * alpha[:, :, None]
        aggr = jax.ops.segment_sum(msg, i, num_segments=N_NODES)
        out = aggr.mean(1) + bias
        return out

    def _L1_gnn_ref(x, edge_index):
        import jax, jax.numpy as jnp
        import numpy as np
        N_NODES = 12500
        src, dst = (edge_index[0], edge_index[1])
        msgs = x[src]
        out = jax.ops.segment_sum(msgs, dst, num_segments=x.shape[0])
        return out

    def _L2_gnn_ref(h, src, dst, rel, W1, W2):
        import jax, jax.numpy as jnp
        import numpy as np
        N_NODES = 12500
        N_EDGES = 150000
        HDIM = 64
        NUM_RELS = 24

        def _rel_graph_conv(h, src, dst, rel, W):
            n = h.shape[0]
            hw = jnp.einsum('nd,rdh->nrh', h, W)
            msgs = hw[src, rel]
            agg = jax.ops.segment_sum(msgs, dst, num_segments=n)
            deg = jax.ops.segment_sum(jnp.ones((src.shape[0],), h.dtype), dst, num_segments=n)
            agg = agg / jnp.maximum(deg, 1.0)[:, None]
            return jax.nn.relu(agg)
        h = _rel_graph_conv(h, src, dst, rel, W1)
        h = _rel_graph_conv(h, src, dst, rel, W2)
        return h

    def _L3_gnn_ref(feat, norm, src, dst, W_self, b_self, W_self_high, b_self_high, W_neigh, b_neigh, W_neigh_high, b_neigh_high, W_id, b_id, w_att_low, w_att_high, w_att_mlp, W_att):
        import jax, jax.numpy as jnp
        import numpy as np
        N = 8192
        E = 131072
        DIN = 64
        DOUT = 64

        def _linear(x, W, b):
            return x @ W.T + b

        def _mean_agg(h, norm, src, dst, n_nodes):
            msg = (h * norm)[src]
            summed = jax.ops.segment_sum(msg, dst, num_segments=n_nodes)
            deg = jax.ops.segment_sum(jnp.ones((dst.shape[0],), h.dtype), dst, num_segments=n_nodes)
            return summed / jnp.maximum(deg, 1.0)[:, None]
        n = feat.shape[0]
        self_low = jax.nn.relu(_linear(feat, W_self, b_self))
        self_high = jax.nn.relu(_linear(feat, W_self_high, b_self_high))
        neigh_low = _mean_agg(jax.nn.relu(_linear(feat, W_neigh, b_neigh)), norm, src, dst, n)
        neigh_high = _mean_agg(jax.nn.relu(_linear(feat, W_neigh_high, b_neigh_high)), norm, src, dst, n)
        low = self_low + neigh_low
        high = self_high - neigh_high
        identity = jax.nn.relu(_linear(feat, W_id, b_id))
        logits = jnp.concatenate([low @ w_att_low.T, high @ w_att_high.T, identity @ w_att_mlp.T], axis=1)
        att = jax.nn.softmax(jax.nn.sigmoid(logits) @ W_att.T / 3.0, axis=1)
        rst = 3.0 * (att[:, 0:1] * low + att[:, 1:2] * high + att[:, 2:3] * identity)
        return rst
    edge_index = jnp.stack([src, dst])
    deg = jnp.maximum(jax.ops.segment_sum(jnp.ones(dst.shape, jnp.float32), dst, num_segments=6250), 1.0)
    deg_isqrt = deg ** (-0.5)
    h = jnp.maximum(_layernorm(x, axis=-1), 0.0)
    x = x + _L0_gnn_ref(h, edge_attr_64, L0_gnn_W, L0_gnn_att, L0_gnn_bias, L0_gnn_bn_gamma, L0_gnn_bn_beta, edge_index)
    h = jnp.maximum(_layernorm(x, axis=-1), 0.0)
    x = x + _L1_gnn_ref(h, edge_index)
    h = jnp.maximum(_layernorm(x, axis=-1), 0.0)
    x = x + _L2_gnn_ref(h, src, dst, edge_type_24, L2_gnn_W1, L2_gnn_W2)
    h = jnp.maximum(_layernorm(x, axis=-1), 0.0)
    x = x + _L3_gnn_ref(h, deg_isqrt[:, None], src, dst, L3_gnn_W_self, L3_gnn_b_self, L3_gnn_W_self_high, L3_gnn_b_self_high, L3_gnn_W_neigh, L3_gnn_b_neigh, L3_gnn_W_neigh_high, L3_gnn_b_neigh_high, L3_gnn_W_id, L3_gnn_b_id, L3_gnn_w_att_low, L3_gnn_w_att_high, L3_gnn_w_att_mlp, L3_gnn_W_att)
    return x

_drawn_inputs = setup_inputs


def setup_inputs(seed=0):
    import zlib

    import numpy as np

    out = dict(_drawn_inputs(seed))
    spreads = {'L0_gnn_bias': (0.0, 0.1),
     'L0_gnn_bn_gamma': (1.0, 0.6),
     'L0_gnn_bn_beta': (0.0, 2.0),
     'L3_gnn_b_self': (0.0, 2.0),
     'L3_gnn_b_self_high': (0.0, 2.0),
     'L3_gnn_b_neigh': (0.0, 2.0),
     'L3_gnn_b_neigh_high': (0.0, 2.0),
     'L3_gnn_b_id': (0.0, 2.0)}
    factors = {'edge_attr_64': 6.956,
     'L2_gnn_W1': 8.0,
     'L2_gnn_W2': 8.0,
     'L3_gnn_W_self': 7.73,
     'L3_gnn_W_self_high': 8.0,
     'L3_gnn_W_neigh': 55.611,
     'L3_gnn_W_neigh_high': 51.729,
     'L3_gnn_W_id': 7.682,
     'L3_gnn_w_att_low': 64.0,
     'L3_gnn_w_att_high': 64.0,
     'L3_gnn_w_att_mlp': 64.0,
     'L3_gnn_W_att': 64.0}
    for name, (base, spread) in spreads.items():
        noise = np.random.default_rng([zlib.crc32(name.encode()), seed]).standard_normal(out[name].shape)
        drawn = base * np.exp(spread * noise) if base else spread * noise
        out[name] = jnp.asarray(drawn.astype(out[name].dtype))
    for name, factor in factors.items():
        out[name] = (out[name] * factor).astype(out[name].dtype)
    return out
```

```python
from contextlib import ExitStack

import numpy as np

import concourse.bass as bass
from concourse import mybir
from concourse.alu_op_type import AluOpType as ALU

F32, BF16, I32, U32 = mybir.dt.float32, mybir.dt.bfloat16, mybir.dt.int32, mybir.dt.uint32
ACT = mybir.ActivationFunctionType
AX = mybir.AxisListType

N, E, D, HEADS, RELS = 6250, 200000, 64, 4, 24
P = 128
NB = 50
NBU = 49
G = 8
T = -(-E // (2 * G * P)) * 2 * G
EP = T * P
PAD_NODE = NBU * P - 1
W = -(-(T + NB) // (2 * G)) * 2 * G
WK = -(-(W + G) // P)
WP = WK * P
TC = 112
KC = T // TC
NPAD = NB * P
OUTJ, ROW = HEADS * D, 264
EPS = 1e-5
assert KC * TC == T and TC <= P


class Count:

    def __init__(self, nc, name):
        self.sem = nc.alloc_semaphore(name)
        self.base, self.off, self.loop, self.per = 0, 0, None, 0

    def up(self, ins, n=1):
        ins.then_inc(self.sem, n)
        self.off += n
        return ins

    def credit(self, eng, n):
        eng.sem_inc(self.sem, n)
        self.base += n


class Temporaries:

    def __init__(self, nc, *engines):
        self.nc, self.engines = nc, engines

    def __enter__(self):
        self.first = self.nc.next_id()

    def __exit__(self, *a):
        if a[0] is None:
            for eng in self.engines:
                for n in range(self.first, self.nc.next_id()):
                    self.free(f"{eng.engine.value}_tmp_{n}", eng.engine)

    def free(self, name, engine):
        try:
            known = self.nc.lookup_reg(name)
        except (KeyError, ValueError, AssertionError):
            return
        if known is not None and known.allocated:
            self.nc.free_register(bass.RegisterHandle(name=name, engine=engine))


def wait(eng, count, back=0):
    v = count.base + count.off - back
    if count.loop is None:
        eng.wait_ge(count.sem, v)
    else:
        count.loop.wait(eng, count, v)


class Loop:

    SCRATCH, made = 4, 0

    def __init__(self, nc, trips, per):
        self.nc, self.trips, self.per = nc, trips, per
        self.share, self.scratch, self.met, self.turn = {}, {}, {}, 0

    def new(self, eng):
        Loop.made += 1
        return eng.alloc_register(f"loop_r{Loop.made}")

    def wait(self, eng, count, v):
        if self.met.get((eng.engine, count), -1) >= v:
            return
        self.met[(eng.engine, count)] = v
        if (eng.engine, count.per) not in self.share:
            r = self.share[(eng.engine, count.per)] = self.new(eng)
            eng.reg_mul(r, self.it, count.per)
        if eng.engine not in self.scratch:
            self.scratch[eng.engine] = (eng, [self.new(eng) for _ in range(self.SCRATCH)])
        self.turn += 1
        r = self.scratch[eng.engine][1][self.turn % self.SCRATCH]
        eng.reg_add(r, self.share[(eng.engine, count.per)], v)
        eng.wait_ge(count.sem, r)

    def __enter__(self):
        self.fori = self.nc.Fori(0, self.trips)
        self.it = self.fori.__enter__()
        nc = self.nc
        self.temporaries = Temporaries(nc, nc.vector, nc.scalar, nc.tensor, nc.gpsimd, nc.sync)
        self.temporaries.__enter__()
        for c, n in self.per.items():
            c.base, c.off, c.loop, c.per = c.base + c.off, 0, self, n
        return self.it

    def __exit__(self, *a):
        r = self.fori.__exit__(*a)
        if a[0] is None:
            for c, n in self.per.items():
                assert c.off == n, (str(c.sem), c.off, n)
                c.base, c.off, c.loop = c.base + n * self.trips, 0, None
            for reg in [*self.share.values(), *(r for _, rs in self.scratch.values() for r in rs)]:
                self.nc.free_register(reg)
            self.temporaries.__exit__(None, None, None)
            for reg in self.it.val.handles:
                self.nc.free_register(reg)
        return r


class Chain:

    def __init__(self, nc, eng, name):
        self.eng, self.count = eng, Count(nc, name)

    def __call__(self, ins, n=1):
        self.count.up(ins, n)
        wait(self.eng, self.count)


class Mem:

    def __init__(self, nc, tag, side="left"):
        self.nc, self.tag, self.side, self.ctx = nc, tag, side, ExitStack()

    def __enter__(self):
        self.ctx.__enter__()
        return self

    def __exit__(self, *a):
        if a[0] is None:
            self.nc.all_engine_barrier()
        return self.ctx.__exit__(*a)

    def sb(self, name, shape, dt=F32):
        return self.ctx.enter_context(self.nc.sbuf_tensor(f"{self.tag}_{name}", shape, dt, side=self.side))

    def ps(self, name, shape, dt=F32):
        return self.ctx.enter_context(self.nc.psum_tensor(f"{self.tag}_{name}", shape, dt))


class Net:

    def __init__(self, nc, args):
        self.nc, self.a = nc, args
        self.dve = Chain(nc, nc.vector, "dve_chain")
        self.act = Chain(nc, nc.scalar, "act_chain")
        self.pe = Chain(nc, nc.tensor, "pe_chain")
        self.pool = Chain(nc, nc.gpsimd, "pool_chain")
        self.sp = Chain(nc, nc.sync, "sp_chain")
        self.dma = Chain(nc, nc.gpsimd, "indirect_chain")

    def load(self, out, in_):
        with self.nc.allow_non_contiguous_dma("index lists and transposed vectors, once"):
            self.sp(self.nc.sync.dma_start(out, in_), 16)

    def after(self, eng, *chains):
        for c in chains:
            wait(eng, c.count)


def make_constants(net, m):
    nc = net.nc
    net.iota_i = m.sb("iota_i", [P, P], I32)
    net.iota = m.sb("iota", [P, P])
    net.iota_b = m.sb("iota_b", [P, P], BF16)
    net.part = m.sb("part", [P, 1])
    net.ident = m.sb("ident", [P, P])
    net.ones = m.sb("ones", [P, P])
    part_i = m.sb("part_i", [P, 1], I32)
    net.pool(nc.gpsimd.iota(net.iota_i[:, :], [[1, P]], base=0, channel_multiplier=0))
    net.pool(nc.gpsimd.iota(part_i[:, :], [[1, 1]], base=0, channel_multiplier=1))
    net.after(nc.vector, net.pool)
    net.dve(nc.vector.memset(net.ones[:, :], 1.0))
    net.dve(nc.vector.tensor_copy(net.iota[:, :], net.iota_i[:, :]))
    net.dve(nc.vector.tensor_copy(net.iota_b[:, :], net.iota_i[:, :]))
    net.dve(nc.vector.tensor_copy(net.part[:, :], part_i[:, :]))
    net.dve(nc.vector.tensor_scalar(net.ident[:, :], net.iota[:, :], net.part[:, 0:1], None, ALU.is_equal))


def index_lists(net, m):
    nc, a = net.nc, net.a
    net.src_f = m.sb("src_f", [P, T])
    net.dst_f = m.sb("dst_f", [P, T])
    net.src_u = m.sb("src_u", [P, T + G], U32)
    net.dst_u = m.sb("dst_u", [P, T + G], U32)
    net.lo_b = m.sb("lo_b", [P, T], BF16)
    net.hi_b = m.sb("hi_b", [P, T], BF16)
    net.hi_f = m.sb("hi_f", [P, T])
    with Mem(nc, "il") as t:
        raw = t.sb("raw", [TC, KC, P], I32)
        low = t.sb("low", [TC, KC, P], I32)
        flt = t.sb("flt", [TC, KC, P])
        digit = t.sb("digit", [P, T], I32)
        tp = t.ps("tp", [P, 4, P])
        for name, f, u in (("src", net.src_f, net.src_u), ("dst", net.dst_f, net.dst_u)):
            net.after(nc.sync, net.dve)
            net.load(raw[:, :, :], a[name].rearrange("(k p e) -> p k e", p=TC, e=P))
            net.after(nc.vector, net.sp)
            if name == "src":
                net.dve(nc.vector.tensor_scalar(low[:, :, :], raw[:, :, :], P - 1, None, ALU.bitwise_and))
                net.dve(nc.vector.tensor_copy(flt[:, :, :], low[:, :, :]))
                net.after(nc.sync, net.dve)
                net.load(net.lo_d.rearrange("(k p e) -> p k e", p=TC, e=P), flt[:, :, :])
                net.after(nc.vector, net.sp)
            net.dve(nc.vector.tensor_copy(flt[:, :, :], raw[:, :, :]))
            for k0 in range(0, KC, 4):
                n = min(4, KC - k0)
                net.after(nc.tensor, net.dve)
                for k in range(n):
                    net.pe(nc.tensor.transpose(tp[:, k, 0:TC], flt[:, k0 + k, :], net.ident[0:TC, 0:TC]))
                net.after(nc.vector, net.pe)
                net.dve(nc.vector.tensor_copy(
                    f[:, k0 * TC:(k0 + n) * TC].rearrange("p (k c) -> p k c", k=n), tp[:, 0:n, 0:TC]))
            net.dve(nc.vector.memset(u[:, T:T + G], 0))
            net.dve(nc.vector.tensor_copy(u[:, 0:T], f[:, :]))
        for shift, out in ((False, net.lo_b), (True, net.hi_b)):
            op, val = (ALU.logical_shift_right, 7) if shift else (ALU.bitwise_and, P - 1)
            net.dve(nc.vector.tensor_scalar(digit[:, :], net.src_u[:, 0:T].bitcast(I32), val, None, op))
            net.dve(nc.vector.tensor_copy(out[:, :], digit[:, :]))
        net.dve(nc.vector.tensor_copy(net.hi_f[:, :], net.hi_b[:, :]))


def count_dst_blocks(net, m):
    nc = net.nc
    net.start_dst = m.sb("start_dst", [P, NB])
    with Mem(nc, "cb") as t:
        hit = t.sb("hit", [P, T])
        cnt = t.sb("cnt", [P, NB])
        tot = t.ps("tot", [P, NB])
        for b in range(NB):
            net.dve(nc.vector.tensor_scalar(hit[:, :], net.dst_f[:, :], float(P * b), 0.0, ALU.is_lt, ALU.add,
                                            accum_out=cnt[:, b:b + 1]))
        net.after(nc.tensor, net.dve)
        net.pe(nc.tensor.matmul(tot[:, :], net.ones[:, :], cnt[:, :], start=True, stop=True))
        net.after(nc.vector, net.pe)
        net.dve(nc.vector.tensor_copy(net.start_dst[:, :], tot[:, :]))


def histogram_src(net, m):
    nc = net.nc
    net.start_src = m.sb("start_src", [P, NB])
    net.first = m.sb("first", [P, NBU])
    GH = 16
    with Mem(nc, "hi") as t:
        oh_lo = [t.sb(f"oh_lo{q}", [P, GH, P], BF16) for q in range(2)]
        oh_hi = [t.sb(f"oh_hi{q}", [P, GH, NBU], BF16) for q in range(2)]
        zero = t.sb("zero", [P, P], BF16)
        lower = t.sb("lower", [P, P])
        counts = t.sb("counts", [P, NBU])
        hist = t.ps("hist", [P, NBU])
        ex = t.ps("ex", [P, NBU])
        tot = t.ps("tot", [P, NBU])
        made, used = Count(nc, "hist_onehots"), Count(nc, "hist_summed")
        net.dve(nc.vector.memset(zero[:, :], 0.0))
        net.dve(nc.vector.tensor_scalar(lower[:, :], net.iota[:, :], net.part[:, 0:1], None, ALU.is_gt))
        net.after(nc.tensor, net.dve)
        net.pe(nc.tensor.matmul(hist[:, :], zero[:, :], zero[:, 0:NBU], start=True, stop=False,
                                skip_group_check=True))
        used.credit(nc.tensor, 2)
        with Loop(nc, T // (2 * GH), {made: 4, used: 2}) as it:
            for q in range(2):
                c0 = (it * 2 + q) * GH
                wait(nc.vector, used, back=1)
                made.up(nc.vector.tensor_tensor(
                    oh_lo[q][:, :, :], net.iota_b[:, None, :].to_broadcast([P, GH, P]),
                    net.lo_b[:, bass.ds(c0, GH)].unsqueeze(2).to_broadcast([P, GH, P]), ALU.is_equal))
                made.up(nc.vector.tensor_tensor(
                    oh_hi[q][:, :, :], net.iota_b[:, None, 0:NBU].to_broadcast([P, GH, NBU]),
                    net.hi_b[:, bass.ds(c0, GH)].unsqueeze(2).to_broadcast([P, GH, NBU]), ALU.is_equal))
                wait(nc.tensor, made)
                for j in range(GH):
                    ins = nc.tensor.matmul(hist[:, :], oh_lo[q][:, j, :], oh_hi[q][:, j, :], start=False,
                                           stop=False, skip_group_check=True)
                used.up(ins)
        wait(nc.vector, used)
        net.dve(nc.vector.tensor_copy(counts[:, :], hist[:, :]))
        net.after(nc.tensor, net.dve)
        net.pe(nc.tensor.matmul(tot[:, :], net.ones[:, :], counts[:, :], start=True, stop=True))
        net.pe(nc.tensor.matmul(ex[:, :], lower[:, :], counts[:, :], start=True, stop=True))
        net.after(nc.vector, net.pe)
        net.dve(nc.vector.tensor_copy(counts[:, :], tot[:, :]))
        net.dve(nc.vector.memset(net.start_src[:, 0:1], 0.0))
        net.dve(nc.vector.tensor_tensor_scan(net.start_src[:, 1:NB], net.ones[:, 0:NBU], counts[:, :], 0.0,
                                             ALU.mult, ALU.add))
        net.dve(nc.vector.tensor_tensor(net.first[:, :], ex[:, :], net.start_src[:, 0:NBU], ALU.add))


def item_list(net, m, tag, start):
    nc = net.nc
    base128 = m.sb(f"{tag}_b128", [P, WK])
    tile_u = m.sb(f"{tag}_t", [P, WK], U32)
    with Mem(nc, tag) as t:
        si = t.sb("si", [P, NB], I32)
        fl = t.sb("fl", [P, NB])
        ce = t.sb("ce", [P, NB])
        n = t.sb("n", [P, NBU])
        c = t.sb("c", [P, NBU])
        g = t.sb("g", [P, NBU])
        dg = t.sb("dg", [P, NBU])
        s1 = t.sb("s1", [P, NBU])
        w_i = t.sb("w_i", [P, WK], I32)
        w = t.sb("w", [P, WK])
        bt = t.sb("bt", [P, WK, 2])
        v = nc.vector
        net.pool(nc.gpsimd.iota(w_i[:, :], [[P, WK]], base=0, channel_multiplier=1))
        net.after(v, net.pool)
        net.dve(v.tensor_copy(w[:, :], w_i[:, :]))
        net.dve(v.tensor_copy(si[:, :], start[:, :]))
        net.dve(v.tensor_scalar(si[:, :], si[:, :], 7, None, ALU.logical_shift_right))
        net.dve(v.tensor_copy(fl[:, :], si[:, :]))
        net.dve(v.tensor_scalar(ce[:, :], start[:, :], float(P - 1), None, ALU.add))
        net.dve(v.tensor_copy(si[:, :], ce[:, :]))
        net.dve(v.tensor_scalar(si[:, :], si[:, :], 7, None, ALU.logical_shift_right))
        net.dve(v.tensor_copy(ce[:, :], si[:, :]))
        net.dve(v.tensor_tensor(n[:, :], ce[:, 1:NB], fl[:, 0:NBU], ALU.subtract))
        net.dve(v.tensor_scalar(n[:, :], n[:, :], 1.0, None, ALU.max))
        net.dve(v.tensor_scalar(fl[:, :], fl[:, :], float(T - 1), None, ALU.min))
        net.dve(v.tensor_tensor_scan(c[:, :], net.ones[:, 0:NBU], n[:, :], 0.0, ALU.mult, ALU.add))
        net.dve(v.tensor_tensor(g[:, :], fl[:, 0:NBU], c[:, :], ALU.subtract))
        net.dve(v.tensor_tensor(g[:, :], g[:, :], n[:, :], ALU.add))
        net.dve(v.memset(dg[:, :], 0.0))
        net.dve(v.tensor_tensor(dg[:, 0:NBU - 1], g[:, 1:NBU], g[:, 0:NBU - 1], ALU.subtract))
        for k in range(WK):
            net.dve(v.scalar_tensor_tensor(s1[:, :], c[:, :], w[:, k:k + 1], net.ones[:, 0:NBU], ALU.is_le,
                                           ALU.mult, accum_out=bt[:, k, 0:1]))
            net.dve(v.scalar_tensor_tensor(s1[:, :], c[:, :], w[:, k:k + 1], dg[:, :], ALU.is_le,
                                           ALU.mult, accum_out=bt[:, k, 1:2]))
        net.dve(v.tensor_scalar(base128[:, :], bt[:, :, 0], float(P), None, ALU.mult))
        net.dve(v.tensor_tensor(w[:, :], w[:, :], bt[:, :, 1], ALU.add))
        net.dve(v.tensor_scalar(w[:, :], w[:, :], g[:, 0:1], float(T - 1), ALU.add, ALU.min))
        net.dve(v.tensor_copy(tile_u[:, :], w[:, :]))
    return base128, tile_u


def to_rows(net, m, tag, cols, dt, broadcast):
    nc = net.nc
    flat = nc.dram_tensor(f"{tag}_flat", [WP], dt).ap()
    row = m.sb(tag, [P if broadcast else 1, WP], dt)
    net.after(nc.sync, net.dve)
    net.load(flat.rearrange("(k p) -> p k", p=P), cols)
    net.load(row[:, :], flat.partition_broadcast(P) if broadcast else flat.rearrange("(a w) -> a w", a=1))
    return row


def item_tables(net, m):
    nc, a = net.nc, net.a
    v = nc.vector
    b128, tiles = item_list(net, m, "itd", net.start_dst)
    net.gsrc = m.sb("gsrc", [P, WP], U32)
    net.grel = m.sb("grel", [P, WP], U32)
    net.dloc = m.sb("dloc", [P, WP])
    with Mem(nc, "ix") as t:
        raw = [t.sb(f"raw{i}", [P, P], I32) for i in range(3)]
        flt = [t.sb(f"flt{i}", [P, P]) for i in range(3)]
        tp = t.ps("tp", [P, 3, P])
        bi = t.sb("bi", [P, WK], I32)
        net.dve(v.tensor_copy(bi[:, :], b128[:, :]))
        net.row_dst = to_rows(net, m, "row_dst", bi[:, :], I32, False)
        for k in range(WK):
            net.after(nc.gpsimd, net.dve)
            for i, name in enumerate(("src", "dst", "rel")):
                net.dma(nc.gpsimd.indirect_dma_start(
                    out=raw[i][:, :], out_offset=None, in_=a[name].rearrange("(t e) -> t e", e=P),
                    in_offset=bass.IndirectOffsetOnAxis(ap=tiles[:, k:k + 1], axis=0)), 16)
            net.after(v, net.dma, net.pe)
            for i in range(3):
                net.dve(v.tensor_copy(flt[i][:, :], raw[i][:, :]))
            net.dve(v.tensor_scalar(flt[1][:, :], flt[1][:, :], b128[:, k:k + 1], None, ALU.subtract))
            net.dve(v.scalar_tensor_tensor(flt[2][:, :], flt[0][:, :], float(RELS), flt[2][:, :], ALU.mult,
                                           ALU.add))
            net.after(nc.tensor, net.dve)
            for i in range(3):
                net.pe(nc.tensor.transpose(tp[:, i, :], flt[i][:, :], net.ident[:, :]))
            net.after(v, net.pe)
            for i, out in enumerate((net.gsrc, net.dloc, net.grel)):
                net.dve(v.tensor_copy(out[:, k * P:(k + 1) * P], tp[:, i, :]))


def node_view(ap):
    return ap.rearrange("(b p) d -> p b d", p=P)


def layer_norm(net, m, dest):
    nc, v, x = net.nc, net.nc.vector, net.x
    h = m.sb("h", [P, NB, D])
    sq = m.sb("sq", [P, NB, D])
    mean = m.sb("mean", [P, NB])
    var = m.sb("var", [P, NB])
    bc = lambda s: s[:, :].unsqueeze(2).to_broadcast([P, NB, D])
    net.dve(v.tensor_reduce(mean[:, :], x[:, :, :], AX.X, ALU.add))
    net.dve(v.tensor_scalar(mean[:, :], mean[:, :], 1.0 / D, None, ALU.mult))
    net.dve(v.tensor_tensor(h[:, :, :], x[:, :, :], bc(mean), ALU.subtract))
    net.dve(v.tensor_tensor(sq[:, :, :], h[:, :, :], h[:, :, :], ALU.mult))
    net.dve(v.tensor_reduce(var[:, :], sq[:, :, :], AX.X, ALU.add))
    net.dve(v.tensor_scalar(var[:, :], var[:, :], 1.0 / D, EPS, ALU.mult, ALU.add))
    net.after(nc.scalar, net.dve)
    net.act(nc.scalar.activation(var[:, :], var[:, :], ACT.Sqrt))
    net.after(v, net.act)
    net.dve(v.reciprocal(var[:, :], var[:, :]))
    net.dve(v.tensor_tensor(h[:, :, :], h[:, :, :], bc(var), ALU.mult))
    net.dve(v.tensor_scalar(h[:, :, :], h[:, :, :], 0.0, None, ALU.max))
    if dest is not None:
        net.after(nc.sync, net.dve)
        net.load(node_view(dest), h[:, :, :])
    return h


def edge_pass(net, e):
    nc, a = net.nc, net.a
    v, s, pe, pool, sp = nc.vector, nc.scalar, nc.tensor, nc.gpsimd, nc.sync
    GP = G * P
    two = range(2)
    w_i = e.sb("w_i", [P, OUTJ])
    w_j = e.sb("w_j", [P, OUTJ])
    att = e.sb("att", [P, 2 * OUTJ])
    before = e.sb("before", [P, P])
    gath = [e.sb(f"gath{q}", [P, G, P]) for q in two]
    in_i = [e.sb(f"in_i{q}", [P, GP]) for q in two]
    in_j = [e.sb(f"in_j{q}", [P, GP]) for q in two]
    srow = [e.sb(f"srow{q}", [P, GP], I32) for q in two]
    lrow = [e.sb(f"lrow{q}", [P, GP]) for q in two]
    oh_lo = [e.sb(f"oh_lo{q}", [P, G, P], BF16) for q in two]
    oh_hi = [e.sb(f"oh_hi{q}", [P, G, NBU], BF16) for q in two]
    oh_loT = [e.sb(f"oh_loT{q}", [P, GP]) for q in two]
    idx_s = [e.sb(f"idx_s{q}", [P, G], U32) for q in two]
    idx_d = [e.sb(f"idx_d{q}", [P, G], U32) for q in two]
    rows = [e.sb(f"rows{q}", [P, G, OUTJ + ROW]) for q in two]
    soft = [e.sb(f"soft{q}", [P, 2 * 2 * OUTJ]) for q in two]
    prod = [e.sb(f"prod{q}", [P, 2 * 2 * OUTJ]) for q in two]
    dots = [e.sb(f"dots{q}", [P, G, 2 * HEADS]) for q in two]
    upto = [e.sb(f"upto{q}", [P, NBU]) for q in two]
    junk_r = e.sb("junk_r", [P, G, P], BF16)
    pick = e.sb("pick", [P, G, NBU])
    rank = [e.sb(f"rank{q}", [P, G]) for q in two]
    base = [e.sb(f"base{q}", [P, G]) for q in two]
    src_g = [e.sb(f"src_g{q}", [P, G]) for q in two]
    hi_g = [e.sb(f"hi_g{q}", [P, G]) for q in two]
    place = [e.sb(f"place{q}", [P, G], U32) for q in two]
    tp = e.ps("tp", [P, 4, P])
    z = [e.ps(f"z{q}", [P, 2, 2 * OUTJ]) for q in two]
    at = [e.ps(f"at{q}", [P, G, D]) for q in two]
    nxt = e.ps("nxt", [P, NBU])

    net.load(w_i[:, :], a["W"])
    net.load(w_j[0:D, :], a["W"][D:2 * D, :])
    net.load(w_j[D:2 * D, :], a["W"][0:D, :])
    for half in two:
        net.load(att[:, half * OUTJ:(half + 1) * OUTJ].rearrange("p (h d) -> p h d", h=HEADS),
                 a["att"][:, half * D:(half + 1) * D].partition_broadcast(P))
    net.dve(v.tensor_scalar(before[:, :], net.iota[:, :], net.part[:, 0:1], None, ALU.is_lt))
    net.dve(v.memset(prod[0][:, 0:3 * G], 0.0))
    net.after(pe, net.dve, net.sp)
    net.after(v, net.sp)
    net.pe(pe.matmul(nxt[:, :], net.ident[:, :], net.first[:, :], start=True, stop=False, skip_group_check=True))

    c = lambda name: Count(nc, "edge_" + name)
    indexed, gathered = c("indexed"), [c(f"gathered{q}") for q in two]
    loaded_e, loaded_s = [c(f"loaded_e{q}") for q in two], [c(f"loaded_s{q}") for q in two]
    turned, copied = c("turned"), c("copied")
    z_done = c("z_done")
    abs_done, exp_done, ln_done = c("abs_done"), c("exp_done"), c("ln_done")
    soft_done, prod_done, dot_done = c("soft_done"), c("prod_done"), c("dot_done")
    picked = c("picked")
    onehots, ranked, saved, moved, based = c("onehots"), c("ranked"), c("saved"), c("moved"), c("based")
    place_read, rows_done = c("place_read"), c("rows_done")
    scattered = [c(f"scattered{q}") for q in two]

    def gather(c0, q):
        wait(pool, turned, back=2)
        indexed.up(pool.tensor_copy(idx_s[q][:, :], net.src_u[:, bass.ds(c0, G)]))
        indexed.up(pool.tensor_copy(idx_d[q][:, :], net.dst_u[:, bass.ds(c0, G)]))
        wait(pool, indexed)
        for j in range(G):
            for half, idx in ((0, idx_s), (1, idx_d)):
                gathered[q].up(pool.indirect_dma_start(
                    out=gath[q][:, j, half * D:(half + 1) * D], out_offset=None, in_=net.h0_d,
                    in_offset=bass.IndirectOffsetOnAxis(ap=idx[q][:, j:j + 1], axis=0)), 16)

    for cnt, eng, n in ((turned, pe, 3), (z_done, pe, G), (copied, s, 1), (soft_done, v, 2),
                        (moved, pe, 1), (onehots, v, 2), (ranked, v, 2 * G), (based, v, 2)):
        cnt.credit(eng, n)
    net.after(pool, net.dve)
    for q in two:
        scattered[q].up(pool.dma_start(rows[q][:, :, OUTJ + ROW - 3:OUTJ + ROW],
                                       prod[0][:, 0:3 * G].rearrange("p (g c) -> p g c", g=G)), 16)
    gather(0, 0)
    per = {indexed: 4, gathered[0]: 256, gathered[1]: 256, loaded_e[0]: 32, loaded_e[1]: 32,
           loaded_s[0]: 32, loaded_s[1]: 32, turned: 4, copied: 4, z_done: 8,
           abs_done: 8, exp_done: 8, ln_done: 8, soft_done: 8, prod_done: 8, dot_done: 8, onehots: 2,
           ranked: 2 * G, saved: 2 * G, moved: 2 * G, based: 2, picked: 2, rows_done: 2,
           scattered[0]: 128, scattered[1]: 128}
    with Loop(nc, T // (2 * G), per) as it:
        for q in two:
            c0 = (it * 2 + q) * G
            e0 = c0 * P
            wait(sp, z_done, back=G // 2)
            loaded_e[q].up(sp.dma_start(in_i[q][D:2 * D, :], a["edge_t"][:, bass.ds(e0, GP)]), 16)
            loaded_e[q].up(sp.dma_start(in_j[q][0:D, :], a["edge_t"][:, bass.ds(e0, GP)]), 16)
            wait(sp, ranked, back=G)
            wait(sp, onehots, back=1)
            loaded_s[q].up(sp.dma_start(srow[q][:, :], a["src"][bass.ds(e0, GP)].partition_broadcast(P)), 16)
            loaded_s[q].up(sp.dma_start(lrow[q][:, :], net.lo_d[bass.ds(e0, GP)].partition_broadcast(P)), 16)

            wait(pe, gathered[q])
            for half in two:
                wait(pe, copied)
                for j in range(4):
                    ins = pe.transpose(tp[:, j, :], gath[q][:, 4 * half + j, :], net.ident[:, :])
                turned.up(ins)
                wait(s, turned)
                if half == 0:
                    wait(s, z_done, back=G // 2)
                cols = bass.ds(half * 4 * P, 4 * P)
                s.copy(in_i[q][0:D, cols], tp[0:D, :, :].rearrange("p j e -> p (j e)"))
                copied.up(s.copy(in_j[q][D:2 * D, cols], tp[D:2 * D, :, :].rearrange("p j e -> p (j e)")))

            gather(c0 + G, 1 - q)

            wait(v, loaded_s[q])
            wait(v, moved)
            v.tensor_copy(src_g[q][:, :], net.src_f[:, bass.ds(c0, G)])
            v.tensor_copy(hi_g[q][:, :], net.hi_f[:, bass.ds(c0, G)])
            v.tensor_tensor(oh_lo[q][:, :, :], net.iota_b[:, None, :].to_broadcast([P, G, P]),
                            net.lo_b[:, bass.ds(c0, G)].unsqueeze(2).to_broadcast([P, G, P]), ALU.is_equal)
            v.tensor_tensor(oh_hi[q][:, :, :], net.iota_b[:, None, 0:NBU].to_broadcast([P, G, NBU]),
                            net.hi_b[:, bass.ds(c0, G)].unsqueeze(2).to_broadcast([P, G, NBU]), ALU.is_equal)
            onehots.up(v.tensor_scalar(oh_loT[q][:, :], lrow[q][:, :], net.part[:, 0:1], None, ALU.is_equal))

            for k in range(G // 2):
                if k == 0:
                    wait(pe, loaded_e[q])
                    wait(pe, copied)
                wait(pe, soft_done, back=1)
                for j in (2 * k, 2 * k + 1):
                    pe.matmul(z[k % 2][:, j % 2, 0:OUTJ], in_i[q][:, j * P:(j + 1) * P], w_i[:, :],
                              start=True, stop=True)
                    ins = pe.matmul(z[k % 2][:, j % 2, OUTJ:2 * OUTJ], in_j[q][:, j * P:(j + 1) * P],
                                    w_j[:, :], start=True, stop=True)
                z_done.up(ins)

                def running(j):
                    wait(s, moved)
                    saved.up(s.copy(upto[j % 2][:, :], nxt[:, :]))
                    if j == 0:
                        wait(pe, onehots)
                        wait(pe, based, back=1)
                    wait(pe, saved)
                    pe.matmul(at[q][:, j, 0:NBU], oh_loT[q][:, j * P:(j + 1) * P], upto[j % 2][:, :],
                              start=True, stop=True)
                    moved.up(pe.matmul(nxt[:, :], oh_lo[q][:, j, :], oh_hi[q][:, j, :], start=False,
                                       stop=False, skip_group_check=True))

                zz = z[k % 2][:, :, :].rearrange("p t f -> p (t f)")
                wait(s, z_done)
                wait(s, soft_done, back=1)
                abs_done.up(s.activation(soft[k % 2][:, :], zz, ACT.Abs))
                running(2 * k)
                wait(s, abs_done)
                exp_done.up(s.activation(soft[k % 2][:, :], soft[k % 2][:, :], ACT.Exp, scale=-1.0))
                running(2 * k + 1)
                wait(s, exp_done)
                ln_done.up(s.activation(soft[k % 2][:, :], soft[k % 2][:, :], ACT.Ln, bias=1.0))

                if k == 0:
                    if q == 0:
                        wait(v, scattered[1])
                    wait(v, scattered[q])
                wait(v, ln_done)
                rk = rows[q][:, 2 * k:2 * k + 2, 0:2 * OUTJ]
                soft_done.up(v.scalar_tensor_tensor(rk, z[k % 2][:, :, :], 0.0,
                                                    soft[k % 2][:, :].rearrange("p (t f) -> p t f", t=2),
                                                    ALU.max, ALU.add))
                if k == 0:
                    wait(v, onehots)
                for j in (2 * k, 2 * k + 1):
                    ranked.up(v.scalar_tensor_tensor(
                        junk_r[:, j, :], srow[q][:, j * P:(j + 1) * P], src_g[q][:, j:j + 1],
                        before[:, :], ALU.is_equal, ALU.mult, accum_out=rank[q][:, j:j + 1]))
                wait(v, soft_done)
                prod_done.up(v.tensor_tensor(prod[k % 2][:, :].rearrange("p (t f) -> p t f", t=2), rk,
                                             att[:, None, :].to_broadcast([P, 2, 2 * OUTJ]), ALU.mult))
                wait(v, prod_done)
                dot_done.up(v.tensor_reduce(
                    dots[q][:, 2 * k:2 * k + 2, :].rearrange("p t h -> p (t h)"),
                    prod[k % 2][:, :].rearrange("p (g d) -> p g d", d=D), AX.X, ALU.add))

            wait(v, moved)
            picked.up(v.tensor_tensor(pick[:, :, :], oh_hi[q][:, :, :], at[q][:, :, 0:NBU], ALU.mult))
            wait(v, picked)
            based.up(v.tensor_reduce(base[q][:, :], pick[:, :, :], AX.X, ALU.add))
            wait(v, based)
            wait(v, dot_done)
            v.tensor_copy(rows[q][:, :, 2 * OUTJ + HEADS:2 * OUTJ + HEADS + 1],
                          src_g[q][:, :].unsqueeze(2))
            v.tensor_tensor(place[q][:, :], rank[q][:, :], base[q][:, :], ALU.add)
            rows_done.up(v.tensor_tensor(rows[q][:, :, 2 * OUTJ:2 * OUTJ + HEADS], dots[q][:, :, 0:HEADS],
                                         dots[q][:, :, HEADS:2 * HEADS], ALU.add))

            wait(pool, rows_done)
            for j in range(G):
                scattered[q].up(pool.indirect_dma_start(
                    out=net.rows_d, out_offset=bass.IndirectOffsetOnAxis(ap=place[q][:, j:j + 1], axis=0),
                    in_=rows[q][:, j, OUTJ:OUTJ + ROW], in_offset=None), 16)
    for q in two:
        wait(pool, scattered[q])
        wait(pool, gathered[q])


def softplus(net, out, x, tmp):
    nc = net.nc
    net.after(nc.scalar, net.dve)
    net.act(nc.scalar.activation(tmp, x, ACT.Abs))
    net.act(nc.scalar.activation(tmp, tmp, ACT.Exp, scale=-1.0))
    net.act(nc.scalar.activation(tmp, tmp, ACT.Ln, bias=1.0))
    net.after(nc.vector, net.act)
    net.dve(nc.vector.scalar_tensor_tensor(out, x, 0.0, tmp, ALU.max, ALU.add))


def all_sum(net, out, part, ps):
    nc = net.nc
    net.after(nc.tensor, net.dve)
    net.pe(nc.tensor.matmul(ps, net.ones[:, :], part, start=True, stop=True))
    net.after(nc.vector, net.pe)
    net.dve(nc.vector.tensor_copy(out, ps))


def edge_softmax(net):
    nc, a = net.nc, net.a
    v = nc.vector
    view = net.rows_d.rearrange("(p c) r -> p c r", c=T)
    with Mem(nc, "sm") as t:
        al = t.sb("al", [P, T, HEADS + 1])
        keep_f = t.sb("keep_f", [P, T])
        keep_b = t.sb("keep_b", [P, T])
        be = t.sb("be", [P, HEADS, T])
        fw = t.sb("fw", [P, HEADS, T])
        tot = t.sb("tot", [P, HEADS, T])
        prv, nxt = t.sb("prv", [P, 1]), t.sb("nxt", [P, 1])
        k_f, k_b = t.sb("k_f", [P, HEADS]), t.sb("k_b", [P, HEADS])
        s1, s2 = t.sb("s1", [P, HEADS]), t.sb("s2", [P, HEADS])
        mu, scale = t.sb("mu", [P, HEADS]), t.sb("scale", [P, HEADS])
        gam, bet = t.sb("gam", [P, HEADS]), t.sb("bet", [P, HEADS])
        line, line_k = t.sb("line", [HEADS, P]), t.sb("line_k", [HEADS, P])
        carry = t.sb("carry", [HEADS, P])
        ps = t.ps("ps", [P, HEADS])
        ps_l = t.ps("ps_l", [HEADS, 2, P])

        net.dve(v.memset(prv[:, :], -1.0))
        net.dve(v.memset(nxt[:, :], -1.0))
        net.after(nc.sync, net.dve)
        net.load(al[:, :, :], view[:, :, OUTJ:OUTJ + HEADS + 1])
        net.load(prv[1:P, :], view[0:P - 1, T - 1, OUTJ + HEADS:OUTJ + HEADS + 1])
        net.load(nxt[0:P - 1, :], view[1:P, 0, OUTJ + HEADS:OUTJ + HEADS + 1])
        net.load(gam[:, :], a["gamma"].partition_broadcast(P))
        net.load(bet[:, :], a["beta"].partition_broadcast(P))
        net.after(v, net.sp)
        src = al[:, :, HEADS]
        net.dve(v.tensor_tensor(keep_f[:, 1:T], src[:, 1:T], src[:, 0:T - 1], ALU.is_equal))
        net.dve(v.tensor_tensor(keep_f[:, 0:1], src[:, 0:1], prv[:, :], ALU.is_equal))
        net.dve(v.tensor_copy(keep_b[:, 0:T - 1], keep_f[:, 1:T]))
        net.dve(v.tensor_tensor(keep_b[:, T - 1:T], src[:, T - 1:T], nxt[:, :], ALU.is_equal))
        for k, keep in ((k_f, keep_f), (k_b, keep_b)):
            net.dve(v.tensor_reduce(prv[:, :], keep[:, :], AX.X, ALU.min))
            net.dve(v.tensor_copy(k[:, :], prv[:, :].to_broadcast([P, HEADS])))

        softplus(net, be[:, :, :], al[:, :, 0:HEADS].rearrange("p c h -> p h c"), fw[:, :, :])
        mask_i, mask = tot[:, 0, :].bitcast(I32), tot[:, 1, :]
        net.after(nc.gpsimd, net.dve)
        net.pool(nc.gpsimd.iota(mask_i, [[1, T]], base=0, channel_multiplier=T))
        net.after(v, net.pool)
        net.dve(v.tensor_copy(mask, mask_i))
        net.dve(v.tensor_scalar(mask, mask, float(E), None, ALU.is_lt))
        mask_h = tot[:, 1:2, :].to_broadcast([P, HEADS, T])
        head = lambda s: s[:, :].unsqueeze(2).to_broadcast([P, HEADS, T])
        net.dve(v.tensor_tensor(fw[:, :, :], be[:, :, :], mask_h, ALU.mult))
        net.dve(v.tensor_reduce(s1[:, :], fw[:, :, :], AX.X, ALU.add))
        all_sum(net, mu[:, :], s1[:, :], ps[:, :])
        net.dve(v.tensor_scalar(mu[:, :], mu[:, :], 1.0 / E, None, ALU.mult))
        net.dve(v.tensor_tensor(be[:, :, :], be[:, :, :], head(mu), ALU.subtract))
        net.dve(v.tensor_tensor(fw[:, :, :], be[:, :, :], mask_h, ALU.mult))
        net.dve(v.tensor_tensor(fw[:, :, :], fw[:, :, :], fw[:, :, :], ALU.mult))
        net.dve(v.tensor_reduce(s1[:, :], fw[:, :, :], AX.X, ALU.add))
        all_sum(net, scale[:, :], s1[:, :], ps[:, :])
        net.dve(v.tensor_scalar(scale[:, :], scale[:, :], 1.0 / E, EPS, ALU.mult, ALU.add))
        net.after(nc.scalar, net.dve)
        net.act(nc.scalar.activation(scale[:, :], scale[:, :], ACT.Sqrt))
        net.after(v, net.act)
        net.dve(v.reciprocal(scale[:, :], scale[:, :]))
        net.dve(v.tensor_tensor(scale[:, :], scale[:, :], gam[:, :], ALU.mult))
        for h in range(HEADS):
            net.dve(v.tensor_scalar(be[:, h, :], be[:, h, :], scale[:, h:h + 1], bet[:, h:h + 1], ALU.mult,
                                    ALU.add))
        softplus(net, be[:, :, :], be[:, :, :], fw[:, :, :])

        def carried(ends, keeps, op, back):
            net.dve(v.tensor_copy(s2[:, :], ends))
            net.after(nc.tensor, net.dve)
            net.pe(nc.tensor.transpose(ps_l[:, 0, :], s2[:, :], net.ident[:, :]))
            net.pe(nc.tensor.transpose(ps_l[:, 1, :], keeps[:, :], net.ident[:, :]))
            net.after(v, net.pe)
            net.dve(v.tensor_copy(line[:, :], ps_l[:, 0, :]))
            net.dve(v.tensor_copy(line_k[:, :], ps_l[:, 1, :]))
            net.dve(v.memset(carry[:, :], 0.0))
            if back:
                net.dve(v.tensor_tensor_scan(carry[:, P - 2::-1], line_k[:, P - 1:0:-1], line[:, P - 1:0:-1],
                                             0.0, ALU.mult, op))
            else:
                net.dve(v.tensor_tensor_scan(carry[:, 1:P], line_k[:, 0:P - 1], line[:, 0:P - 1], 0.0,
                                             ALU.mult, op))
            net.after(nc.tensor, net.dve)
            net.pe(nc.tensor.transpose(ps[:, :], carry[:, :], net.ident[0:HEADS, 0:HEADS]))
            net.after(v, net.pe)
            net.dve(v.tensor_copy(s2[:, :], ps[:, :]))

        def segments(op):
            for first in (True, False):
                for h in range(HEADS):
                    net.dve(v.tensor_tensor_scan(fw[:, h, :], keep_f[:, :], be[:, h, :],
                                                 0.0 if first else s2[:, h:h + 1], ALU.mult, op))
                if first:
                    carried(fw[:, :, T - 1], k_f, op, False)
            for first in (True, False):
                for h in range(HEADS):
                    net.dve(v.tensor_tensor_scan(tot[:, h, ::-1], keep_b[:, ::-1], fw[:, h, ::-1],
                                                 0.0 if first else s2[:, h:h + 1], ALU.mult, ALU.max))
                if first:
                    carried(tot[:, :, 0], k_b, ALU.max, True)

        segments(ALU.max)
        net.dve(v.tensor_tensor(be[:, :, :], be[:, :, :], tot[:, :, :], ALU.subtract))
        net.after(nc.scalar, net.dve)
        net.act(nc.scalar.activation(be[:, :, :], be[:, :, :], ACT.Exp))
        net.after(v, net.act)
        segments(ALU.add)
        net.dve(v.tensor_scalar(tot[:, :, :], tot[:, :, :], 1e-16, None, ALU.add))
        net.dve(v.reciprocal(tot[:, :, :], tot[:, :, :]))
        net.dve(v.tensor_tensor(al[:, :, 0:HEADS].rearrange("p c h -> p h c"), be[:, :, :], tot[:, :, :],
                                ALU.mult))
        net.after(nc.sync, net.dve)
        net.load(view[:, :, OUTJ:OUTJ + HEADS], al[:, :, 0:HEADS])


def item_values(nc, eng, row, top):
    _, values = nc.values_load_multi_w_load_instructions(
        row[0:1, :], engines=(eng.engine,), min_val=0, max_val=top,
        skip_runtime_bounds_check_because="the item lists are clamped to this range")
    return values


def free_values(nc, values):
    for value in values:
        for reg in value.val.handles:
            nc.free_register(reg)


def add_items(net, acc, added, blk, sums, cols):
    nc, v = net.nc, net.nc.vector
    blocks = item_values(nc, v, blk, NBU * P)
    with Temporaries(nc, v):
        for j in range(G):
            wait(v, added)
            here = acc[:, bass.ds(blocks[j], cols)]
            added.up(v.tensor_tensor(here, here, sums(j), ALU.add))
    free_values(nc, blocks)


def attention_sum(net, m, acc):
    nc = net.nc
    v, pe, pool, sp = nc.vector, nc.tensor, nc.gpsimd, nc.sync
    two = range(2)
    flat = net.rows_d.rearrange("e r -> (e r)")
    with Mem(nc, "at") as t:
        rows = [t.sb(f"rows{q}", [P, G, ROW]) for q in two]
        wtd = [t.sb(f"wtd{q}", [P, G, OUTJ]) for q in two]
        msg = [t.sb(f"msg{q}", [P, G, D]) for q in two]
        loc = [t.sb(f"loc{q}", [P, G]) for q in two]
        oh = [t.sb(f"oh{q}", [P, G, P]) for q in two]
        blk = [t.sb(f"blk{q}", [1, G], I32) for q in two]
        til = [t.sb(f"til{q}", [1, G], I32) for q in two]
        ps = [t.ps(f"ps{q}", [P, G, D]) for q in two]
        c = lambda name: Count(nc, "att_" + name)
        loaded = [c(f"loaded{q}") for q in two]
        weighted, placed, summed, added, messaged, onehot, listed = map(
            c, ("weighted", "placed", "summed", "added", "messaged", "onehot", "listed"))
        net.dve(v.memset(acc[:, :], 0.0))
        for cnt, eng, n in ((weighted, pool, 2), (messaged, v, 2), (onehot, v, 2), (summed, pe, 2),
                            (added, v, G + 1)):
            cnt.credit(eng, n)
        per = {loaded[0]: 16 * G, loaded[1]: 16 * G, weighted: 2, placed: 2, summed: 2, added: 2 * G,
               messaged: 2, onehot: 2, listed: 4}
        with Loop(nc, W // (2 * G), per) as it:
            for q in two:
                w0 = (it * 2 + q) * G
                wait(nc.scalar, weighted, back=1)
                wait(nc.scalar, added, back=G)
                listed.up(nc.scalar.copy(til[q][:, :], net.row_tsrc[:, bass.ds(w0, G)]))
                listed.up(nc.scalar.copy(blk[q][:, :], net.row_bsrc[:, bass.ds(w0, G)]))
                wait(sp, listed)
                wait(sp, weighted, back=1)
                wait(sp, onehot, back=1)
                starts = item_values(nc, sp, til[q], (T - 1) * P * ROW)
                with Temporaries(nc, sp):
                    for j in range(G):
                        tile = flat[bass.ds(starts[j], P * ROW)].rearrange("(p r) -> p r", p=P)
                        loaded[q].up(sp.dma_start(rows[q][:, j, :], tile), 16)
                free_values(nc, starts)
                wait(pool, loaded[q])
                wait(pool, messaged, back=1)
                weighted.up(pool.tensor_tensor(
                    wtd[q][:, :, :].rearrange("p g (h d) -> p g h d", h=HEADS),
                    rows[q][:, :, 0:OUTJ].rearrange("p g (h d) -> p g h d", h=HEADS),
                    rows[q][:, :, OUTJ:OUTJ + HEADS].unsqueeze(3).to_broadcast([P, G, HEADS, D]), ALU.mult))
                wait(v, loaded[q])
                wait(v, summed, back=1)
                placed.up(v.tensor_tensor(loc[q][:, :], rows[q][:, :, OUTJ + HEADS],
                                          net.bsrc[:, bass.ds(w0, G)], ALU.subtract))
                wait(v, placed)
                onehot.up(v.tensor_tensor(oh[q][:, :, :], net.iota[:, None, :].to_broadcast([P, G, P]),
                                          loc[q][:, :].unsqueeze(2).to_broadcast([P, G, P]), ALU.is_equal))
                wait(v, weighted)
                messaged.up(v.tensor_reduce(msg[q][:, :, :],
                                            wtd[q][:, :, :].rearrange("p g (h d) -> p g d h", h=HEADS),
                                            AX.X, ALU.add))
                wait(pe, messaged)
                wait(pe, added, back=G)
                for j in range(G):
                    ins = pe.matmul(ps[q][:, j, :], oh[q][:, j, :], msg[q][:, j, :], start=True, stop=True)
                summed.up(ins)
                wait(v, listed)
                wait(v, summed)
                add_items(net, acc, added, blk[q], lambda j: ps[q][:, j, :], D)


def gather_sum(net, tag, table, index, acc, cols, ones=False):
    nc = net.nc
    v, pe, pool = nc.vector, nc.tensor, nc.gpsimd
    two = range(2)
    wide = cols + (1 if ones else 0)
    with Mem(nc, tag) as t:
        got = [t.sb(f"got{q}", [P, G, wide + wide % 2]) for q in two]
        idx = [t.sb(f"idx{q}", [P, G], U32) for q in two]
        oh = [t.sb(f"oh{q}", [P, G, P]) for q in two]
        blk = [t.sb(f"blk{q}", [1, G], I32) for q in two]
        ps = [t.ps(f"ps{q}", [P, G, P]) for q in two]
        c = lambda name: Count(nc, f"{tag}_{name}")
        gathered = [c(f"gathered{q}") for q in two]
        indexed, onehot, summed, added, listed = map(c, ("indexed", "onehot", "summed", "added", "listed"))
        net.dve(v.memset(acc[:, :], 0.0))
        if ones:
            for q in two:
                net.dve(v.memset(got[q][:, :, cols:wide], 1.0))
            net.after(pe, net.dve)
        for cnt, eng, n in ((onehot, v, 2), (summed, pe, 2), (added, v, G + 1)):
            cnt.credit(eng, n)
        with Loop(nc, W // (2 * G), {gathered[0]: 16 * G, gathered[1]: 16 * G, indexed: 2, onehot: 2,
                                     summed: 2, added: 2 * G, listed: 2}) as it:
            for q in two:
                w0 = (it * 2 + q) * G
                wait(nc.scalar, added, back=G)
                listed.up(nc.scalar.copy(blk[q][:, :], net.row_dst[:, bass.ds(w0, G)]))
                wait(pool, summed, back=1)
                indexed.up(pool.tensor_copy(idx[q][:, :], index[:, bass.ds(w0, G)]))
                wait(pool, indexed)
                for j in range(G):
                    gathered[q].up(pool.indirect_dma_start(
                        out=got[q][:, j, 0:cols], out_offset=None, in_=table,
                        in_offset=bass.IndirectOffsetOnAxis(ap=idx[q][:, j:j + 1], axis=0)), 16)
                wait(v, summed, back=1)
                onehot.up(v.tensor_tensor(oh[q][:, :, :], net.iota[:, None, :].to_broadcast([P, G, P]),
                                          net.dloc[:, bass.ds(w0, G)].unsqueeze(2).to_broadcast([P, G, P]),
                                          ALU.is_equal))
                wait(pe, onehot)
                wait(pe, gathered[q])
                wait(pe, added, back=G)
                for j in range(G):
                    ins = pe.matmul(ps[q][:, j, 0:wide], oh[q][:, j, :], got[q][:, j, 0:wide], start=True,
                                    stop=True)
                summed.up(ins)
                wait(v, listed)
                wait(v, summed)
                add_items(net, acc, added, blk[q], lambda j: ps[q][:, j, 0:wide], wide)


def by_block(acc):
    return acc[:, :].rearrange("p (b s) -> p b s", s=P)


def relation_table(net, tag, h, w, table):
    nc = net.nc
    v, s, pe, sp = nc.vector, nc.scalar, nc.tensor, nc.sync
    two = range(2)
    wide = RELS * D
    part = wide // 3
    with Mem(nc, tag) as t:
        ws = t.sb("ws", [D, RELS, D])
        hs = [t.sb(f"hs{q}", [P, D]) for q in two]
        ht = [t.sb(f"ht{q}", [D, P]) for q in two]
        out = [t.sb(f"out{q}", [P, wide]) for q in two]
        tp = t.ps("tp", [D, P])
        ps = [t.ps(f"ps{q}", [P, wide]) for q in two]
        c = lambda name: Count(nc, f"{tag}_{name}")
        taken, turned, copied, done, emptied_s, emptied_v = map(
            c, ("taken", "turned", "copied", "done", "emptied_s", "emptied_v"))
        stored = [c(f"stored{q}") for q in two]
        net.load(ws[:, :, :], w.rearrange("r d f -> d r f"))
        net.after(pe, net.sp, net.dve)
        for cnt, eng, n in ((turned, pe, 2), (done, pe, 2), (emptied_s, s, 2), (emptied_v, v, 2)):
            cnt.credit(eng, n)
        for q in two:
            net.dve(v.memset(out[q][:, 0:1], 0.0))
            net.after(sp, net.dve)
            stored[q].up(sp.dma_start(net.spare_d[q], out[q][:, 0:1]), 16)
        with Loop(nc, NB // 2, {taken: 2, turned: 2, copied: 2, done: 2, emptied_s: 2, emptied_v: 2,
                                stored[0]: 16, stored[1]: 16}) as it:
            for q in two:
                b = it * 2 + q
                wait(v, turned, back=1)
                taken.up(v.tensor_copy(hs[q][:, :], h[:, bass.ds(b, 1), :].rearrange("p b d -> p (b d)")))
                wait(pe, taken)
                turned.up(pe.transpose(tp[:, :], hs[q][:, :], net.ident[:, :]))
                wait(v, turned)
                wait(v, done, back=1)
                copied.up(v.tensor_copy(ht[q][:, :], tp[:, :]))
                wait(pe, copied)
                wait(pe, emptied_s, back=1)
                wait(pe, emptied_v, back=1)
                for k in range(3):
                    ins = pe.matmul(ps[q][:, k * part:(k + 1) * part], ht[q][:, :],
                                    ws[:, :, :].rearrange("d r f -> d (r f)")[:, k * part:(k + 1) * part],
                                    start=True, stop=True)
                done.up(ins)
                wait(s, done)
                wait(s, stored[q])
                emptied_s.up(s.copy(out[q][:, 0:2 * part], ps[q][:, 0:2 * part]))
                wait(v, done)
                wait(v, stored[q])
                emptied_v.up(v.tensor_copy(out[q][:, 2 * part:wide], ps[q][:, 2 * part:wide]))
                wait(sp, emptied_s)
                wait(sp, emptied_v)
                stored[q].up(sp.dma_start(
                    table.rearrange("(b p) f -> p b f", p=P)[:, bass.ds(b, 1), :],
                    out[q][:, :].unsqueeze(1)), 16)
        for q in two:
            wait(sp, stored[q])


def relation_layer(net, tag, table, acc, h):
    v = net.nc.vector
    gather_sum(net, tag, table.rearrange("n (r f) -> (n r) f", f=D), net.grel, acc, D)
    net.dve(v.tensor_tensor(h[:, :, :], by_block(acc)[:, :, 0:D],
                            net.rdeg[:, :].unsqueeze(2).to_broadcast([P, NB, D]), ALU.mult))
    net.dve(v.tensor_scalar(h[:, :, :], h[:, :, :], 0.0, None, ALU.max))


def channel_tables(net, h, own, table):
    nc, a = net.nc, net.a
    v, s, pe, sp = nc.vector, nc.scalar, nc.tensor, nc.sync
    two = range(2)
    with Mem(nc, "ch") as t:
        ws = t.sb("ws", [D + 1, 5 * D])
        hs = [t.sb(f"hs{q}", [P, D + 1]) for q in two]
        nb = [t.sb(f"nb{q}", [P, 1]) for q in two]
        ht = [t.sb(f"ht{q}", [D + 1, P]) for q in two]
        out = [t.sb(f"out{q}", [P, 2 * D]) for q in two]
        tp = t.ps("tp", [D + 1, P])
        ps = [t.ps(f"ps{q}", [P, 5 * D]) for q in two]
        c = lambda name: Count(nc, f"ch_{name}")
        taken, turned, copied, done, kept, scaled = map(
            c, ("taken", "turned", "copied", "done", "kept", "scaled"))
        stored = [c(f"stored{q}") for q in two]
        for i, name in enumerate(("self", "self_high", "id", "neigh", "neigh_high")):
            net.load(ws[0:D, i * D:(i + 1) * D], a["Wt_" + name])
            net.load(ws[D:D + 1, i * D:(i + 1) * D], a["b_" + name].rearrange("(a d) -> a d", a=1))
        for q in two:
            net.dve(v.memset(hs[q][:, D:D + 1], 1.0))
            net.dve(v.memset(out[q][:, 0:1], 0.0))
            net.after(sp, net.dve)
            stored[q].up(sp.dma_start(net.spare_d[q], out[q][:, 0:1]), 16)
        net.after(pe, net.sp, net.dve)
        for cnt, eng, n in ((turned, pe, 2), (done, pe, 2), (kept, s, 2), (scaled, v, 2)):
            cnt.credit(eng, n)
        with Loop(nc, NB // 2, {taken: 2, turned: 2, copied: 2, done: 2, kept: 2, scaled: 2,
                                stored[0]: 16, stored[1]: 16}) as it:
            for q in two:
                b = it * 2 + q
                wait(v, turned, back=1)
                wait(v, scaled, back=1)
                v.tensor_copy(nb[q][:, :], net.norm[:, bass.ds(b, 1)])
                taken.up(v.tensor_copy(hs[q][:, 0:D], h[:, bass.ds(b, 1), :].rearrange("p b d -> p (b d)")))
                wait(pe, taken)
                turned.up(pe.transpose(tp[:, :], hs[q][:, :], net.ident[:, :]))
                wait(v, turned)
                wait(v, done, back=1)
                copied.up(v.tensor_copy(ht[q][:, :], tp[:, :]))
                wait(pe, copied)
                wait(pe, kept, back=1)
                wait(pe, scaled, back=1)
                done.up(pe.matmul(ps[q][:, :], ht[q][:, :], ws[:, :], start=True, stop=True))
                wait(s, done)
                kept.up(s.activation(own[:, bass.ds(b, 1), :].rearrange("p b f -> p (b f)"),
                                     ps[q][:, 0:3 * D], ACT.Relu))
                wait(v, kept)
                wait(v, taken)
                wait(v, stored[q])
                scaled.up(v.tensor_scalar(out[q][:, :], ps[q][:, 3 * D:5 * D], 0.0, nb[q][:, 0:1], ALU.max,
                                          ALU.mult))
                wait(sp, scaled)
                stored[q].up(sp.dma_start(
                    table.rearrange("(b p) f -> p b f", p=P)[:, bass.ds(b, 1), :],
                    out[q][:, :].unsqueeze(1)), 16)
        for q in two:
            wait(sp, stored[q])


def channel_mix(net, acc, own):
    nc, a = net.nc, net.a
    v, s = nc.vector, nc.scalar
    with Mem(nc, "mix") as t:
        wa = t.sb("wa", [P, 3, D])
        w3 = t.sb("w3", [P, 3, 3])
        tmp = t.sb("tmp", [P, NB, D])
        lg = t.sb("lg", [P, NB, 3])
        at = t.sb("at", [P, NB, 3])
        pr = t.sb("pr", [P, NB, 3])
        mx = t.sb("mx", [P, NB])
        for i, name in enumerate(("low", "high", "mlp")):
            net.load(wa[:, i, :], a["att_" + name].partition_broadcast(P))
        net.load(w3[:, :, :], a["W_att"].partition_broadcast(P))
        net.after(v, net.sp)
        by_node = lambda x, n: x[:, :].unsqueeze(2).to_broadcast([P, NB, n])
        for i, op in ((0, ALU.add), (1, ALU.subtract)):
            o = own[:, :, i * D:(i + 1) * D]
            net.dve(v.tensor_tensor(tmp[:, :, :], by_block(acc)[:, :, i * D:(i + 1) * D],
                                    by_node(net.rdeg, D), ALU.mult))
            net.dve(v.tensor_tensor(o, o, tmp[:, :, :], op))
        for i in range(3):
            net.dve(v.tensor_tensor(tmp[:, :, :], own[:, :, i * D:(i + 1) * D],
                                    wa[:, i:i + 1, :].to_broadcast([P, NB, D]), ALU.mult))
            net.dve(v.tensor_reduce(lg[:, :, i], tmp[:, :, :], AX.X, ALU.add))
        net.after(s, net.dve)
        net.act(s.activation(lg[:, :, :], lg[:, :, :], ACT.Sigmoid))
        net.after(v, net.act)
        for j in range(3):
            net.dve(v.tensor_tensor(pr[:, :, :], lg[:, :, :], w3[:, j:j + 1, :].to_broadcast([P, NB, 3]),
                                    ALU.mult))
            net.dve(v.tensor_reduce(at[:, :, j], pr[:, :, :], AX.X, ALU.add))
        net.dve(v.tensor_scalar(at[:, :, :], at[:, :, :], 1.0 / 3.0, None, ALU.mult))
        net.dve(v.tensor_reduce(mx[:, :], at[:, :, :], AX.X, ALU.max))
        net.dve(v.tensor_tensor(at[:, :, :], at[:, :, :], by_node(mx, 3), ALU.subtract))
        net.after(s, net.dve)
        net.act(s.activation(at[:, :, :], at[:, :, :], ACT.Exp))
        net.after(v, net.act)
        net.dve(v.tensor_reduce(mx[:, :], at[:, :, :], AX.X, ALU.add))
        net.dve(v.reciprocal(mx[:, :], mx[:, :]))
        net.dve(v.tensor_scalar(mx[:, :], mx[:, :], 3.0, None, ALU.mult))
        net.dve(v.tensor_tensor(at[:, :, :], at[:, :, :], by_node(mx, 3), ALU.mult))
        for i in range(3):
            net.dve(v.tensor_tensor(tmp[:, :, :], own[:, :, i * D:(i + 1) * D],
                                    at[:, :, i:i + 1].to_broadcast([P, NB, D]), ALU.mult))
            net.dve(v.tensor_tensor(net.x[:, :, :], net.x[:, :, :], tmp[:, :, :], ALU.add))
        net.after(nc.sync, net.dve)
        net.load(node_view(net.out), net.x[:, :, :])


def build(nc, a, out):
    net = Net(nc, a)
    net.out = out
    dram = lambda name, shape: nc.dram_tensor(name, shape, F32).ap()
    net.lo_d = dram("lo_d", [EP])
    net.h0_d, h1_d = dram("h0_d", [NPAD, D]), dram("h1_d", [NPAD, D])
    net.rows_d = dram("rows_d", [EP, ROW])
    rel_d = [dram(f"rel{i}_d", [NPAD, RELS * D]) for i in range(2)]
    ch_d = dram("ch_d", [NPAD, 2 * D])
    net.spare_d = dram("spare_d", [2, P, 1])
    v = nc.vector
    with Mem(nc, "all", "right") as m:
        make_constants(net, m)
        with Mem(nc, "prep") as t:
            net.x = t.sb("x", [P, NB, D])
            net.load(net.x[:, :, :], node_view(a["x"]))
            net.after(v, net.sp)
            layer_norm(net, t, net.h0_d)
        with Mem(nc, "edge") as e:
            index_lists(net, e)
            count_dst_blocks(net, e)
            item_tables(net, m)
            histogram_src(net, e)
            b128, tiles = item_list(net, e, "its", net.start_src)
            both = e.sb("both", [P, 2, WK], I32)
            net.dve(v.tensor_copy(both[:, 0, :], b128[:, :]))
            net.dve(v.tensor_scalar(both[:, 1, :], tiles[:, :], float(P * ROW), None, ALU.mult))
            net.row_bsrc = to_rows(net, m, "row_bsrc", both[:, 0, :], I32, False)
            net.row_tsrc = to_rows(net, m, "row_tsrc", both[:, 1, :], I32, False)
            net.bsrc = to_rows(net, m, "bsrc", b128[:, :], F32, True)
            nc.all_engine_barrier()
            edge_pass(net, e)
        edge_softmax(net)
        with Mem(nc, "net") as t:
            net.x = t.sb("x", [P, NB, D])
            acc = t.sb("acc", [P, NB * P])
            bias = t.sb("bias", [P, D])
            net.norm, net.rdeg = t.sb("norm", [P, NB]), t.sb("rdeg", [P, NB])
            net.load(net.x[:, :, :], node_view(a["x"]))
            net.load(bias[:, :], a["bias"].partition_broadcast(P))
            net.after(v, net.sp)
            attention_sum(net, t, acc)
            net.dve(v.scalar_tensor_tensor(net.x[:, :, :], by_block(acc)[:, :, 0:D], 1.0 / HEADS,
                                           net.x[:, :, :], ALU.mult, ALU.add))
            net.dve(v.tensor_tensor(net.x[:, :, :], net.x[:, :, :],
                                    bias[:, None, :].to_broadcast([P, NB, D]), ALU.add))
            with Mem(nc, "l1") as n:
                layer_norm(net, n, h1_d)
            gather_sum(net, "l1s", h1_d, net.gsrc, acc, D, ones=True)
            net.dve(v.tensor_tensor(net.x[:, :, :], net.x[:, :, :], by_block(acc)[:, :, 0:D], ALU.add))
            net.dve(v.tensor_scalar(net.norm[:, :], by_block(acc)[:, :, D], 1.0, None, ALU.max))
            net.dve(v.reciprocal(net.rdeg[:, :], net.norm[:, :]))
            net.after(nc.scalar, net.dve)
            net.act(nc.scalar.activation(net.norm[:, :], net.norm[:, :], ACT.Sqrt))
            net.after(v, net.act)
            net.dve(v.reciprocal(net.norm[:, :], net.norm[:, :]))
            with Mem(nc, "l2") as n:
                h = layer_norm(net, n, None)
                for i in range(2):
                    relation_table(net, f"l2t{i}", h, a[f"W{i + 1}"], rel_d[i])
                    relation_layer(net, f"l2s{i}", rel_d[i], acc, h)
                net.dve(v.tensor_tensor(net.x[:, :, :], net.x[:, :, :], h[:, :, :], ALU.add))
            own = t.sb("own", [P, NB, 3 * D])
            with Mem(nc, "l3") as n:
                channel_tables(net, layer_norm(net, n, None), own, ch_d)
            gather_sum(net, "l3s", ch_d, net.gsrc, acc, 2 * D)
            channel_mix(net, acc, own)


def pad_to(a, n, fill=0):
    out = np.full((n,) + a.shape[1:], fill, a.dtype)
    out[:a.shape[0]] = a
    return out


def kernel(**inputs):
    from concourse.bass_utils import run_bass_kernel_spmd

    i = {k: np.asarray(v) for k, v in inputs.items()}
    arrays = {
        "x": pad_to(i["x"], NPAD), "src": pad_to(i["src"], EP, PAD_NODE), "dst": pad_to(i["dst"], EP, PAD_NODE),
        "rel": pad_to(i["edge_type_24"], EP),
        "edge_t": np.ascontiguousarray(pad_to(i["edge_attr_64"], EP).T),
        "W": i["L0_gnn_W"], "att": i["L0_gnn_att"][0], "bias": i["L0_gnn_bias"],
        "gamma": i["L0_gnn_bn_gamma"], "beta": i["L0_gnn_bn_beta"],
        "W1": i["L2_gnn_W1"], "W2": i["L2_gnn_W2"], "W_att": i["L3_gnn_W_att"],
    }
    for name in ("self", "self_high", "id", "neigh", "neigh_high"):
        arrays["Wt_" + name] = np.ascontiguousarray(i["L3_gnn_W_" + name].T)
        arrays["b_" + name] = i["L3_gnn_b_" + name]
    for name in ("low", "high", "mlp"):
        arrays["att_" + name] = i["L3_gnn_w_att_" + name][0]
    nc = bass.Bass("TRN2", target_bir_lowering=False, num_devices=1)
    args = {k: nc.dram_tensor(f"in_{k}", v.shape, mybir.dt.from_np(v.dtype), kind="ExternalInput").ap()
            for k, v in arrays.items()}
    out = nc.dram_tensor("out", (NPAD, D), F32, kind="ExternalOutput").ap()
    build(nc, args, out)
    res = run_bass_kernel_spmd(nc, [{f"in_{k}": v for k, v in arrays.items()}], core_ids=[0]).results[0]
    return res["out"][:N]
```

```python
from contextlib import ExitStack

import numpy as np

import concourse.bass as bass
from concourse import mybir
from concourse.alu_op_type import AluOpType as ALU

F32, BF16, I32, U32 = mybir.dt.float32, mybir.dt.bfloat16, mybir.dt.int32, mybir.dt.uint32
ACT = mybir.ActivationFunctionType
AX = mybir.AxisListType

N, E, D, HEADS, RELS = 6250, 200000, 64, 4, 24
P = 128
NB = 50
NBU = 49
G = 8
T = -(-E // (2 * G * P)) * 2 * G
EP = T * P
PAD_NODE = NBU * P - 1
W = -(-(T + NB) // (2 * G)) * 2 * G
SPAN = 2
GS = G // SPAN
WS = -(-(T // SPAN + NB) // (2 * GS)) * 2 * GS
WK = -(-(W + G) // P)
WKS = -(-(WS + GS) // P)
TC = 112
KC = T // TC
NPAD = NB * P
OUTJ, ROW = HEADS * D, 264
EPS = 1e-5

assert KC * TC == T and TC <= P


class Count:

    def __init__(self, nc, name):
        self.sem = nc.alloc_semaphore(name)
        self.base, self.off, self.loop, self.per = 0, 0, None, 0

    def up(self, ins, n=1):
        ins.then_inc(self.sem, n)
        self.off += n
        return ins

    def credit(self, eng, n):
        eng.sem_inc(self.sem, n)
        self.base += n


class Temporaries:

    def __init__(self, nc, *engines):
        self.nc, self.engines = nc, engines

    def __enter__(self):
        self.first = self.nc.next_id()

    def __exit__(self, *a):
        if a[0] is None:
            for eng in self.engines:
                for n in range(self.first, self.nc.next_id()):
                    self.free(f"{eng.engine.value}_tmp_{n}", eng.engine)

    def free(self, name, engine):
        try:
            known = self.nc.lookup_reg(name)
        except (KeyError, ValueError, AssertionError):
            return
        if known is not None and known.allocated:
            self.nc.free_register(bass.RegisterHandle(name=name, engine=engine))


def wait(eng, count, back=0):
    v = count.base + count.off - back
    if count.loop is None:
        eng.wait_ge(count.sem, v)
    else:
        count.loop.wait(eng, count, v)


class Loop:

    SCRATCH, made = 4, 0

    def __init__(self, nc, trips, per):
        self.nc, self.trips, self.per = nc, trips, per
        self.share, self.scratch, self.met, self.turn = {}, {}, {}, 0

    def new(self, eng):
        Loop.made += 1
        return eng.alloc_register(f"loop_r{Loop.made}")

    def wait(self, eng, count, v):
        if self.met.get((eng.engine, count), -1) >= v:
            return
        self.met[(eng.engine, count)] = v
        if (eng.engine, count.per) not in self.share:
            r = self.share[(eng.engine, count.per)] = self.new(eng)
            eng.reg_mul(r, self.it, count.per)
        if eng.engine not in self.scratch:
            self.scratch[eng.engine] = (eng, [self.new(eng) for _ in range(self.SCRATCH)])
        self.turn += 1
        r = self.scratch[eng.engine][1][self.turn % self.SCRATCH]
        eng.reg_add(r, self.share[(eng.engine, count.per)], v)
        eng.wait_ge(count.sem, r)

    def __enter__(self):
        self.fori = self.nc.Fori(0, self.trips)
        self.it = self.fori.__enter__()
        nc = self.nc
        self.temporaries = Temporaries(nc, nc.vector, nc.scalar, nc.tensor, nc.gpsimd, nc.sync)
        self.temporaries.__enter__()
        for c, n in self.per.items():
            c.base, c.off, c.loop, c.per = c.base + c.off, 0, self, n
        return self.it

    def __exit__(self, *a):
        r = self.fori.__exit__(*a)
        if a[0] is None:
            for c, n in self.per.items():
                assert c.off == n, (str(c.sem), c.off, n)
                c.base, c.off, c.loop = c.base + n * self.trips, 0, None
            for reg in [*self.share.values(), *(r for _, rs in self.scratch.values() for r in rs)]:
                self.nc.free_register(reg)
            self.temporaries.__exit__(None, None, None)
            for reg in self.it.val.handles:
                self.nc.free_register(reg)
        return r


class Chain:

    def __init__(self, nc, eng, name):
        self.eng, self.count = eng, Count(nc, name)

    def __call__(self, ins, n=1):
        self.count.up(ins, n)
        wait(self.eng, self.count)


class Mem:

    def __init__(self, nc, tag, side="left"):
        self.nc, self.tag, self.side, self.ctx = nc, tag, side, ExitStack()

    def __enter__(self):
        self.ctx.__enter__()
        return self

    def __exit__(self, *a):
        if a[0] is None:
            self.nc.all_engine_barrier()
        return self.ctx.__exit__(*a)

    def sb(self, name, shape, dt=F32):
        return self.ctx.enter_context(self.nc.sbuf_tensor(f"{self.tag}_{name}", shape, dt, side=self.side))

    def ps(self, name, shape, dt=F32):
        return self.ctx.enter_context(self.nc.psum_tensor(f"{self.tag}_{name}", shape, dt))


class Net:

    def __init__(self, nc, args):
        self.nc, self.a = nc, args
        self.dve = Chain(nc, nc.vector, "dve_chain")
        self.act = Chain(nc, nc.scalar, "act_chain")
        self.pe = Chain(nc, nc.tensor, "pe_chain")
        self.pool = Chain(nc, nc.gpsimd, "pool_chain")
        self.sp = Chain(nc, nc.sync, "sp_chain")
        self.dma = Chain(nc, nc.gpsimd, "indirect_chain")

    def load(self, out, in_):
        with self.nc.allow_non_contiguous_dma("index lists and transposed vectors, once"):
            self.sp(self.nc.sync.dma_start(out, in_), 16)

    def after(self, eng, *chains):
        for c in chains:
            wait(eng, c.count)


def make_constants(net, m):
    nc = net.nc
    net.iota_i = m.sb("iota_i", [P, P], I32)
    net.iota = m.sb("iota", [P, P])
    net.iota_b = m.sb("iota_b", [P, P], BF16)
    net.part = m.sb("part", [P, 1])
    net.ident = m.sb("ident", [P, P])
    net.ones = m.sb("ones", [P, P])
    part_i = m.sb("part_i", [P, 1], I32)
    net.pool(nc.gpsimd.iota(net.iota_i[:, :], [[1, P]], base=0, channel_multiplier=0))
    net.pool(nc.gpsimd.iota(part_i[:, :], [[1, 1]], base=0, channel_multiplier=1))
    net.after(nc.vector, net.pool)
    net.dve(nc.vector.memset(net.ones[:, :], 1.0))
    net.dve(nc.vector.tensor_copy(net.iota[:, :], net.iota_i[:, :]))
    net.dve(nc.vector.tensor_copy(net.iota_b[:, :], net.iota_i[:, :]))
    net.dve(nc.vector.tensor_copy(net.part[:, :], part_i[:, :]))
    net.dve(nc.vector.tensor_scalar(net.ident[:, :], net.iota[:, :], net.part[:, 0:1], None, ALU.is_equal))


def index_lists(net, m):
    nc, a = net.nc, net.a
    net.src_f = m.sb("src_f", [P, T + G])
    net.src_u = m.sb("src_u", [P, T + G], U32)
    net.dst_u = m.sb("dst_u", [P, T + G], U32)
    net.lo_b = m.sb("lo_b", [P, T + G], BF16)
    net.hi_b = m.sb("hi_b", [P, T + G], BF16)
    with Mem(nc, "il") as t:
        raw = t.sb("raw", [TC, KC, P], I32)
        low = t.sb("low", [TC, KC, P], I32)
        flt = t.sb("flt", [TC, KC, P])
        digit = t.sb("digit", [P, T + G], I32)
        tp = t.ps("tp", [P, 4, P])
        for name, u in (("src", net.src_u), ("dst", net.dst_u)):
            net.after(nc.sync, net.dve)
            net.load(raw[:, :, :], a[name][0:EP].rearrange("(k p e) -> p k e", p=TC, e=P))
            net.after(nc.vector, net.sp)
            if name == "src":
                net.dve(nc.vector.tensor_scalar(low[:, :, :], raw[:, :, :], P - 1, None, ALU.bitwise_and))
                net.dve(nc.vector.tensor_copy(flt[:, :, :], low[:, :, :]))
                net.after(nc.sync, net.dve)
                net.load(net.lo_d[0:EP].rearrange("(k p e) -> p k e", p=TC, e=P), flt[:, :, :])
                net.load(net.lo_d[EP:EP + G * P].rearrange("(g e) -> g e", e=P), flt[0:G, 0, :])
                net.after(nc.vector, net.sp)
            net.dve(nc.vector.tensor_copy(flt[:, :, :], raw[:, :, :]))
            for k0 in range(0, KC, 4):
                n = min(4, KC - k0)
                net.after(nc.tensor, net.dve)
                for k in range(n):
                    net.pe(nc.tensor.transpose(tp[:, k, 0:TC], flt[:, k0 + k, :], net.ident[0:TC, 0:TC]))
                net.after(nc.vector, net.pe)
                net.dve(nc.vector.tensor_copy(
                    u[:, k0 * TC:(k0 + n) * TC].rearrange("p (k c) -> p k c", k=n), tp[:, 0:n, 0:TC]))
            net.dve(nc.vector.memset(u[:, T:T + G], 0))
        net.dve(nc.vector.tensor_copy(net.src_f[:, :], net.src_u[:, :]))
        for shift, out in ((False, net.lo_b), (True, net.hi_b)):
            op, val = (ALU.logical_shift_right, 7) if shift else (ALU.bitwise_and, P - 1)
            net.dve(nc.vector.tensor_scalar(digit[:, :], net.src_u[:, :].bitcast(I32), val, None, op))
            net.dve(nc.vector.tensor_copy(out[:, :], digit[:, :]))


def count_dst_blocks(net, m):
    nc = net.nc
    net.start_dst = m.sb("start_dst", [P, NB])
    with Mem(nc, "cb") as t:
        hit = t.sb("hit", [P, T])
        cnt = t.sb("cnt", [P, NB])
        tot = t.ps("tot", [P, NB])
        for b in range(NB):
            net.dve(nc.vector.tensor_scalar(hit[:, :], net.dst_u[:, 0:T], float(P * b), 0.0, ALU.is_lt, ALU.add,
                                            accum_out=cnt[:, b:b + 1]))
        net.after(nc.tensor, net.dve)
        net.pe(nc.tensor.matmul(tot[:, :], net.ones[:, :], cnt[:, :], start=True, stop=True))
        net.after(nc.vector, net.pe)
        net.dve(nc.vector.tensor_copy(net.start_dst[:, :], tot[:, :]))


def histogram_src(net, m):
    nc = net.nc
    net.start_src = m.sb("start_src", [P, NB])
    net.first = m.sb("first", [P, NBU])
    GH = 16
    with Mem(nc, "hi") as t:
        oh_lo = [t.sb(f"oh_lo{q}", [P, GH, P], BF16) for q in range(2)]
        oh_hi = [t.sb(f"oh_hi{q}", [P, GH, NBU], BF16) for q in range(2)]
        zero = t.sb("zero", [P, P], BF16)
        lower = t.sb("lower", [P, P])
        counts = t.sb("counts", [P, NBU])
        hist = t.ps("hist", [P, NBU])
        ex = t.ps("ex", [P, NBU])
        tot = t.ps("tot", [P, NBU])
        made, used = Count(nc, "hist_onehots"), Count(nc, "hist_summed")
        net.dve(nc.vector.memset(zero[:, :], 0.0))
        net.dve(nc.vector.tensor_scalar(lower[:, :], net.iota[:, :], net.part[:, 0:1], None, ALU.is_gt))
        net.after(nc.tensor, net.dve)
        net.pe(nc.tensor.matmul(hist[:, :], zero[:, :], zero[:, 0:NBU], start=True, stop=False,
                                skip_group_check=True))
        used.credit(nc.tensor, 2)
        with Loop(nc, T // (2 * GH), {made: 4, used: 2}) as it:
            for q in range(2):
                c0 = (it * 2 + q) * GH
                wait(nc.vector, used, back=1)
                made.up(nc.vector.tensor_tensor(
                    oh_lo[q][:, :, :], net.iota_b[:, None, :].to_broadcast([P, GH, P]),
                    net.lo_b[:, bass.ds(c0, GH)].unsqueeze(2).to_broadcast([P, GH, P]), ALU.is_equal))
                made.up(nc.vector.tensor_tensor(
                    oh_hi[q][:, :, :], net.iota_b[:, None, 0:NBU].to_broadcast([P, GH, NBU]),
                    net.hi_b[:, bass.ds(c0, GH)].unsqueeze(2).to_broadcast([P, GH, NBU]), ALU.is_equal))
                wait(nc.tensor, made)
                for j in range(GH):
                    ins = nc.tensor.matmul(hist[:, :], oh_lo[q][:, j, :], oh_hi[q][:, j, :], start=False,
                                           stop=False, skip_group_check=True)
                used.up(ins)
        wait(nc.vector, used)
        net.dve(nc.vector.tensor_copy(counts[:, :], hist[:, :]))
        net.after(nc.tensor, net.dve)
        net.pe(nc.tensor.matmul(tot[:, :], net.ones[:, :], counts[:, :], start=True, stop=True))
        net.pe(nc.tensor.matmul(ex[:, :], lower[:, :], counts[:, :], start=True, stop=True))
        net.after(nc.vector, net.pe)
        net.dve(nc.vector.tensor_copy(counts[:, :], tot[:, :]))
        net.dve(nc.vector.memset(net.start_src[:, 0:1], 0.0))
        net.dve(nc.vector.tensor_tensor_scan(net.start_src[:, 1:NB], net.ones[:, 0:NBU], counts[:, :], 0.0,
                                             ALU.mult, ALU.add))
        net.dve(nc.vector.tensor_tensor(net.first[:, :], ex[:, :], net.start_src[:, 0:NBU], ALU.add))


def item_list(net, m, tag, start, span, wk):
    nc = net.nc
    base128 = m.sb(f"{tag}_b128", [P, wk])
    tile_u = m.sb(f"{tag}_t", [P, wk], U32)
    size = span * P
    shift = size.bit_length() - 1
    with Mem(nc, tag) as t:
        si = t.sb("si", [P, NB], I32)
        fl = t.sb("fl", [P, NB])
        ce = t.sb("ce", [P, NB])
        n = t.sb("n", [P, NBU])
        c = t.sb("c", [P, NBU])
        g = t.sb("g", [P, NBU])
        dg = t.sb("dg", [P, NBU])
        s1 = t.sb("s1", [P, NBU])
        w_i = t.sb("w_i", [P, wk], I32)
        w = t.sb("w", [P, wk])
        bt = t.sb("bt", [P, wk, 2])
        v = nc.vector
        net.pool(nc.gpsimd.iota(w_i[:, :], [[P, wk]], base=0, channel_multiplier=1))
        net.after(v, net.pool)
        net.dve(v.tensor_copy(w[:, :], w_i[:, :]))
        net.dve(v.tensor_copy(si[:, :], start[:, :]))
        net.dve(v.tensor_scalar(si[:, :], si[:, :], shift, None, ALU.logical_shift_right))
        net.dve(v.tensor_copy(fl[:, :], si[:, :]))
        net.dve(v.tensor_scalar(ce[:, :], start[:, :], float(size - 1), None, ALU.add))
        net.dve(v.tensor_copy(si[:, :], ce[:, :]))
        net.dve(v.tensor_scalar(si[:, :], si[:, :], shift, None, ALU.logical_shift_right))
        net.dve(v.tensor_copy(ce[:, :], si[:, :]))
        net.dve(v.tensor_tensor(n[:, :], ce[:, 1:NB], fl[:, 0:NBU], ALU.subtract))
        net.dve(v.tensor_scalar(n[:, :], n[:, :], 1.0, None, ALU.max))
        net.dve(v.tensor_scalar(fl[:, :], fl[:, :], float(T // span - 1), None, ALU.min))
        net.dve(v.tensor_tensor_scan(c[:, :], net.ones[:, 0:NBU], n[:, :], 0.0, ALU.mult, ALU.add))
        net.dve(v.tensor_tensor(g[:, :], fl[:, 0:NBU], c[:, :], ALU.subtract))
        net.dve(v.tensor_tensor(g[:, :], g[:, :], n[:, :], ALU.add))
        net.dve(v.memset(dg[:, :], 0.0))
        net.dve(v.tensor_tensor(dg[:, 0:NBU - 1], g[:, 1:NBU], g[:, 0:NBU - 1], ALU.subtract))
        for k in range(wk):
            net.dve(v.scalar_tensor_tensor(s1[:, :], c[:, :], w[:, k:k + 1], net.ones[:, 0:NBU], ALU.is_le,
                                           ALU.mult, accum_out=bt[:, k, 0:1]))
            net.dve(v.scalar_tensor_tensor(s1[:, :], c[:, :], w[:, k:k + 1], dg[:, :], ALU.is_le,
                                           ALU.mult, accum_out=bt[:, k, 1:2]))
        net.dve(v.tensor_scalar(base128[:, :], bt[:, :, 0], float(P), None, ALU.mult))
        net.dve(v.tensor_tensor(w[:, :], w[:, :], bt[:, :, 1], ALU.add))
        net.dve(v.tensor_scalar(w[:, :], w[:, :], g[:, 0:1], float(T // span - 1), ALU.add, ALU.min))
        net.dve(v.tensor_copy(tile_u[:, :], w[:, :]))
    return base128, tile_u


def to_rows(net, m, tag, cols, dt, broadcast):
    nc = net.nc
    WP = cols.shape[1] * P
    flat = nc.dram_tensor(f"{tag}_flat", [WP], dt).ap()
    row = m.sb(tag, [P if broadcast else 1, WP], dt)
    net.after(nc.sync, net.dve)
    net.load(flat.rearrange("(k p) -> p k", p=P), cols)
    net.load(row[:, :], flat.partition_broadcast(P) if broadcast else flat.rearrange("(a w) -> a w", a=1))
    return row


def item_tables(net, m):
    nc, a = net.nc, net.a
    v = nc.vector
    b128, tiles = item_list(net, m, "itd", net.start_dst, 1, WK)
    net.gsrc = m.sb("gsrc", [P, WK * P], U32)
    net.grel = m.sb("grel", [P, WK * P], U32)
    net.dloc = m.sb("dloc", [P, WK * P])
    with Mem(nc, "ix") as t:
        raw = [t.sb(f"raw{i}", [P, P], I32) for i in range(3)]
        flt = [t.sb(f"flt{i}", [P, P]) for i in range(3)]
        tp = t.ps("tp", [P, 3, P])
        bi = t.sb("bi", [P, WK], I32)
        net.dve(v.tensor_copy(bi[:, :], b128[:, :]))
        net.row_dst = to_rows(net, m, "row_dst", bi[:, :], I32, False)
        for k in range(WK):
            net.after(nc.gpsimd, net.dve)
            for i, name in enumerate(("src", "dst", "rel")):
                net.dma(nc.gpsimd.indirect_dma_start(
                    out=raw[i][:, :], out_offset=None, in_=a[name].rearrange("(t e) -> t e", e=P),
                    in_offset=bass.IndirectOffsetOnAxis(ap=tiles[:, k:k + 1], axis=0)), 16)
            net.after(v, net.dma, net.pe)
            for i in range(3):
                net.dve(v.tensor_copy(flt[i][:, :], raw[i][:, :]))
            net.dve(v.tensor_scalar(flt[1][:, :], flt[1][:, :], b128[:, k:k + 1], None, ALU.subtract))
            net.dve(v.scalar_tensor_tensor(flt[2][:, :], flt[0][:, :], float(RELS), flt[2][:, :], ALU.mult,
                                           ALU.add))
            net.after(nc.tensor, net.dve)
            for i in range(3):
                net.pe(nc.tensor.transpose(tp[:, i, :], flt[i][:, :], net.ident[:, :]))
            net.after(v, net.pe)
            for i, out in enumerate((net.gsrc, net.dloc, net.grel)):
                net.dve(v.tensor_copy(out[:, k * P:(k + 1) * P], tp[:, i, :]))


def node_view(ap):
    return ap.rearrange("(b p) d -> p b d", p=P)


def layer_norm(net, m, dest):
    nc, v, x = net.nc, net.nc.vector, net.x
    h = m.sb("h", [P, NB, D])
    sq = m.sb("sq", [P, NB, D])
    mean = m.sb("mean", [P, NB])
    var = m.sb("var", [P, NB])
    bc = lambda s: s[:, :].unsqueeze(2).to_broadcast([P, NB, D])
    net.dve(v.tensor_reduce(mean[:, :], x[:, :, :], AX.X, ALU.add))
    net.dve(v.tensor_scalar(mean[:, :], mean[:, :], 1.0 / D, None, ALU.mult))
    net.dve(v.tensor_tensor(h[:, :, :], x[:, :, :], bc(mean), ALU.subtract))
    net.dve(v.tensor_tensor(sq[:, :, :], h[:, :, :], h[:, :, :], ALU.mult))
    net.dve(v.tensor_reduce(var[:, :], sq[:, :, :], AX.X, ALU.add))
    net.dve(v.tensor_scalar(var[:, :], var[:, :], 1.0 / D, EPS, ALU.mult, ALU.add))
    net.after(nc.scalar, net.dve)
    net.act(nc.scalar.activation(var[:, :], var[:, :], ACT.Sqrt))
    net.after(v, net.act)
    net.dve(v.reciprocal(var[:, :], var[:, :]))
    net.dve(v.tensor_tensor(h[:, :, :], h[:, :, :], bc(var), ALU.mult))
    net.dve(v.tensor_scalar(h[:, :, :], h[:, :, :], 0.0, None, ALU.max))
    if dest is not None:
        net.after(nc.sync, net.dve)
        net.load(node_view(dest), h[:, :, :])
    return h


def edge_pass(net, e):
    nc, a = net.nc, net.a
    v, s, pe, pool, sp = nc.vector, nc.scalar, nc.tensor, nc.gpsimd, nc.sync
    GP = G * P
    two = range(2)
    w_i = e.sb("w_i", [P, OUTJ])
    w_j = e.sb("w_j", [P, OUTJ])
    att = e.sb("att", [P, 2 * OUTJ])
    before = e.sb("before", [P, P])
    gath = [e.sb(f"gath{q}", [P, G, P]) for q in two]
    in_i = [e.sb(f"in_i{q}", [P, GP]) for q in two]
    in_j = [e.sb(f"in_j{q}", [P, GP]) for q in two]
    srow = [e.sb(f"srow{q}", [P, GP], I32) for q in two]
    lrow = [e.sb(f"lrow{q}", [P, GP]) for q in two]
    oh_lo = [e.sb(f"oh_lo{q}", [P, G, P], BF16) for q in two]
    oh_hi = [e.sb(f"oh_hi{q}", [P, G, NBU], BF16) for q in two]
    oh_loT = [e.sb(f"oh_loT{q}", [P, GP]) for q in two]
    idx_s = [e.sb(f"idx_s{q}", [P, G], U32) for q in two]
    idx_d = [e.sb(f"idx_d{q}", [P, G], U32) for q in two]
    rows = [e.sb(f"rows{q}", [P, G, OUTJ + ROW]) for q in two]
    soft = [e.sb(f"soft{q}", [P, 2 * 2 * OUTJ]) for q in two]
    prod = [e.sb(f"prod{q}", [P, 2 * 2 * OUTJ]) for q in two]
    dots = [e.sb(f"dots{q}", [P, G, 2 * HEADS]) for q in two]
    upto = [e.sb(f"upto{q}", [P, NBU]) for q in two]
    junk_r = e.sb("junk_r", [P, G, P], BF16)
    pick = e.sb("pick", [P, G, NBU])
    rank = [e.sb(f"rank{q}", [P, G]) for q in two]
    base = [e.sb(f"base{q}", [P, G]) for q in two]
    src_g = [e.sb(f"src_g{q}", [P, G]) for q in two]
    place = [e.sb(f"place{q}", [P, G], U32) for q in two]
    tp = e.ps("tp", [P, 4, P])
    z = [e.ps(f"z{q}", [P, 2, 2 * OUTJ]) for q in two]
    at = [e.ps(f"at{q}", [P, G, D]) for q in two]
    nxt = e.ps("nxt", [P, NBU])

    net.load(w_i[:, :], a["W"])
    net.load(w_j[0:D, :], a["W"][D:2 * D, :])
    net.load(w_j[D:2 * D, :], a["W"][0:D, :])
    for half in two:
        net.load(att[:, half * OUTJ:(half + 1) * OUTJ].rearrange("p (h d) -> p h d", h=HEADS),
                 a["att"][:, half * D:(half + 1) * D].partition_broadcast(P))
    net.dve(v.tensor_scalar(before[:, :], net.iota[:, :], net.part[:, 0:1], None, ALU.is_lt))
    net.dve(v.memset(rows[1][:, :, :], 0.0))
    net.dve(v.memset(rows[0][:, :, OUTJ + ROW - 3:OUTJ + ROW], 0.0))
    spare_i = place[1][:, :].bitcast(I32)
    net.pool(pool.iota(spare_i, [[P, G]], base=EP, channel_multiplier=1))
    net.after(pe, net.dve, net.sp)
    net.after(v, net.sp)
    net.pe(pe.matmul(nxt[:, :], net.ident[:, :], net.first[:, :], start=True, stop=False, skip_group_check=True))

    c = lambda name: Count(nc, "edge_" + name)
    indexed, gathered = c("indexed"), [c(f"gathered{q}") for q in two]
    loaded_e, loaded_s = [c(f"loaded_e{q}") for q in two], [c(f"loaded_s{q}") for q in two]
    turned, copied = c("turned"), c("copied")
    z_done = c("z_done")
    abs_done, exp_done, ln_done = c("abs_done"), c("exp_done"), c("ln_done")
    soft_done, prod_done, dot_done = c("soft_done"), c("prod_done"), c("dot_done")
    picked = c("picked")
    onehots, ranked, saved, moved, based = c("onehots"), c("ranked"), c("saved"), c("moved"), c("based")
    rows_done = c("rows_done")
    scattered = [c(f"scattered{q}") for q in two]

    def load_group(c0, q):
        e0 = c0 * P
        wait(sp, z_done, back=1)
        loaded_e[q].up(sp.dma_start(in_i[q][D:2 * D, :], a["edge_t"][:, bass.ds(e0, GP)]), 16)
        loaded_e[q].up(sp.dma_start(in_j[q][0:D, :], a["edge_t"][:, bass.ds(e0, GP)]), 16)
        wait(sp, ranked)
        wait(sp, onehots, back=1)
        loaded_s[q].up(sp.dma_start(srow[q][:, :], a["src"][bass.ds(e0, GP)].partition_broadcast(P)), 16)
        loaded_s[q].up(sp.dma_start(lrow[q][:, :], net.lo_d[bass.ds(e0, GP)].partition_broadcast(P)), 16)

    def gather(c0, q):
        wait(pool, turned, back=2)
        indexed.up(pool.tensor_copy(idx_s[q][:, :], net.src_u[:, bass.ds(c0, G)]))
        indexed.up(pool.tensor_copy(idx_d[q][:, :], net.dst_u[:, bass.ds(c0, G)]))
        wait(pool, indexed)
        for j in range(G):
            for half, idx in ((0, idx_s), (1, idx_d)):
                gathered[q].up(pool.indirect_dma_start(
                    out=gath[q][:, j, half * D:(half + 1) * D], out_offset=None, in_=net.h0_d,
                    in_offset=bass.IndirectOffsetOnAxis(ap=idx[q][:, j:j + 1], axis=0)), 16)

    def turn(q):
        wait(pe, gathered[q])
        for half in two:
            wait(pe, copied)
            for j in range(4):
                ins = pe.transpose(tp[:, j, :], gath[q][:, 4 * half + j, :], net.ident[:, :])
            turned.up(ins)
            wait(s, turned)
            cols = bass.ds(half * 4 * P, 4 * P)
            s.copy(in_i[q][0:D, cols], tp[0:D, :, :].rearrange("p j e -> p (j e)"))
            copied.up(s.copy(in_j[q][D:2 * D, cols], tp[D:2 * D, :, :].rearrange("p j e -> p (j e)")))
        wait(pe, loaded_e[q])
        wait(pe, copied)

    def out_of(q, j):
        zj = z[j // 2 % 2][:, j % 2, :]
        pe.matmul(zj[:, 0:OUTJ], in_i[q][:, j * P:(j + 1) * P], w_i[:, :], start=True, stop=True)
        return pe.matmul(zj[:, OUTJ:2 * OUTJ], in_j[q][:, j * P:(j + 1) * P], w_j[:, :], start=True,
                         stop=True)

    def one_hots(c0, q):
        wait(v, loaded_s[q])
        v.tensor_copy(src_g[q][:, :], net.src_f[:, bass.ds(c0, G)])
        v.tensor_tensor(oh_lo[q][:, :, :], net.iota_b[:, None, :].to_broadcast([P, G, P]),
                        net.lo_b[:, bass.ds(c0, G)].unsqueeze(2).to_broadcast([P, G, P]), ALU.is_equal)
        v.tensor_tensor(oh_hi[q][:, :, :], net.iota_b[:, None, 0:NBU].to_broadcast([P, G, NBU]),
                        net.hi_b[:, bass.ds(c0, G)].unsqueeze(2).to_broadcast([P, G, NBU]), ALU.is_equal)
        onehots.up(v.tensor_scalar(oh_loT[q][:, :], lrow[q][:, :], net.part[:, 0:1], None, ALU.is_equal))

    def running(q, j):
        wait(s, moved)
        saved.up(s.copy(upto[j % 2][:, :], nxt[:, :]))
        if j == 0:
            wait(pe, onehots)
            wait(pe, based, back=1)
        wait(pe, saved)
        pe.matmul(at[q][:, j, 0:NBU], oh_loT[q][:, j * P:(j + 1) * P], upto[j % 2][:, :],
                  start=True, stop=True)
        moved.up(pe.matmul(nxt[:, :], oh_lo[q][:, j, :], oh_hi[q][:, j, :], start=False,
                           stop=False, skip_group_check=True))

    def scatter(q):
        wait(pool, rows_done)
        for j in range(G):
            scattered[q].up(pool.indirect_dma_start(
                out=net.rows_d, out_offset=bass.IndirectOffsetOnAxis(ap=place[q][:, j:j + 1], axis=0),
                in_=rows[q][:, j, OUTJ:OUTJ + ROW], in_offset=None), 16)

    for cnt, eng, n in ((turned, pe, 3), (z_done, pe, 2), (copied, s, 1), (soft_done, v, 2),
                        (moved, pe, 1), (onehots, v, 2), (ranked, v, 1), (based, v, 2), (rows_done, v, 1)):
        cnt.credit(eng, n)
    net.after(pool, net.dve)
    scattered[0].up(pool.dma_start(net.spare_d[0], rows[1][:, 0, 0:1]), 16)
    load_group(0, 0)
    gather(0, 0)
    turn(0)
    for j in (0, 1):
        ins = out_of(0, j)
    z_done.up(ins)
    one_hots(0, 0)
    per = {indexed: 4, gathered[0]: 256, gathered[1]: 256, loaded_e[0]: 32, loaded_e[1]: 32,
           loaded_s[0]: 32, loaded_s[1]: 32, turned: 4, copied: 4, z_done: 8,
           abs_done: 8, exp_done: 8, ln_done: 8, soft_done: 8, prod_done: 8, dot_done: 8, onehots: 2,
           ranked: 2 * G, saved: 2 * G, moved: 2 * G, based: 2, picked: 2, rows_done: 2,
           scattered[0]: 128, scattered[1]: 128}
    with Loop(nc, T // (2 * G), per) as it:
        for q in two:
            c0 = (it * 2 + q) * G
            load_group(c0 + G, 1 - q)
            gather(c0 + G, 1 - q)
            scatter(1 - q)
            for k in range(G // 2):
                soft_k = soft[k % 2][:, :]
                running(q, 2 * k)
                wait(s, z_done)
                wait(s, soft_done, back=1)
                abs_done.up(s.activation(soft_k, z[k % 2][:, :, :].rearrange("p t f -> p (t f)"), ACT.Abs))
                if k + 1 < G // 2:
                    wait(pe, soft_done)
                    out_of(q, 2 * k + 2)
                wait(s, abs_done)
                exp_done.up(s.activation(soft_k, soft_k, ACT.Exp, scale=-1.0))
                running(q, 2 * k + 1)
                if k + 1 < G // 2:
                    z_done.up(out_of(q, 2 * k + 3))
                wait(s, exp_done)
                ln_done.up(s.activation(soft_k, soft_k, ACT.Ln, bias=1.0))
                if k + 1 == G // 2:
                    turn(1 - q)
                    wait(pe, soft_done)
                    for j in (0, 1):
                        ins = out_of(1 - q, j)
                    z_done.up(ins)

                if k == 0:
                    wait(v, scattered[q])
                wait(v, ln_done)
                rk = rows[q][:, 2 * k:2 * k + 2, 0:2 * OUTJ]
                soft_done.up(v.scalar_tensor_tensor(rk, z[k % 2][:, :, :], 0.0,
                                                    soft_k.rearrange("p (t f) -> p t f", t=2),
                                                    ALU.max, ALU.add))
                if k == 0:
                    wait(v, onehots)
                for j in (2 * k, 2 * k + 1):
                    ranked.up(v.scalar_tensor_tensor(
                        junk_r[:, j, :], srow[q][:, j * P:(j + 1) * P], src_g[q][:, j:j + 1],
                        before[:, :], ALU.is_equal, ALU.mult, accum_out=rank[q][:, j:j + 1]))
                wait(v, soft_done)
                prod_done.up(v.tensor_tensor(prod[k % 2][:, :].rearrange("p (t f) -> p t f", t=2), rk,
                                             att[:, None, :].to_broadcast([P, 2, 2 * OUTJ]), ALU.mult))
                wait(v, prod_done)
                dot_done.up(v.tensor_reduce(
                    dots[q][:, 2 * k:2 * k + 2, :].rearrange("p t h -> p (t h)"),
                    prod[k % 2][:, :].rearrange("p (g d) -> p g d", d=D), AX.X, ALU.add))
                if k == 2:
                    wait(v, moved, back=6)
                    one_hots(c0 + G, 1 - q)

            wait(v, moved)
            picked.up(v.tensor_tensor(pick[:, :, :], oh_hi[q][:, :, :], at[q][:, :, 0:NBU], ALU.mult))
            wait(v, picked)
            based.up(v.tensor_reduce(base[q][:, :], pick[:, :, :], AX.X, ALU.add))
            wait(v, based)
            wait(v, dot_done)
            v.tensor_copy(rows[q][:, :, 2 * OUTJ + HEADS:2 * OUTJ + HEADS + 1],
                          src_g[q][:, :].unsqueeze(2))
            v.tensor_tensor(place[q][:, :], rank[q][:, :], base[q][:, :], ALU.add)
            rows_done.up(v.tensor_tensor(rows[q][:, :, 2 * OUTJ:2 * OUTJ + HEADS], dots[q][:, :, 0:HEADS],
                                         dots[q][:, :, HEADS:2 * HEADS], ALU.add))
    scatter(1)
    for q in two:
        wait(pool, scattered[q])
        wait(pool, gathered[q])


def softplus(net, out, x, tmp):
    nc = net.nc
    net.after(nc.scalar, net.dve)
    net.act(nc.scalar.activation(tmp, x, ACT.Abs))
    net.act(nc.scalar.activation(tmp, tmp, ACT.Exp, scale=-1.0))
    net.act(nc.scalar.activation(tmp, tmp, ACT.Ln, bias=1.0))
    net.after(nc.vector, net.act)
    net.dve(nc.vector.scalar_tensor_tensor(out, x, 0.0, tmp, ALU.max, ALU.add))


def all_sum(net, out, part, ps):
    nc = net.nc
    net.after(nc.tensor, net.dve)
    net.pe(nc.tensor.matmul(ps, net.ones[:, :], part, start=True, stop=True))
    net.after(nc.vector, net.pe)
    net.dve(nc.vector.tensor_copy(out, ps))


def edge_softmax(net):
    nc, a = net.nc, net.a
    v = nc.vector
    view = net.rows_d[0:EP].rearrange("(p c) r -> p c r", c=T)
    with Mem(nc, "sm") as t:
        al = t.sb("al", [P, T, HEADS + 1])
        keep_f = t.sb("keep_f", [P, T])
        keep_b = t.sb("keep_b", [P, T])
        be = t.sb("be", [P, HEADS, T])
        fw = t.sb("fw", [P, HEADS, T])
        tot = t.sb("tot", [P, HEADS, T])
        prv, nxt = t.sb("prv", [P, 1]), t.sb("nxt", [P, 1])
        k_f, k_b = t.sb("k_f", [P, HEADS]), t.sb("k_b", [P, HEADS])
        s1, s2 = t.sb("s1", [P, HEADS]), t.sb("s2", [P, HEADS])
        mu, scale = t.sb("mu", [P, HEADS]), t.sb("scale", [P, HEADS])
        gam, bet = t.sb("gam", [P, HEADS]), t.sb("bet", [P, HEADS])
        line, line_k = t.sb("line", [HEADS, P]), t.sb("line_k", [HEADS, P])
        carry = t.sb("carry", [HEADS, P])
        ps = t.ps("ps", [P, HEADS])
        ps_l = t.ps("ps_l", [HEADS, 2, P])

        net.dve(v.memset(prv[:, :], -1.0))
        net.dve(v.memset(nxt[:, :], -1.0))
        net.after(nc.sync, net.dve)
        net.load(al[:, :, :], view[:, :, OUTJ:OUTJ + HEADS + 1])
        net.load(prv[1:P, :], view[0:P - 1, T - 1, OUTJ + HEADS:OUTJ + HEADS + 1])
        net.load(nxt[0:P - 1, :], view[1:P, 0, OUTJ + HEADS:OUTJ + HEADS + 1])
        net.load(gam[:, :], a["gamma"].partition_broadcast(P))
        net.load(bet[:, :], a["beta"].partition_broadcast(P))
        net.after(v, net.sp)
        src = al[:, :, HEADS]
        net.dve(v.tensor_tensor(keep_f[:, 1:T], src[:, 1:T], src[:, 0:T - 1], ALU.is_equal))
        net.dve(v.tensor_tensor(keep_f[:, 0:1], src[:, 0:1], prv[:, :], ALU.is_equal))
        net.dve(v.tensor_copy(keep_b[:, 0:T - 1], keep_f[:, 1:T]))
        net.dve(v.tensor_tensor(keep_b[:, T - 1:T], src[:, T - 1:T], nxt[:, :], ALU.is_equal))
        for k, keep in ((k_f, keep_f), (k_b, keep_b)):
            net.dve(v.tensor_reduce(prv[:, :], keep[:, :], AX.X, ALU.min))
            net.dve(v.tensor_copy(k[:, :], prv[:, :].to_broadcast([P, HEADS])))

        softplus(net, be[:, :, :], al[:, :, 0:HEADS].rearrange("p c h -> p h c"), fw[:, :, :])
        mask_i, mask = tot[:, 0, :].bitcast(I32), tot[:, 1, :]
        net.after(nc.gpsimd, net.dve)
        net.pool(nc.gpsimd.iota(mask_i, [[1, T]], base=0, channel_multiplier=T))
        net.after(v, net.pool)
        net.dve(v.tensor_copy(mask, mask_i))
        net.dve(v.tensor_scalar(mask, mask, float(E), None, ALU.is_lt))
        mask_h = tot[:, 1:2, :].to_broadcast([P, HEADS, T])
        head = lambda s: s[:, :].unsqueeze(2).to_broadcast([P, HEADS, T])
        net.dve(v.tensor_tensor(fw[:, :, :], be[:, :, :], mask_h, ALU.mult))
        net.dve(v.tensor_reduce(s1[:, :], fw[:, :, :], AX.X, ALU.add))
        all_sum(net, mu[:, :], s1[:, :], ps[:, :])
        net.dve(v.tensor_scalar(mu[:, :], mu[:, :], 1.0 / E, None, ALU.mult))
        net.dve(v.tensor_tensor(be[:, :, :], be[:, :, :], head(mu), ALU.subtract))
        net.dve(v.tensor_tensor(fw[:, :, :], be[:, :, :], mask_h, ALU.mult))
        net.dve(v.tensor_tensor(fw[:, :, :], fw[:, :, :], fw[:, :, :], ALU.mult))
        net.dve(v.tensor_reduce(s1[:, :], fw[:, :, :], AX.X, ALU.add))
        all_sum(net, scale[:, :], s1[:, :], ps[:, :])
        net.dve(v.tensor_scalar(scale[:, :], scale[:, :], 1.0 / E, EPS, ALU.mult, ALU.add))
        net.after(nc.scalar, net.dve)
        net.act(nc.scalar.activation(scale[:, :], scale[:, :], ACT.Sqrt))
        net.after(v, net.act)
        net.dve(v.reciprocal(scale[:, :], scale[:, :]))
        net.dve(v.tensor_tensor(scale[:, :], scale[:, :], gam[:, :], ALU.mult))
        for h in range(HEADS):
            net.dve(v.tensor_scalar(be[:, h, :], be[:, h, :], scale[:, h:h + 1], bet[:, h:h + 1], ALU.mult,
                                    ALU.add))
        softplus(net, be[:, :, :], be[:, :, :], fw[:, :, :])

        def carried(ends, keeps, op, back):
            net.dve(v.tensor_copy(s2[:, :], ends))
            net.after(nc.tensor, net.dve)
            net.pe(nc.tensor.transpose(ps_l[:, 0, :], s2[:, :], net.ident[:, :]))
            net.pe(nc.tensor.transpose(ps_l[:, 1, :], keeps[:, :], net.ident[:, :]))
            net.after(v, net.pe)
            net.dve(v.tensor_copy(line[:, :], ps_l[:, 0, :]))
            net.dve(v.tensor_copy(line_k[:, :], ps_l[:, 1, :]))
            net.dve(v.memset(carry[:, :], 0.0))
            if back:
                net.dve(v.tensor_tensor_scan(carry[:, P - 2::-1], line_k[:, P - 1:0:-1], line[:, P - 1:0:-1],
                                             0.0, ALU.mult, op))
            else:
                net.dve(v.tensor_tensor_scan(carry[:, 1:P], line_k[:, 0:P - 1], line[:, 0:P - 1], 0.0,
                                             ALU.mult, op))
            net.after(nc.tensor, net.dve)
            net.pe(nc.tensor.transpose(ps[:, :], carry[:, :], net.ident[0:HEADS, 0:HEADS]))
            net.after(v, net.pe)
            net.dve(v.tensor_copy(s2[:, :], ps[:, :]))

        def segments(op):
            for first in (True, False):
                for h in range(HEADS):
                    net.dve(v.tensor_tensor_scan(fw[:, h, :], keep_f[:, :], be[:, h, :],
                                                 0.0 if first else s2[:, h:h + 1], ALU.mult, op))
                if first:
                    carried(fw[:, :, T - 1], k_f, op, False)
            for first in (True, False):
                for h in range(HEADS):
                    net.dve(v.tensor_tensor_scan(tot[:, h, ::-1], keep_b[:, ::-1], fw[:, h, ::-1],
                                                 0.0 if first else s2[:, h:h + 1], ALU.mult, ALU.max))
                if first:
                    carried(tot[:, :, 0], k_b, ALU.max, True)

        segments(ALU.max)
        net.dve(v.tensor_tensor(be[:, :, :], be[:, :, :], tot[:, :, :], ALU.subtract))
        net.after(nc.scalar, net.dve)
        net.act(nc.scalar.activation(be[:, :, :], be[:, :, :], ACT.Exp))
        net.after(v, net.act)
        segments(ALU.add)
        net.dve(v.tensor_scalar(tot[:, :, :], tot[:, :, :], 1e-16, None, ALU.add))
        net.dve(v.reciprocal(tot[:, :, :], tot[:, :, :]))
        net.dve(v.tensor_tensor(al[:, :, 0:HEADS].rearrange("p c h -> p h c"), be[:, :, :], tot[:, :, :],
                                ALU.mult))
        net.after(nc.sync, net.dve)
        net.load(view[:, :, OUTJ:OUTJ + HEADS], al[:, :, 0:HEADS])


def item_values(nc, eng, row, top):
    _, values = nc.values_load_multi_w_load_instructions(
        row[0:1, :], engines=(eng.engine,), min_val=0, max_val=top,
        skip_runtime_bounds_check_because="the item lists are clamped to this range")
    return values


def free_values(nc, values):
    for value in values:
        for reg in value.val.handles:
            nc.free_register(reg)


def add_items(net, acc, added, blk, sums, cols):
    nc, v = net.nc, net.nc.vector
    blocks = item_values(nc, v, blk, NBU * P)
    for j in range(blk.shape[1]):
        wait(v, added)
        with Temporaries(nc, v):
            here = acc[:, bass.ds(blocks[j], cols)]
            added.up(v.tensor_tensor(here, here, sums(j), ALU.add))
    free_values(nc, blocks)


def attention_sum(net, acc):
    nc = net.nc
    v, s, pe, pool, sp = nc.vector, nc.scalar, nc.tensor, nc.gpsimd, nc.sync
    two = range(2)
    flat = net.rows_d.rearrange("e r -> (e r)")
    size = SPAN * P * ROW
    with Mem(nc, "at") as t:
        rows = [t.sb(f"rows{q}", [P, GS, SPAN, ROW]) for q in two]
        wtd = [t.sb(f"wtd{q}", [P, G, OUTJ]) for q in two]
        msg = [t.sb(f"msg{q}", [P, G, D]) for q in two]
        loc = [t.sb(f"loc{q}", [P, G]) for q in two]
        oh = [t.sb(f"oh{q}", [P, G, P]) for q in two]
        blk = [t.sb(f"blk{q}", [1, GS], I32) for q in two]
        til = [t.sb(f"til{q}", [1, GS], I32) for q in two]
        ps = [t.ps(f"ps{q}", [P, GS, P]) for q in two]
        c = lambda name: Count(nc, "att_" + name)
        loaded = [c(f"loaded{q}") for q in two]
        weighted, placed, summed, added, messaged, onehot, listed_t, listed_b = map(
            c, ("weighted", "placed", "summed", "added", "messaged", "onehot", "listed_t", "listed_b"))
        net.dve(v.memset(acc[:, :], 0.0))
        for cnt, eng, n in ((weighted, pool, 3), (messaged, v, 2), (onehot, v, 3), (summed, pe, 2),
                            (added, v, GS + 1)):
            cnt.credit(eng, n)

        def front(w0, q, ahead):
            wait(s, weighted, back=1)
            listed_t.up(s.copy(til[q][:, :], net.row_tsrc[:, bass.ds(w0, GS)]))
            wait(sp, listed_t)
            wait(sp, weighted, back=1)
            wait(sp, onehot, back=1)
            starts = item_values(nc, sp, til[q], (T // SPAN - 1) * size)
            with Temporaries(nc, sp):
                for j in range(GS):
                    tiles = flat[bass.ds(starts[j], size)].rearrange("(t p r) -> p t r", p=P, t=SPAN)
                    loaded[q].up(sp.dma_start(rows[q][:, j, :, :], tiles), 16)
            free_values(nc, starts)
            rq = rows[q][:, :, :, :].rearrange("p g t r -> p (g t) r")
            wait(pool, loaded[q])
            wait(pool, messaged, back=1)
            weighted.up(pool.tensor_tensor(
                wtd[q][:, :, :].rearrange("p g (h d) -> p g h d", h=HEADS),
                rq[:, :, 0:OUTJ].rearrange("p g (h d) -> p g h d", h=HEADS),
                rq[:, :, OUTJ:OUTJ + HEADS].unsqueeze(3).to_broadcast([P, G, HEADS, D]), ALU.mult))
            wait(v, loaded[q])
            wait(v, summed, back=ahead)
            placed.up(v.tensor_tensor(
                loc[q][:, :].rearrange("p (g t) -> p g t", t=SPAN), rows[q][:, :, :, OUTJ + HEADS],
                net.bsrc[:, bass.ds(w0, GS)].unsqueeze(2).to_broadcast([P, GS, SPAN]), ALU.subtract))
            wait(v, placed)
            onehot.up(v.tensor_tensor(oh[q][:, :, :], net.iota[:, None, :].to_broadcast([P, G, P]),
                                      loc[q][:, :].unsqueeze(2).to_broadcast([P, G, P]), ALU.is_equal))
            wait(v, weighted)
            messaged.up(v.tensor_reduce(msg[q][:, :, :],
                                        wtd[q][:, :, :].rearrange("p g (h d) -> p g d h", h=HEADS),
                                        AX.X, ALU.add))

        front(0, 0, 1)
        per = {loaded[0]: 16 * GS, loaded[1]: 16 * GS, weighted: 2, placed: 2, summed: 2, added: 2 * GS,
               messaged: 2, onehot: 2, listed_t: 2, listed_b: 2}
        with Loop(nc, WS // (2 * GS), per) as it:
            for q in two:
                w0 = (it * 2 + q) * GS
                wait(s, added, back=GS)
                listed_b.up(s.copy(blk[q][:, :], net.row_bsrc[:, bass.ds(w0, GS)]))
                wait(pe, messaged)
                wait(pe, added, back=GS)
                for j in range(GS):
                    for k in range(SPAN):
                        n = j * SPAN + k
                        ins = pe.matmul(ps[q][:, j, 0:D], oh[q][:, n, :], msg[q][:, n, :],
                                        start=k == 0, stop=k == SPAN - 1)
                summed.up(ins)
                front(w0 + GS, 1 - q, 1)
                wait(v, listed_b)
                wait(v, summed)
                add_items(net, acc, added, blk[q], lambda j: ps[q][:, j, 0:D], D)


def gather_sum(net, tag, table, index, acc, cols, ones=False):
    nc = net.nc
    v, s, pe, pool = nc.vector, nc.scalar, nc.tensor, nc.gpsimd
    two = range(2)
    wide = cols + (1 if ones else 0)
    with Mem(nc, tag) as t:
        got = [t.sb(f"got{q}", [P, G, wide + wide % 2]) for q in two]
        idx = [t.sb(f"idx{q}", [P, G], U32) for q in two]
        oh = [t.sb(f"oh{q}", [P, G, P]) for q in two]
        blk = [t.sb(f"blk{q}", [1, G], I32) for q in two]
        ps = [t.ps(f"ps{q}", [P, G, P]) for q in two]
        c = lambda name: Count(nc, f"{tag}_{name}")
        gathered = [c(f"gathered{q}") for q in two]
        indexed, onehot, summed, added, listed = map(c, ("indexed", "onehot", "summed", "added", "listed"))
        net.dve(v.memset(acc[:, :], 0.0))
        if ones:
            for q in two:
                net.dve(v.memset(got[q][:, :, cols:wide], 1.0))
            net.after(pe, net.dve)
        for cnt, eng, n in ((summed, pe, 2), (added, v, G + 1)):
            cnt.credit(eng, n)

        def one_hots(w0, q):
            onehot.up(v.tensor_tensor(oh[q][:, :, :], net.iota[:, None, :].to_broadcast([P, G, P]),
                                      net.dloc[:, bass.ds(w0, G)].unsqueeze(2).to_broadcast([P, G, P]),
                                      ALU.is_equal))

        one_hots(0, 0)
        with Loop(nc, W // (2 * G), {gathered[0]: 16 * G, gathered[1]: 16 * G, indexed: 2, onehot: 2,
                                     summed: 2, added: 2 * G, listed: 2}) as it:
            for q in two:
                w0 = (it * 2 + q) * G
                wait(s, summed, back=1)
                indexed.up(s.copy(idx[q][:, :], index[:, bass.ds(w0, G)]))
                wait(s, added, back=G)
                listed.up(s.copy(blk[q][:, :], net.row_dst[:, bass.ds(w0, G)]))
                wait(pool, indexed)
                wait(pool, summed, back=1)
                for j in range(G):
                    gathered[q].up(pool.indirect_dma_start(
                        out=got[q][:, j, 0:cols], out_offset=None, in_=table,
                        in_offset=bass.IndirectOffsetOnAxis(ap=idx[q][:, j:j + 1], axis=0)), 16)
                wait(v, summed)
                wait(pe, onehot)
                one_hots(w0 + G, 1 - q)
                wait(pe, gathered[q])
                wait(pe, added, back=G)
                for j in range(G):
                    ins = pe.matmul(ps[q][:, j, 0:wide], oh[q][:, j, :], got[q][:, j, 0:wide], start=True,
                                    stop=True)
                summed.up(ins)
                wait(v, listed)
                wait(v, summed)
                add_items(net, acc, added, blk[q], lambda j: ps[q][:, j, 0:wide], wide)


def by_block(acc):
    return acc[:, :].rearrange("p (b s) -> p b s", s=P)


def relation_table(net, tag, h, w, table):
    nc = net.nc
    v, s, pe, sp = nc.vector, nc.scalar, nc.tensor, nc.sync
    two = range(2)
    wide = RELS * D
    part = wide // 3
    with Mem(nc, tag) as t:
        ws = t.sb("ws", [D, RELS, D])
        hs = [t.sb(f"hs{q}", [P, D]) for q in two]
        ht = [t.sb(f"ht{q}", [D, P]) for q in two]
        out = [t.sb(f"out{q}", [P, wide]) for q in two]
        tp = t.ps("tp", [D, P])
        ps = [t.ps(f"ps{q}", [P, wide]) for q in two]
        c = lambda name: Count(nc, f"{tag}_{name}")
        taken, turned, copied, done, emptied_s, emptied_v = map(
            c, ("taken", "turned", "copied", "done", "emptied_s", "emptied_v"))
        stored = [c(f"stored{q}") for q in two]
        net.load(ws[:, :, :], w.rearrange("r d f -> d r f"))
        net.after(pe, net.sp, net.dve)
        for cnt, eng, n in ((turned, pe, 2), (done, pe, 2), (emptied_s, s, 2), (emptied_v, v, 2)):
            cnt.credit(eng, n)
        for q in two:
            net.dve(v.memset(out[q][:, 0:1], 0.0))
            net.after(sp, net.dve)
            stored[q].up(sp.dma_start(net.spare_d[q], out[q][:, 0:1]), 16)
        with Loop(nc, NB // 2, {taken: 2, turned: 2, copied: 2, done: 2, emptied_s: 2, emptied_v: 2,
                                stored[0]: 16, stored[1]: 16}) as it:
            for q in two:
                b = it * 2 + q
                wait(v, turned, back=1)
                taken.up(v.tensor_copy(hs[q][:, :], h[:, bass.ds(b, 1), :].rearrange("p b d -> p (b d)")))
                wait(pe, taken)
                turned.up(pe.transpose(tp[:, :], hs[q][:, :], net.ident[:, :]))
                wait(v, turned)
                wait(v, done, back=1)
                copied.up(v.tensor_copy(ht[q][:, :], tp[:, :]))
                wait(pe, copied)
                wait(pe, emptied_s, back=1)
                wait(pe, emptied_v, back=1)
                for k in range(3):
                    ins = pe.matmul(ps[q][:, k * part:(k + 1) * part], ht[q][:, :],
                                    ws[:, :, :].rearrange("d r f -> d (r f)")[:, k * part:(k + 1) * part],
                                    start=True, stop=True)
                done.up(ins)
                wait(s, done)
                wait(s, stored[q])
                emptied_s.up(s.copy(out[q][:, 0:2 * part], ps[q][:, 0:2 * part]))
                wait(v, done)
                wait(v, stored[q])
                emptied_v.up(v.tensor_copy(out[q][:, 2 * part:wide], ps[q][:, 2 * part:wide]))
                wait(sp, emptied_s)
                wait(sp, emptied_v)
                stored[q].up(sp.dma_start(
                    table.rearrange("(b p) f -> p b f", p=P)[:, bass.ds(b, 1), :],
                    out[q][:, :].unsqueeze(1)), 16)
        for q in two:
            wait(sp, stored[q])


def relation_layer(net, tag, table, acc, h):
    v = net.nc.vector
    gather_sum(net, tag, table.rearrange("n (r f) -> (n r) f", f=D), net.grel, acc, D)
    net.dve(v.tensor_tensor(h[:, :, :], by_block(acc)[:, :, 0:D],
                            net.rdeg[:, :].unsqueeze(2).to_broadcast([P, NB, D]), ALU.mult))
    net.dve(v.tensor_scalar(h[:, :, :], h[:, :, :], 0.0, None, ALU.max))


def channel_tables(net, h, own, table):
    nc, a = net.nc, net.a
    v, s, pe, sp = nc.vector, nc.scalar, nc.tensor, nc.sync
    two = range(2)
    with Mem(nc, "ch") as t:
        ws = t.sb("ws", [D + 1, 5 * D])
        hs = [t.sb(f"hs{q}", [P, D + 1]) for q in two]
        nb = [t.sb(f"nb{q}", [P, 1]) for q in two]
        ht = [t.sb(f"ht{q}", [D + 1, P]) for q in two]
        out = [t.sb(f"out{q}", [P, 2 * D]) for q in two]
        tp = t.ps("tp", [D + 1, P])
        ps = [t.ps(f"ps{q}", [P, 5 * D]) for q in two]
        c = lambda name: Count(nc, f"ch_{name}")
        taken, turned, copied, done, kept, scaled = map(
            c, ("taken", "turned", "copied", "done", "kept", "scaled"))
        stored = [c(f"stored{q}") for q in two]
        for i, name in enumerate(("self", "self_high", "id", "neigh", "neigh_high")):
            net.load(ws[0:D, i * D:(i + 1) * D], a["Wt_" + name])
            net.load(ws[D:D + 1, i * D:(i + 1) * D], a["b_" + name].rearrange("(a d) -> a d", a=1))
        for q in two:
            net.dve(v.memset(hs[q][:, D:D + 1], 1.0))
            net.dve(v.memset(out[q][:, 0:1], 0.0))
            net.after(sp, net.dve)
            stored[q].up(sp.dma_start(net.spare_d[q], out[q][:, 0:1]), 16)
        net.after(pe, net.sp, net.dve)
        for cnt, eng, n in ((turned, pe, 2), (done, pe, 2), (kept, s, 2), (scaled, v, 2)):
            cnt.credit(eng, n)
        with Loop(nc, NB // 2, {taken: 2, turned: 2, copied: 2, done: 2, kept: 2, scaled: 2,
                                stored[0]: 16, stored[1]: 16}) as it:
            for q in two:
                b = it * 2 + q
                wait(v, turned, back=1)
                wait(v, scaled, back=1)
                v.tensor_copy(nb[q][:, :], net.norm[:, bass.ds(b, 1)])
                taken.up(v.tensor_copy(hs[q][:, 0:D], h[:, bass.ds(b, 1), :].rearrange("p b d -> p (b d)")))
                wait(pe, taken)
                turned.up(pe.transpose(tp[:, :], hs[q][:, :], net.ident[:, :]))
                wait(v, turned)
                wait(v, done, back=1)
                copied.up(v.tensor_copy(ht[q][:, :], tp[:, :]))
                wait(pe, copied)
                wait(pe, kept, back=1)
                wait(pe, scaled, back=1)
                done.up(pe.matmul(ps[q][:, :], ht[q][:, :], ws[:, :], start=True, stop=True))
                wait(s, done)
                kept.up(s.activation(own[:, bass.ds(b, 1), :].rearrange("p b f -> p (b f)"),
                                     ps[q][:, 0:3 * D], ACT.Relu))
                wait(v, kept)
                wait(v, taken)
                wait(v, stored[q])
                scaled.up(v.tensor_scalar(out[q][:, :], ps[q][:, 3 * D:5 * D], 0.0, nb[q][:, 0:1], ALU.max,
                                          ALU.mult))
                wait(sp, scaled)
                stored[q].up(sp.dma_start(
                    table.rearrange("(b p) f -> p b f", p=P)[:, bass.ds(b, 1), :],
                    out[q][:, :].unsqueeze(1)), 16)
        for q in two:
            wait(sp, stored[q])


def channel_mix(net, acc, own):
    nc, a = net.nc, net.a
    v, s = nc.vector, nc.scalar
    with Mem(nc, "mix") as t:
        wa = t.sb("wa", [P, 3, D])
        w3 = t.sb("w3", [P, 3, 3])
        tmp = t.sb("tmp", [P, NB, D])
        lg = t.sb("lg", [P, NB, 3])
        at = t.sb("at", [P, NB, 3])
        pr = t.sb("pr", [P, NB, 3])
        mx = t.sb("mx", [P, NB])
        for i, name in enumerate(("low", "high", "mlp")):
            net.load(wa[:, i, :], a["att_" + name].partition_broadcast(P))
        net.load(w3[:, :, :], a["W_att"].partition_broadcast(P))
        net.after(v, net.sp)
        by_node = lambda x, n: x[:, :].unsqueeze(2).to_broadcast([P, NB, n])
        for i, op in ((0, ALU.add), (1, ALU.subtract)):
            o = own[:, :, i * D:(i + 1) * D]
            net.dve(v.tensor_tensor(tmp[:, :, :], by_block(acc)[:, :, i * D:(i + 1) * D],
                                    by_node(net.rdeg, D), ALU.mult))
            net.dve(v.tensor_tensor(o, o, tmp[:, :, :], op))
        for i in range(3):
            net.dve(v.tensor_tensor(tmp[:, :, :], own[:, :, i * D:(i + 1) * D],
                                    wa[:, i:i + 1, :].to_broadcast([P, NB, D]), ALU.mult))
            net.dve(v.tensor_reduce(lg[:, :, i], tmp[:, :, :], AX.X, ALU.add))
        net.after(s, net.dve)
        net.act(s.activation(lg[:, :, :], lg[:, :, :], ACT.Sigmoid))
        net.after(v, net.act)
        for j in range(3):
            net.dve(v.tensor_tensor(pr[:, :, :], lg[:, :, :], w3[:, j:j + 1, :].to_broadcast([P, NB, 3]),
                                    ALU.mult))
            net.dve(v.tensor_reduce(at[:, :, j], pr[:, :, :], AX.X, ALU.add))
        net.dve(v.tensor_scalar(at[:, :, :], at[:, :, :], 1.0 / 3.0, None, ALU.mult))
        net.dve(v.tensor_reduce(mx[:, :], at[:, :, :], AX.X, ALU.max))
        net.dve(v.tensor_tensor(at[:, :, :], at[:, :, :], by_node(mx, 3), ALU.subtract))
        net.after(s, net.dve)
        net.act(s.activation(at[:, :, :], at[:, :, :], ACT.Exp))
        net.after(v, net.act)
        net.dve(v.tensor_reduce(mx[:, :], at[:, :, :], AX.X, ALU.add))
        net.dve(v.reciprocal(mx[:, :], mx[:, :]))
        net.dve(v.tensor_scalar(mx[:, :], mx[:, :], 3.0, None, ALU.mult))
        net.dve(v.tensor_tensor(at[:, :, :], at[:, :, :], by_node(mx, 3), ALU.mult))
        for i in range(3):
            net.dve(v.tensor_tensor(tmp[:, :, :], own[:, :, i * D:(i + 1) * D],
                                    at[:, :, i:i + 1].to_broadcast([P, NB, D]), ALU.mult))
            net.dve(v.tensor_tensor(net.x[:, :, :], net.x[:, :, :], tmp[:, :, :], ALU.add))
        net.after(nc.sync, net.dve)
        net.load(node_view(net.out), net.x[:, :, :])


def build(nc, a, out):
    net = Net(nc, a)
    net.out = out
    dram = lambda name, shape: nc.dram_tensor(name, shape, F32).ap()
    net.lo_d = dram("lo_d", [EP + G * P])
    net.h0_d, h1_d = dram("h0_d", [NPAD, D]), dram("h1_d", [NPAD, D])
    net.rows_d = dram("rows_d", [EP + G * P, ROW])
    rel_d = [dram(f"rel{i}_d", [NPAD, RELS * D]) for i in range(2)]
    ch_d = dram("ch_d", [NPAD, 2 * D])
    net.spare_d = dram("spare_d", [2, P, 1])
    v = nc.vector
    with Mem(nc, "all", "right") as m:
        make_constants(net, m)
        with Mem(nc, "prep") as t:
            net.x = t.sb("x", [P, NB, D])
            net.load(net.x[:, :, :], node_view(a["x"]))
            net.after(v, net.sp)
            layer_norm(net, t, net.h0_d)
        with Mem(nc, "edge") as e:
            index_lists(net, e)
            count_dst_blocks(net, e)
            item_tables(net, m)
            histogram_src(net, e)
            b128, tiles = item_list(net, e, "its", net.start_src, SPAN, WKS)
            both = e.sb("both", [P, 2, WKS], I32)
            net.dve(v.tensor_copy(both[:, 0, :], b128[:, :]))
            net.dve(v.tensor_scalar(both[:, 1, :], tiles[:, :], float(SPAN * P * ROW), None,
                                    ALU.mult))
            net.row_bsrc = to_rows(net, m, "row_bsrc", both[:, 0, :], I32, False)
            net.row_tsrc = to_rows(net, m, "row_tsrc", both[:, 1, :], I32, False)
            net.bsrc = to_rows(net, m, "bsrc", b128[:, :], F32, True)
            nc.all_engine_barrier()
            edge_pass(net, e)
        edge_softmax(net)
        with Mem(nc, "net") as t:
            net.x = t.sb("x", [P, NB, D])
            acc = t.sb("acc", [P, NB * P])
            bias = t.sb("bias", [P, D])
            net.norm, net.rdeg = t.sb("norm", [P, NB]), t.sb("rdeg", [P, NB])
            net.load(net.x[:, :, :], node_view(a["x"]))
            net.load(bias[:, :], a["bias"].partition_broadcast(P))
            net.after(v, net.sp)
            attention_sum(net, acc)
            net.dve(v.scalar_tensor_tensor(net.x[:, :, :], by_block(acc)[:, :, 0:D], 1.0 / HEADS,
                                           net.x[:, :, :], ALU.mult, ALU.add))
            net.dve(v.tensor_tensor(net.x[:, :, :], net.x[:, :, :],
                                    bias[:, None, :].to_broadcast([P, NB, D]), ALU.add))
            with Mem(nc, "l1") as n:
                layer_norm(net, n, h1_d)
            gather_sum(net, "l1s", h1_d, net.gsrc, acc, D, ones=True)
            net.dve(v.tensor_tensor(net.x[:, :, :], net.x[:, :, :], by_block(acc)[:, :, 0:D], ALU.add))
            net.dve(v.tensor_scalar(net.norm[:, :], by_block(acc)[:, :, D], 1.0, None, ALU.max))
            net.dve(v.reciprocal(net.rdeg[:, :], net.norm[:, :]))
            net.after(nc.scalar, net.dve)
            net.act(nc.scalar.activation(net.norm[:, :], net.norm[:, :], ACT.Sqrt))
            net.after(v, net.act)
            net.dve(v.reciprocal(net.norm[:, :], net.norm[:, :]))
            with Mem(nc, "l2") as n:
                h = layer_norm(net, n, None)
                for i in range(2):
                    relation_table(net, f"l2t{i}", h, a[f"W{i + 1}"], rel_d[i])
                    relation_layer(net, f"l2s{i}", rel_d[i], acc, h)
                net.dve(v.tensor_tensor(net.x[:, :, :], net.x[:, :, :], h[:, :, :], ALU.add))
            own = t.sb("own", [P, NB, 3 * D])
            with Mem(nc, "l3") as n:
                channel_tables(net, layer_norm(net, n, None), own, ch_d)
            gather_sum(net, "l3s", ch_d, net.gsrc, acc, 2 * D)
            channel_mix(net, acc, own)


def pad_to(a, n, fill=0):
    out = np.full((n,) + a.shape[1:], fill, a.dtype)
    out[:a.shape[0]] = a
    return out


def kernel(**inputs):
    from concourse.bass_utils import run_bass_kernel_spmd

    i = {k: np.asarray(v) for k, v in inputs.items()}
    arrays = {
        "x": pad_to(i["x"], NPAD), "src": pad_to(i["src"], EP + G * P, PAD_NODE), "dst": pad_to(i["dst"], EP, PAD_NODE),
        "rel": pad_to(i["edge_type_24"], EP),
        "edge_t": np.ascontiguousarray(pad_to(i["edge_attr_64"], EP + G * P).T),
        "W": i["L0_gnn_W"], "att": i["L0_gnn_att"][0], "bias": i["L0_gnn_bias"],
        "gamma": i["L0_gnn_bn_gamma"], "beta": i["L0_gnn_bn_beta"],
        "W1": i["L2_gnn_W1"], "W2": i["L2_gnn_W2"], "W_att": i["L3_gnn_W_att"],
    }
    for name in ("self", "self_high", "id", "neigh", "neigh_high"):
        arrays["Wt_" + name] = np.ascontiguousarray(i["L3_gnn_W_" + name].T)
        arrays["b_" + name] = i["L3_gnn_b_" + name]
    for name in ("low", "high", "mlp"):
        arrays["att_" + name] = i["L3_gnn_w_att_" + name][0]
    nc = bass.Bass("TRN2", target_bir_lowering=False, num_devices=1)
    args = {k: nc.dram_tensor(f"in_{k}", v.shape, mybir.dt.from_np(v.dtype), kind="ExternalInput").ap()
            for k, v in arrays.items()}
    out = nc.dram_tensor("out", (NPAD, D), F32, kind="ExternalOutput").ap()
    build(nc, args, out)
    res = run_bass_kernel_spmd(nc, [{f"in_{k}": v for k, v in arrays.items()}], core_ids=[0]).results[0]
    return res["out"][:N]
```

```python
from contextlib import ExitStack

import numpy as np

import concourse.bass as bass
from concourse import mybir
from concourse.alu_op_type import AluOpType as ALU

F32, BF16, I32, U32 = mybir.dt.float32, mybir.dt.bfloat16, mybir.dt.int32, mybir.dt.uint32
ACT = mybir.ActivationFunctionType
AX = mybir.AxisListType

N, E, D, HEADS, RELS = 6250, 200000, 64, 4, 24
P = 128
NB = 50
NBU = 49
G = 8
T = -(-E // (2 * G * P)) * 2 * G
EP = T * P
PAD_NODE = NBU * P - 1
W = -(-(T + NBU - 1) // (2 * G)) * 2 * G
SPAN = 4
GS = G // SPAN
WS = -(-(T // SPAN + NBU - 1) // (4 * GS)) * 4 * GS
WK = -(-(W + G) // P)
WKS = -(-(WS + 2 * GS) // P)
TC = 112
KC = T // TC
NPAD = NB * P
OUTJ, ROW = HEADS * D, 264
EPS = 1e-5

assert KC * TC == T and TC <= P


class Count:

    def __init__(self, nc, name):
        self.sem = nc.alloc_semaphore(name)
        self.base, self.off, self.loop, self.per = 0, 0, None, 0

    def up(self, ins, n=1):
        ins.then_inc(self.sem, n)
        self.off += n
        return ins

    def credit(self, eng, n):
        eng.sem_inc(self.sem, n)
        self.base += n


class Temporaries:

    def __init__(self, nc, *engines):
        self.nc, self.engines = nc, engines

    def __enter__(self):
        self.first = self.nc.next_id()

    def __exit__(self, *a):
        if a[0] is None:
            for eng in self.engines:
                for n in range(self.first, self.nc.next_id()):
                    self.free(f"{eng.engine.value}_tmp_{n}", eng.engine)

    def free(self, name, engine):
        try:
            known = self.nc.lookup_reg(name)
        except (KeyError, ValueError, AssertionError):
            return
        if known is not None and known.allocated:
            self.nc.free_register(bass.RegisterHandle(name=name, engine=engine))


def wait(eng, count, back=0):
    v = count.base + count.off - back
    if count.loop is None:
        eng.wait_ge(count.sem, v)
    else:
        count.loop.wait(eng, count, v)


class Loop:

    SCRATCH, made = 4, 0

    def __init__(self, nc, trips, per):
        self.nc, self.trips, self.per = nc, trips, per
        self.share, self.scratch, self.met, self.turn = {}, {}, {}, 0

    def new(self, eng):
        Loop.made += 1
        return eng.alloc_register(f"loop_r{Loop.made}")

    def wait(self, eng, count, v):
        if self.met.get((eng.engine, count), -1) >= v:
            return
        self.met[(eng.engine, count)] = v
        if (eng.engine, count.per) not in self.share:
            r = self.share[(eng.engine, count.per)] = self.new(eng)
            eng.reg_mul(r, self.it, count.per)
        if eng.engine not in self.scratch:
            self.scratch[eng.engine] = (eng, [self.new(eng) for _ in range(self.SCRATCH)])
        self.turn += 1
        r = self.scratch[eng.engine][1][self.turn % self.SCRATCH]
        eng.reg_add(r, self.share[(eng.engine, count.per)], v)
        eng.wait_ge(count.sem, r)

    def __enter__(self):
        self.fori = self.nc.Fori(0, self.trips)
        self.it = self.fori.__enter__()
        nc = self.nc
        self.temporaries = Temporaries(nc, nc.vector, nc.scalar, nc.tensor, nc.gpsimd, nc.sync)
        self.temporaries.__enter__()
        for c, n in self.per.items():
            c.base, c.off, c.loop, c.per = c.base + c.off, 0, self, n
        return self.it

    def __exit__(self, *a):
        r = self.fori.__exit__(*a)
        if a[0] is None:
            for c, n in self.per.items():
                assert c.off == n, (str(c.sem), c.off, n)
                c.base, c.off, c.loop = c.base + n * self.trips, 0, None
            for reg in [*self.share.values(), *(r for _, rs in self.scratch.values() for r in rs)]:
                self.nc.free_register(reg)
            self.temporaries.__exit__(None, None, None)
            for reg in self.it.val.handles:
                self.nc.free_register(reg)
        return r


class Chain:

    def __init__(self, nc, eng, name):
        self.eng, self.count = eng, Count(nc, name)

    def __call__(self, ins, n=1):
        self.count.up(ins, n)
        wait(self.eng, self.count)


class Mem:

    def __init__(self, nc, tag, side="left"):
        self.nc, self.tag, self.side, self.ctx = nc, tag, side, ExitStack()

    def __enter__(self):
        self.ctx.__enter__()
        return self

    def __exit__(self, *a):
        if a[0] is None:
            self.nc.all_engine_barrier()
        return self.ctx.__exit__(*a)

    def sb(self, name, shape, dt=F32):
        return self.ctx.enter_context(self.nc.sbuf_tensor(f"{self.tag}_{name}", shape, dt, side=self.side))

    def ps(self, name, shape, dt=F32):
        return self.ctx.enter_context(self.nc.psum_tensor(f"{self.tag}_{name}", shape, dt))


class Net:

    def __init__(self, nc, args):
        self.nc, self.a = nc, args
        self.dve = Chain(nc, nc.vector, "dve_chain")
        self.act = Chain(nc, nc.scalar, "act_chain")
        self.pe = Chain(nc, nc.tensor, "pe_chain")
        self.pool = Chain(nc, nc.gpsimd, "pool_chain")
        self.sp = Chain(nc, nc.sync, "sp_chain")
        self.dma = Chain(nc, nc.gpsimd, "indirect_chain")

    def load(self, out, in_):
        with self.nc.allow_non_contiguous_dma("index lists and transposed vectors, once"):
            self.sp(self.nc.sync.dma_start(out, in_), 16)

    def after(self, eng, *chains):
        for c in chains:
            wait(eng, c.count)


def make_constants(net, m):
    nc = net.nc
    net.iota_i = m.sb("iota_i", [P, P], I32)
    net.iota = m.sb("iota", [P, P])
    net.iota_b = m.sb("iota_b", [P, P], BF16)
    net.part = m.sb("part", [P, 1])
    net.ident = m.sb("ident", [P, P])
    net.ones = m.sb("ones", [P, P])
    part_i = m.sb("part_i", [P, 1], I32)
    net.pool(nc.gpsimd.iota(net.iota_i[:, :], [[1, P]], base=0, channel_multiplier=0))
    net.pool(nc.gpsimd.iota(part_i[:, :], [[1, 1]], base=0, channel_multiplier=1))
    net.after(nc.vector, net.pool)
    net.dve(nc.vector.memset(net.ones[:, :], 1.0))
    net.dve(nc.vector.tensor_copy(net.iota[:, :], net.iota_i[:, :]))
    net.dve(nc.vector.tensor_copy(net.iota_b[:, :], net.iota_i[:, :]))
    net.dve(nc.vector.tensor_copy(net.part[:, :], part_i[:, :]))
    net.dve(nc.vector.tensor_scalar(net.ident[:, :], net.iota[:, :], net.part[:, 0:1], None, ALU.is_equal))


def index_lists(net, m, e):
    nc, a = net.nc, net.a
    net.src_f = e.sb("src_f", [P, T + G])
    net.src_u = e.sb("src_u", [P, T + G], U32)
    net.dst_u = m.sb("dst_u", [P, T + G], U32)
    net.lo_b = e.sb("lo_b", [P, T + G], BF16)
    net.hi_b = e.sb("hi_b", [P, T + G], BF16)
    with Mem(nc, "il") as t:
        raw = t.sb("raw", [TC, KC, P], I32)
        low = t.sb("low", [TC, KC, P], I32)
        flt = t.sb("flt", [TC, KC, P])
        digit = t.sb("digit", [P, T + G], I32)
        tp = t.ps("tp", [P, 4, P])
        for name, u in (("src", net.src_u), ("dst", net.dst_u)):
            net.after(nc.sync, net.dve)
            net.load(raw[:, :, :], a[name][0:EP].rearrange("(k p e) -> p k e", p=TC, e=P))
            net.after(nc.vector, net.sp)
            if name == "src":
                net.dve(nc.vector.tensor_scalar(low[:, :, :], raw[:, :, :], P - 1, None, ALU.bitwise_and))
                net.dve(nc.vector.tensor_copy(flt[:, :, :], low[:, :, :]))
                net.after(nc.sync, net.dve)
                net.load(net.lo_d[0:EP].rearrange("(k p e) -> p k e", p=TC, e=P), flt[:, :, :])
                net.load(net.lo_d[EP:EP + G * P].rearrange("(g e) -> g e", e=P), flt[0:G, 0, :])
                net.after(nc.vector, net.sp)
            net.dve(nc.vector.tensor_copy(flt[:, :, :], raw[:, :, :]))
            for k0 in range(0, KC, 4):
                n = min(4, KC - k0)
                net.after(nc.tensor, net.dve)
                for k in range(n):
                    net.pe(nc.tensor.transpose(tp[:, k, 0:TC], flt[:, k0 + k, :], net.ident[0:TC, 0:TC]))
                net.after(nc.vector, net.pe)
                net.dve(nc.vector.tensor_copy(
                    u[:, k0 * TC:(k0 + n) * TC].rearrange("p (k c) -> p k c", k=n), tp[:, 0:n, 0:TC]))
            net.dve(nc.vector.memset(u[:, T:T + G], 0))
        net.dve(nc.vector.tensor_copy(net.src_f[:, :], net.src_u[:, :]))
        for shift, out in ((False, net.lo_b), (True, net.hi_b)):
            op, val = (ALU.logical_shift_right, 7) if shift else (ALU.bitwise_and, P - 1)
            net.dve(nc.vector.tensor_scalar(digit[:, :], net.src_u[:, :].bitcast(I32), val, None, op))
            net.dve(nc.vector.tensor_copy(out[:, :], digit[:, :]))


def count_dst_blocks(net, t):
    nc = net.nc
    net.start_dst = t.sb("start_dst", [P, NB])
    digit = t.sb("count_digit", [P, T], I32)
    block = t.sb("count_block", [P, T], BF16)
    hit = t.sb("count_hit", [P, T], BF16)
    cnt = t.sb("count_cnt", [P, NB])
    tot = t.ps("count_tot", [P, NB])
    net.dve(nc.vector.tensor_scalar(digit[:, :], net.dst_u[:, 0:T].bitcast(I32), 7, None,
                                    ALU.logical_shift_right))
    net.dve(nc.vector.tensor_copy(block[:, :], digit[:, :]))
    for b in range(NB):
        net.dve(nc.vector.tensor_scalar(hit[:, :], block[:, :], float(b), 0.0, ALU.is_lt, ALU.add,
                                        accum_out=cnt[:, b:b + 1]))
    net.after(nc.tensor, net.dve)
    net.pe(nc.tensor.matmul(tot[:, :], net.ones[:, :], cnt[:, :], start=True, stop=True))
    net.after(nc.vector, net.pe)
    net.dve(nc.vector.tensor_copy(net.start_dst[:, :], tot[:, :]))


def histogram_src(net, m):
    nc = net.nc
    net.start_src = m.sb("start_src", [P, NB])
    net.first = m.sb("first", [P, NBU])
    GH = 16
    with Mem(nc, "hi") as t:
        oh_lo = [t.sb(f"oh_lo{q}", [P, GH, P], BF16) for q in range(2)]
        oh_hi = [t.sb(f"oh_hi{q}", [P, GH, NBU], BF16) for q in range(2)]
        diff = [t.sb(f"diff{q}", [P, GH, NBU], BF16) for q in range(2)]
        zero = t.sb("zero", [P, P], BF16)
        lower = t.sb("lower", [P, P])
        counts = t.sb("counts", [P, NBU])
        hist = t.ps("hist", [P, NBU])
        ex = t.ps("ex", [P, NBU])
        tot = t.ps("tot", [P, NBU])
        made_lo, made_hi, used = Count(nc, "hist_lo"), Count(nc, "hist_hi"), Count(nc, "hist_summed")
        far, absd = Count(nc, "hist_far"), Count(nc, "hist_abs")
        net.dve(nc.vector.memset(zero[:, :], 0.0))
        net.dve(nc.vector.tensor_scalar(lower[:, :], net.iota[:, :], net.part[:, 0:1], None, ALU.is_gt))
        net.after(nc.tensor, net.dve)
        net.pe(nc.tensor.matmul(hist[:, :], zero[:, :], zero[:, 0:NBU], start=True, stop=False,
                                skip_group_check=True))
        used.credit(nc.tensor, 2)
        net.after(nc.gpsimd, net.dve)
        with Loop(nc, T // (2 * GH), {made_lo: 2, made_hi: 2, far: 2, absd: 2, used: 2}) as it:
            for q in range(2):
                c0 = (it * 2 + q) * GH
                wait(nc.vector, used, back=1)
                made_lo.up(nc.vector.tensor_tensor(
                    oh_lo[q][:, :, :], net.iota_b[:, None, :].to_broadcast([P, GH, P]),
                    net.lo_b[:, bass.ds(c0, GH)].unsqueeze(2).to_broadcast([P, GH, P]), ALU.is_equal))
                wait(nc.gpsimd, used, back=1)
                far.up(nc.gpsimd.tensor_tensor(
                    diff[q][:, :, :], net.iota_b[:, None, 0:NBU].to_broadcast([P, GH, NBU]),
                    net.hi_b[:, bass.ds(c0, GH)].unsqueeze(2).to_broadcast([P, GH, NBU]), ALU.subtract))
                wait(nc.scalar, far)
                absd.up(nc.scalar.activation(diff[q][:, :, :], diff[q][:, :, :], ACT.Abs))
                wait(nc.scalar, absd)
                made_hi.up(nc.scalar.activation(oh_hi[q][:, :, :], diff[q][:, :, :], ACT.Relu, bias=1.0,
                                                scale=-1.0))
                wait(nc.tensor, made_lo)
                wait(nc.tensor, made_hi)
                for j in range(GH):
                    ins = nc.tensor.matmul(hist[:, :], oh_lo[q][:, j, :], oh_hi[q][:, j, :], start=False,
                                           stop=False, skip_group_check=True)
                used.up(ins)
        wait(nc.vector, used)
        net.dve(nc.vector.tensor_copy(counts[:, :], hist[:, :]))
        net.after(nc.tensor, net.dve)
        net.pe(nc.tensor.matmul(tot[:, :], net.ones[:, :], counts[:, :], start=True, stop=True))
        net.pe(nc.tensor.matmul(ex[:, :], lower[:, :], counts[:, :], start=True, stop=True))
        net.after(nc.vector, net.pe)
        net.dve(nc.vector.tensor_copy(counts[:, :], tot[:, :]))
        net.dve(nc.vector.memset(net.start_src[:, 0:1], 0.0))
        net.dve(nc.vector.tensor_tensor_scan(net.start_src[:, 1:NB], net.ones[:, 0:NBU], counts[:, :], 0.0,
                                             ALU.mult, ALU.add))
        net.dve(nc.vector.tensor_tensor(net.first[:, :], ex[:, :], net.start_src[:, 0:NBU], ALU.add))


def item_list(net, t, start, span, wk):
    nc = net.nc
    base128 = t.sb("item_b128", [P, wk])
    tile_u = t.sb("item_tile", [P, wk], U32)
    size = span * P
    shift = size.bit_length() - 1
    si = t.sb("item_si", [P, NB], I32)
    fl = t.sb("item_fl", [P, NB])
    ce = t.sb("item_ce", [P, NB])
    n = t.sb("item_n", [P, NBU])
    c = t.sb("item_c", [P, NBU])
    g = t.sb("item_g", [P, NBU])
    dg = t.sb("item_dg", [P, NBU])
    s1 = t.sb("item_s1", [P, NBU])
    w_i = t.sb("item_w_i", [P, wk], I32)
    w = t.sb("item_w", [P, wk])
    bt = t.sb("item_bt", [P, wk, 2])
    v = nc.vector
    net.pool(nc.gpsimd.iota(w_i[:, :], [[P, wk]], base=0, channel_multiplier=1))
    net.after(v, net.pool)
    net.dve(v.tensor_copy(w[:, :], w_i[:, :]))
    net.dve(v.tensor_copy(si[:, :], start[:, :]))
    net.dve(v.tensor_scalar(si[:, :], si[:, :], shift, None, ALU.logical_shift_right))
    net.dve(v.tensor_copy(fl[:, :], si[:, :]))
    net.dve(v.tensor_scalar(ce[:, :], start[:, :], float(size - 1), None, ALU.add))
    net.dve(v.tensor_copy(si[:, :], ce[:, :]))
    net.dve(v.tensor_scalar(si[:, :], si[:, :], shift, None, ALU.logical_shift_right))
    net.dve(v.tensor_copy(ce[:, :], si[:, :]))
    net.dve(v.tensor_tensor(n[:, :], ce[:, 1:NB], fl[:, 0:NBU], ALU.subtract))
    net.dve(v.tensor_scalar(n[:, :], n[:, :], 1.0, None, ALU.max))
    net.dve(v.tensor_scalar(fl[:, :], fl[:, :], float(T // span - 1), None, ALU.min))
    net.dve(v.tensor_tensor_scan(c[:, :], net.ones[:, 0:NBU], n[:, :], 0.0, ALU.mult, ALU.add))
    net.dve(v.tensor_tensor(g[:, :], fl[:, 0:NBU], c[:, :], ALU.subtract))
    net.dve(v.tensor_tensor(g[:, :], g[:, :], n[:, :], ALU.add))
    net.dve(v.memset(dg[:, :], 0.0))
    net.dve(v.tensor_tensor(dg[:, 0:NBU - 1], g[:, 1:NBU], g[:, 0:NBU - 1], ALU.subtract))
    for k in range(wk):
        net.dve(v.scalar_tensor_tensor(s1[:, :], c[:, :], w[:, k:k + 1], net.ones[:, 0:NBU], ALU.is_le,
                                       ALU.mult, accum_out=bt[:, k, 0:1]))
        net.dve(v.scalar_tensor_tensor(s1[:, :], c[:, :], w[:, k:k + 1], dg[:, :], ALU.is_le,
                                       ALU.mult, accum_out=bt[:, k, 1:2]))
    net.dve(v.tensor_scalar(base128[:, :], bt[:, :, 0], float(P), None, ALU.mult))
    net.dve(v.tensor_tensor(w[:, :], w[:, :], bt[:, :, 1], ALU.add))
    net.dve(v.tensor_scalar(w[:, :], w[:, :], g[:, 0:1], float(T // span - 1), ALU.add, ALU.min))
    net.dve(v.tensor_copy(tile_u[:, :], w[:, :]))
    return base128, tile_u


def to_rows(net, m, tag, cols, dt, broadcast):
    nc = net.nc
    WP = cols.shape[1] * P
    flat = nc.dram_tensor(f"{tag}_flat", [WP], dt).ap()
    row = m.sb(tag, [P if broadcast else 1, WP], dt)
    net.after(nc.sync, net.dve)
    net.load(flat.rearrange("(k p) -> p k", p=P), cols)
    net.load(row[:, :], flat.partition_broadcast(P) if broadcast else flat.rearrange("(a w) -> a w", a=1))
    return row


def gather_items(net, m, t):
    nc, a = net.nc, net.a
    v = nc.vector
    net.item_b128, net.item_tile = item_list(net, t, net.start_dst, 1, WK)
    net.gsrc = m.sb("gsrc", [P, WK * P], U32)
    net.grel = m.sb("grel", [P, WK * P], U32)
    net.dloc = m.sb("dloc", [P, WK * P])
    net.item_raw = [t.sb(f"item_{name}", [P, WK, P], I32) for name in ("src", "dst", "rel")]
    bi = t.sb("bi", [P, WK], I32)
    net.dve(v.tensor_copy(bi[:, :], net.item_b128[:, :]))
    net.row_dst = to_rows(net, m, "row_dst", bi[:, :], I32, False)
    net.after(nc.gpsimd, net.dve)
    for k in range(WK):
        for raw, name in zip(net.item_raw, ("src", "dst", "rel")):
            net.dma.count.up(nc.gpsimd.indirect_dma_start(
                out=raw[:, k, :], out_offset=None, in_=a[name].rearrange("(t e) -> t e", e=P),
                in_offset=bass.IndirectOffsetOnAxis(ap=net.item_tile[:, k:k + 1], axis=0)), 16)


def item_tables(net, t):
    nc = net.nc
    v = nc.vector
    src, other = t.sb("item_src_f", [P, WK, P]), t.sb("item_other_f", [P, WK, P])
    tp = t.ps("item_tp", [P, 4, P])

    def turned(values, out):
        for k0 in range(0, WK, 4):
            n = min(4, WK - k0)
            net.after(nc.tensor, net.dve)
            for k in range(n):
                net.pe(nc.tensor.transpose(tp[:, k, :], values[:, k0 + k, :], net.ident[:, :]))
            net.after(v, net.pe)
            net.dve(v.tensor_copy(out[:, k0 * P:(k0 + n) * P], tp[:, 0:n, :].rearrange("p k e -> p (k e)")))

    raw_src, raw_dst, raw_rel = net.item_raw
    net.after(v, net.dma)
    net.dve(v.tensor_copy(src[:, :, :], raw_src[:, :, :]))
    turned(src, net.gsrc)
    net.dve(v.tensor_copy(other[:, :, :], raw_dst[:, :, :]))
    net.dve(v.tensor_tensor(other[:, :, :], other[:, :, :],
                            net.item_b128[:, :].unsqueeze(2).to_broadcast([P, WK, P]), ALU.subtract))
    turned(other, net.dloc)
    net.dve(v.tensor_copy(other[:, :, :], raw_rel[:, :, :]))
    net.dve(v.scalar_tensor_tensor(other[:, :, :], src[:, :, :], float(RELS), other[:, :, :], ALU.mult,
                                   ALU.add))
    turned(other, net.grel)


def node_view(ap):
    return ap.rearrange("(b p) d -> p b d", p=P)


def layer_norm(net, m, dest):
    nc, v, x = net.nc, net.nc.vector, net.x
    blocks = m.sb("h", [P, NB + 1, D])
    h = blocks[:, 0:NB, :]
    net.dve(v.memset(blocks[:, NB:NB + 1, :], 0.0))
    sq = m.sb("sq", [P, NB, D])
    mean = m.sb("mean", [P, NB])
    var = m.sb("var", [P, NB])
    bc = lambda s: s[:, :].unsqueeze(2).to_broadcast([P, NB, D])
    net.dve(v.tensor_reduce(mean[:, :], x[:, :, :], AX.X, ALU.add))
    net.dve(v.tensor_scalar(mean[:, :], mean[:, :], 1.0 / D, None, ALU.mult))
    net.dve(v.tensor_tensor(h[:, :, :], x[:, :, :], bc(mean), ALU.subtract))
    net.dve(v.tensor_tensor(sq[:, :, :], h[:, :, :], h[:, :, :], ALU.mult))
    net.dve(v.tensor_reduce(var[:, :], sq[:, :, :], AX.X, ALU.add))
    net.dve(v.tensor_scalar(var[:, :], var[:, :], 1.0 / D, EPS, ALU.mult, ALU.add))
    net.after(nc.scalar, net.dve)
    net.act(nc.scalar.activation(var[:, :], var[:, :], ACT.Sqrt))
    net.after(v, net.act)
    net.dve(v.reciprocal(var[:, :], var[:, :]))
    net.dve(v.tensor_tensor(h[:, :, :], h[:, :, :], bc(var), ALU.mult))
    net.dve(v.tensor_scalar(h[:, :, :], h[:, :, :], 0.0, None, ALU.max))
    if dest is not None:
        net.after(nc.sync, net.dve)
        net.load(node_view(dest), h[:, :, :])
    return blocks


def edge_pass(net, e):
    nc, a = net.nc, net.a
    v, s, pe, pool, sp = nc.vector, nc.scalar, nc.tensor, nc.gpsimd, nc.sync
    GP = G * P
    two = range(2)
    w_i = e.sb("w_i", [P, OUTJ])
    w_j = e.sb("w_j", [P, OUTJ])
    att = e.sb("att", [P, 2 * OUTJ])
    before = e.sb("before", [P, P])
    gath = [e.sb(f"gath{q}", [P, G, P]) for q in two]
    in_i = [e.sb(f"in_i{q}", [P, GP]) for q in two]
    in_j = [e.sb(f"in_j{q}", [P, GP]) for q in two]
    srow = [e.sb(f"srow{q}", [P, GP], I32) for q in two]
    lrow = [e.sb(f"lrow{q}", [P, GP]) for q in two]
    oh_lo = [e.sb(f"oh_lo{q}", [P, G, P], BF16) for q in two]
    oh_hi = [e.sb(f"oh_hi{q}", [P, G, NBU], BF16) for q in two]
    oh_loT = [e.sb(f"oh_loT{q}", [P, GP]) for q in two]
    idx_s = [e.sb(f"idx_s{q}", [P, G], U32) for q in two]
    idx_d = [e.sb(f"idx_d{q}", [P, G], U32) for q in two]
    rows = [e.sb(f"rows{q}", [P, G, OUTJ + ROW]) for q in two]
    soft = [e.sb(f"soft{q}", [P, 2 * 2 * OUTJ]) for q in two]
    prod = [e.sb(f"prod{q}", [P, 2 * 2 * OUTJ]) for q in two]
    dots = [e.sb(f"dots{q}", [P, G, 2 * HEADS]) for q in two]
    upto = [e.sb(f"upto{q}", [P, NBU]) for q in two]
    junk_r = e.sb("junk_r", [P, G, P], BF16)
    pick = e.sb("pick", [P, G, NBU])
    rank = [e.sb(f"rank{q}", [P, G]) for q in two]
    base = [e.sb(f"base{q}", [P, G]) for q in two]
    src_g = [e.sb(f"src_g{q}", [P, G]) for q in two]
    place = [e.sb(f"place{q}", [P, G], U32) for q in two]
    tp = e.ps("tp", [P, 4, P])
    z = [e.ps(f"z{q}", [P, 2, 2 * OUTJ]) for q in two]
    at = [e.ps(f"at{q}", [P, G, D]) for q in two]
    nxt = e.ps("nxt", [P, NBU])

    net.load(w_i[:, :], a["W"])
    net.load(w_j[0:D, :], a["W"][D:2 * D, :])
    net.load(w_j[D:2 * D, :], a["W"][0:D, :])
    for half in two:
        net.load(att[:, half * OUTJ:(half + 1) * OUTJ].rearrange("p (h d) -> p h d", h=HEADS),
                 a["att"][:, half * D:(half + 1) * D].partition_broadcast(P))
    net.dve(v.tensor_scalar(before[:, :], net.iota[:, :], net.part[:, 0:1], None, ALU.is_lt))
    net.dve(v.memset(rows[1][:, :, :], 0.0))
    net.dve(v.memset(rows[0][:, :, OUTJ + ROW - 3:OUTJ + ROW], 0.0))
    spare_i = place[1][:, :].bitcast(I32)
    net.pool(pool.iota(spare_i, [[P, G]], base=EP, channel_multiplier=1))
    net.after(pe, net.dve, net.sp)
    net.after(v, net.sp)
    net.pe(pe.matmul(nxt[:, :], net.ident[:, :], net.first[:, :], start=True, stop=False, skip_group_check=True))

    c = lambda name: Count(nc, "edge_" + name)
    indexed, gathered = c("indexed"), [c(f"gathered{q}") for q in two]
    loaded_e, loaded_s = [c(f"loaded_e{q}") for q in two], [c(f"loaded_s{q}") for q in two]
    turned, copied = c("turned"), c("copied")
    z_done = c("z_done")
    abs_done, exp_done, ln_done = c("abs_done"), c("exp_done"), c("ln_done")
    soft_done, prod_done, dot_done = c("soft_done"), c("prod_done"), c("dot_done")
    picked = c("picked")
    onehots, ranked, saved, moved, based = c("onehots"), c("ranked"), c("saved"), c("moved"), c("based")
    rows_done = c("rows_done")
    scattered = [c(f"scattered{q}") for q in two]

    def load_group(c0, q):
        e0 = c0 * P
        wait(sp, z_done, back=1)
        loaded_e[q].up(sp.dma_start(in_i[q][D:2 * D, :], a["edge_t"][:, bass.ds(e0, GP)]), 16)
        loaded_e[q].up(sp.dma_start(in_j[q][0:D, :], a["edge_t"][:, bass.ds(e0, GP)]), 16)
        wait(sp, ranked)
        wait(sp, onehots, back=1)
        loaded_s[q].up(sp.dma_start(srow[q][:, :], a["src"][bass.ds(e0, GP)].partition_broadcast(P)), 16)
        loaded_s[q].up(sp.dma_start(lrow[q][:, :], net.lo_d[bass.ds(e0, GP)].partition_broadcast(P)), 16)

    def gather(c0, q):
        wait(s, turned, back=2)
        s.copy(idx_s[q][:, :], net.src_u[:, bass.ds(c0, G)])
        indexed.up(s.copy(idx_d[q][:, :], net.dst_u[:, bass.ds(c0, G)]))
        wait(pool, turned, back=2)
        wait(pool, indexed)
        for j in range(G):
            for half, idx in ((0, idx_s), (1, idx_d)):
                gathered[q].up(pool.indirect_dma_start(
                    out=gath[q][:, j, half * D:(half + 1) * D], out_offset=None, in_=net.h0_d,
                    in_offset=bass.IndirectOffsetOnAxis(ap=idx[q][:, j:j + 1], axis=0)), 16)

    def turn(q):
        wait(pe, gathered[q])
        for half in two:
            wait(pe, copied)
            for j in range(4):
                ins = pe.transpose(tp[:, j, :], gath[q][:, 4 * half + j, :], net.ident[:, :])
            turned.up(ins)
            wait(s, turned)
            cols = bass.ds(half * 4 * P, 4 * P)
            s.copy(in_i[q][0:D, cols], tp[0:D, :, :].rearrange("p j e -> p (j e)"))
            copied.up(s.copy(in_j[q][D:2 * D, cols], tp[D:2 * D, :, :].rearrange("p j e -> p (j e)")))
        wait(pe, loaded_e[q])
        wait(pe, copied)

    def out_of(q, j):
        zj = z[j // 2 % 2][:, j % 2, :]
        pe.matmul(zj[:, 0:OUTJ], in_i[q][:, j * P:(j + 1) * P], w_i[:, :], start=True, stop=True)
        return pe.matmul(zj[:, OUTJ:2 * OUTJ], in_j[q][:, j * P:(j + 1) * P], w_j[:, :], start=True,
                         stop=True)

    def one_hots(c0, q):
        wait(v, loaded_s[q])
        v.tensor_copy(src_g[q][:, :], net.src_f[:, bass.ds(c0, G)])
        v.tensor_tensor(oh_lo[q][:, :, :], net.iota_b[:, None, :].to_broadcast([P, G, P]),
                        net.lo_b[:, bass.ds(c0, G)].unsqueeze(2).to_broadcast([P, G, P]), ALU.is_equal)
        v.tensor_tensor(oh_hi[q][:, :, :], net.iota_b[:, None, 0:NBU].to_broadcast([P, G, NBU]),
                        net.hi_b[:, bass.ds(c0, G)].unsqueeze(2).to_broadcast([P, G, NBU]), ALU.is_equal)
        onehots.up(v.tensor_scalar(oh_loT[q][:, :], lrow[q][:, :], net.part[:, 0:1], None, ALU.is_equal))

    def running(q, j):
        wait(s, moved)
        saved.up(s.copy(upto[j % 2][:, :], nxt[:, :]))
        if j == 0:
            wait(pe, onehots)
            wait(pe, based, back=1)
        wait(pe, saved)
        pe.matmul(at[q][:, j, 0:NBU], oh_loT[q][:, j * P:(j + 1) * P], upto[j % 2][:, :],
                  start=True, stop=True)
        moved.up(pe.matmul(nxt[:, :], oh_lo[q][:, j, :], oh_hi[q][:, j, :], start=False,
                           stop=False, skip_group_check=True))

    def scatter(q):
        wait(pool, rows_done)
        for j in range(G):
            scattered[q].up(pool.indirect_dma_start(
                out=net.rows_d, out_offset=bass.IndirectOffsetOnAxis(ap=place[q][:, j:j + 1], axis=0),
                in_=rows[q][:, j, OUTJ:OUTJ + ROW], in_offset=None), 16)

    for cnt, eng, n in ((turned, pe, 3), (z_done, pe, 2), (copied, s, 1), (soft_done, v, 2),
                        (moved, pe, 1), (onehots, v, 2), (ranked, v, 1), (based, v, 2), (rows_done, v, 1)):
        cnt.credit(eng, n)
    net.after(pool, net.dve)
    scattered[0].up(pool.dma_start(net.spare_d[0], rows[1][:, 0, 0:1]), 16)
    load_group(0, 0)
    gather(0, 0)
    turn(0)
    for j in (0, 1):
        ins = out_of(0, j)
    z_done.up(ins)
    one_hots(0, 0)
    per = {indexed: 2, gathered[0]: 256, gathered[1]: 256, loaded_e[0]: 32, loaded_e[1]: 32,
           loaded_s[0]: 32, loaded_s[1]: 32, turned: 4, copied: 4, z_done: 8,
           abs_done: 8, exp_done: 8, ln_done: 8, soft_done: 8, prod_done: 8, dot_done: 8, onehots: 2,
           ranked: 2 * G, saved: 2 * G, moved: 2 * G, based: 2, picked: 2, rows_done: 2,
           scattered[0]: 128, scattered[1]: 128}
    with Loop(nc, T // (2 * G), per) as it:
        for q in two:
            c0 = (it * 2 + q) * G
            load_group(c0 + G, 1 - q)
            gather(c0 + G, 1 - q)
            scatter(1 - q)
            for k in range(G // 2):
                soft_k = soft[k % 2][:, :]
                running(q, 2 * k)
                wait(s, z_done)
                wait(s, soft_done, back=1)
                abs_done.up(s.activation(soft_k, z[k % 2][:, :, :].rearrange("p t f -> p (t f)"), ACT.Abs))
                if k + 1 < G // 2:
                    wait(pe, soft_done)
                    out_of(q, 2 * k + 2)
                wait(s, abs_done)
                exp_done.up(s.activation(soft_k, soft_k, ACT.Exp, scale=-1.0))
                running(q, 2 * k + 1)
                if k + 1 < G // 2:
                    z_done.up(out_of(q, 2 * k + 3))
                wait(s, exp_done)
                ln_done.up(s.activation(soft_k, soft_k, ACT.Ln, bias=1.0))
                if k + 1 == G // 2:
                    turn(1 - q)
                    wait(pe, soft_done)
                    for j in (0, 1):
                        ins = out_of(1 - q, j)
                    z_done.up(ins)

                if k == 0:
                    wait(v, scattered[q])
                wait(v, ln_done)
                rk = rows[q][:, 2 * k:2 * k + 2, 0:2 * OUTJ]
                soft_done.up(v.scalar_tensor_tensor(rk, z[k % 2][:, :, :], 0.0,
                                                    soft_k.rearrange("p (t f) -> p t f", t=2),
                                                    ALU.max, ALU.add))
                if k == 0:
                    wait(v, onehots)
                for j in (2 * k, 2 * k + 1):
                    ranked.up(v.scalar_tensor_tensor(
                        junk_r[:, j, :], srow[q][:, j * P:(j + 1) * P], src_g[q][:, j:j + 1],
                        before[:, :], ALU.is_equal, ALU.mult, accum_out=rank[q][:, j:j + 1]))
                wait(v, soft_done)
                prod_done.up(v.tensor_tensor(prod[k % 2][:, :].rearrange("p (t f) -> p t f", t=2), rk,
                                             att[:, None, :].to_broadcast([P, 2, 2 * OUTJ]), ALU.mult))
                wait(v, prod_done)
                dot_done.up(v.tensor_reduce(
                    dots[q][:, 2 * k:2 * k + 2, :].rearrange("p t h -> p (t h)"),
                    prod[k % 2][:, :].rearrange("p (g d) -> p g d", d=D), AX.X, ALU.add))
                if k == 2:
                    wait(v, moved, back=6)
                    one_hots(c0 + G, 1 - q)

            wait(v, moved)
            picked.up(v.tensor_tensor(pick[:, :, :], oh_hi[q][:, :, :], at[q][:, :, 0:NBU], ALU.mult))
            wait(v, picked)
            based.up(v.tensor_reduce(base[q][:, :], pick[:, :, :], AX.X, ALU.add))
            wait(v, based)
            wait(v, dot_done)
            v.tensor_copy(rows[q][:, :, 2 * OUTJ + HEADS:2 * OUTJ + HEADS + 1],
                          src_g[q][:, :].unsqueeze(2))
            v.tensor_tensor(place[q][:, :], rank[q][:, :], base[q][:, :], ALU.add)
            rows_done.up(v.tensor_tensor(rows[q][:, :, 2 * OUTJ:2 * OUTJ + HEADS], dots[q][:, :, 0:HEADS],
                                         dots[q][:, :, HEADS:2 * HEADS], ALU.add))
    scatter(1)
    for q in two:
        wait(pool, scattered[q])
        wait(pool, gathered[q])


def softplus(net, out, x, tmp):
    nc = net.nc
    net.after(nc.scalar, net.dve)
    net.act(nc.scalar.activation(tmp, x, ACT.Abs))
    net.act(nc.scalar.activation(tmp, tmp, ACT.Exp, scale=-1.0))
    net.act(nc.scalar.activation(tmp, tmp, ACT.Ln, bias=1.0))
    net.after(nc.vector, net.act)
    net.dve(nc.vector.scalar_tensor_tensor(out, x, 0.0, tmp, ALU.max, ALU.add))


def all_sum(net, out, part, ps):
    nc = net.nc
    net.after(nc.tensor, net.dve)
    net.pe(nc.tensor.matmul(ps, net.ones[:, :], part, start=True, stop=True))
    net.after(nc.vector, net.pe)
    net.dve(nc.vector.tensor_copy(out, ps))


def edge_softmax(net, m):
    nc, a = net.nc, net.a
    v = nc.vector
    view = net.rows_d[0:EP].rearrange("(p c) r -> p c r", c=T)
    with Mem(nc, "sm") as t:
        al = t.sb("al", [P, T, HEADS + 1])
        keep_f = t.sb("keep_f", [P, T])
        keep_b = t.sb("keep_b", [P, T])
        be = t.sb("be", [P, HEADS, T])
        fw = t.sb("fw", [P, HEADS, T])
        tot = t.sb("tot", [P, HEADS, T])
        prv, nxt = t.sb("prv", [P, 1]), t.sb("nxt", [P, 1])
        k_f, k_b = t.sb("k_f", [P, HEADS]), t.sb("k_b", [P, HEADS])
        s1, s2 = t.sb("s1", [P, HEADS]), t.sb("s2", [P, HEADS])
        mu, scale = t.sb("mu", [P, HEADS]), t.sb("scale", [P, HEADS])
        gam, bet = t.sb("gam", [P, HEADS]), t.sb("bet", [P, HEADS])
        line, line_k = t.sb("line", [HEADS, P]), t.sb("line_k", [HEADS, P])
        carry = t.sb("carry", [HEADS, P])
        ps = t.ps("ps", [P, HEADS])
        ps_l = t.ps("ps_l", [HEADS, 2, P])

        net.dve(v.memset(prv[:, :], -1.0))
        net.dve(v.memset(nxt[:, :], -1.0))
        net.after(nc.sync, net.dve)
        net.load(al[:, :, :], view[:, :, OUTJ:OUTJ + HEADS + 1])
        net.load(prv[1:P, :], view[0:P - 1, T - 1, OUTJ + HEADS:OUTJ + HEADS + 1])
        net.load(nxt[0:P - 1, :], view[1:P, 0, OUTJ + HEADS:OUTJ + HEADS + 1])
        net.load(gam[:, :], a["gamma"].partition_broadcast(P))
        net.load(bet[:, :], a["beta"].partition_broadcast(P))
        count_dst_blocks(net, t)
        gather_items(net, m, t)
        item_tables(net, t)
        net.after(v, net.sp)
        src = al[:, :, HEADS]
        net.dve(v.tensor_tensor(keep_f[:, 1:T], src[:, 1:T], src[:, 0:T - 1], ALU.is_equal))
        net.dve(v.tensor_tensor(keep_f[:, 0:1], src[:, 0:1], prv[:, :], ALU.is_equal))
        net.dve(v.tensor_copy(keep_b[:, 0:T - 1], keep_f[:, 1:T]))
        net.dve(v.tensor_tensor(keep_b[:, T - 1:T], src[:, T - 1:T], nxt[:, :], ALU.is_equal))
        for k, keep in ((k_f, keep_f), (k_b, keep_b)):
            net.dve(v.tensor_reduce(prv[:, :], keep[:, :], AX.X, ALU.min))
            net.dve(v.tensor_copy(k[:, :], prv[:, :].to_broadcast([P, HEADS])))

        softplus(net, be[:, :, :], al[:, :, 0:HEADS].rearrange("p c h -> p h c"), fw[:, :, :])
        mask_i, mask = tot[:, 0, :].bitcast(I32), tot[:, 1, :]
        net.after(nc.gpsimd, net.dve)
        net.pool(nc.gpsimd.iota(mask_i, [[1, T]], base=0, channel_multiplier=T))
        net.after(v, net.pool)
        net.dve(v.tensor_copy(mask, mask_i))
        net.dve(v.tensor_scalar(mask, mask, float(E), None, ALU.is_lt))
        mask_h = tot[:, 1:2, :].to_broadcast([P, HEADS, T])
        head = lambda s: s[:, :].unsqueeze(2).to_broadcast([P, HEADS, T])
        net.dve(v.tensor_tensor(fw[:, :, :], be[:, :, :], mask_h, ALU.mult))
        net.dve(v.tensor_reduce(s1[:, :], fw[:, :, :], AX.X, ALU.add))
        all_sum(net, mu[:, :], s1[:, :], ps[:, :])
        net.dve(v.tensor_scalar(mu[:, :], mu[:, :], 1.0 / E, None, ALU.mult))
        net.dve(v.tensor_tensor(be[:, :, :], be[:, :, :], head(mu), ALU.subtract))
        net.dve(v.tensor_tensor(fw[:, :, :], be[:, :, :], mask_h, ALU.mult))
        net.dve(v.tensor_tensor(fw[:, :, :], fw[:, :, :], fw[:, :, :], ALU.mult))
        net.dve(v.tensor_reduce(s1[:, :], fw[:, :, :], AX.X, ALU.add))
        all_sum(net, scale[:, :], s1[:, :], ps[:, :])
        net.dve(v.tensor_scalar(scale[:, :], scale[:, :], 1.0 / E, EPS, ALU.mult, ALU.add))
        net.after(nc.scalar, net.dve)
        net.act(nc.scalar.activation(scale[:, :], scale[:, :], ACT.Sqrt))
        net.after(v, net.act)
        net.dve(v.reciprocal(scale[:, :], scale[:, :]))
        net.dve(v.tensor_tensor(scale[:, :], scale[:, :], gam[:, :], ALU.mult))
        for h in range(HEADS):
            net.dve(v.tensor_scalar(be[:, h, :], be[:, h, :], scale[:, h:h + 1], bet[:, h:h + 1], ALU.mult,
                                    ALU.add))
        softplus(net, be[:, :, :], be[:, :, :], fw[:, :, :])

        def carried(ends, keeps, op, back):
            net.dve(v.tensor_copy(s2[:, :], ends))
            net.after(nc.tensor, net.dve)
            net.pe(nc.tensor.transpose(ps_l[:, 0, :], s2[:, :], net.ident[:, :]))
            net.pe(nc.tensor.transpose(ps_l[:, 1, :], keeps[:, :], net.ident[:, :]))
            net.after(v, net.pe)
            net.dve(v.tensor_copy(line[:, :], ps_l[:, 0, :]))
            net.dve(v.tensor_copy(line_k[:, :], ps_l[:, 1, :]))
            net.dve(v.memset(carry[:, :], 0.0))
            if back:
                net.dve(v.tensor_tensor_scan(carry[:, P - 2::-1], line_k[:, P - 1:0:-1], line[:, P - 1:0:-1],
                                             0.0, ALU.mult, op))
            else:
                net.dve(v.tensor_tensor_scan(carry[:, 1:P], line_k[:, 0:P - 1], line[:, 0:P - 1], 0.0,
                                             ALU.mult, op))
            net.after(nc.tensor, net.dve)
            net.pe(nc.tensor.transpose(ps[:, :], carry[:, :], net.ident[0:HEADS, 0:HEADS]))
            net.after(v, net.pe)
            net.dve(v.tensor_copy(s2[:, :], ps[:, :]))

        def segments(op):
            for first in (True, False):
                for h in range(HEADS):
                    net.dve(v.tensor_tensor_scan(fw[:, h, :], keep_f[:, :], be[:, h, :],
                                                 0.0 if first else s2[:, h:h + 1], ALU.mult, op))
                if first:
                    carried(fw[:, :, T - 1], k_f, op, False)
            for first in (True, False):
                for h in range(HEADS):
                    net.dve(v.tensor_tensor_scan(tot[:, h, ::-1], keep_b[:, ::-1], fw[:, h, ::-1],
                                                 0.0 if first else s2[:, h:h + 1], ALU.mult, ALU.max))
                if first:
                    carried(tot[:, :, 0], k_b, ALU.max, True)

        segments(ALU.max)
        net.dve(v.tensor_tensor(be[:, :, :], be[:, :, :], tot[:, :, :], ALU.subtract))
        net.after(nc.scalar, net.dve)
        net.act(nc.scalar.activation(be[:, :, :], be[:, :, :], ACT.Exp))
        net.after(v, net.act)
        segments(ALU.add)
        net.dve(v.tensor_scalar(tot[:, :, :], tot[:, :, :], 1e-16, None, ALU.add))
        net.dve(v.reciprocal(tot[:, :, :], tot[:, :, :]))
        weights = fw[:, :, :].rearrange("p h c -> p (h c)")
        net.dve(v.tensor_tensor(weights.rearrange("p (c h) -> p h c", h=HEADS), be[:, :, :], tot[:, :, :],
                                ALU.mult))
        net.after(nc.sync, net.dve)
        net.load(net.weight_d.rearrange("(p c) h -> p (c h)", c=T), weights)


def item_values(nc, eng, row, top):
    _, values = nc.values_load_multi_w_load_instructions(
        row[0:1, :], engines=(eng.engine,), min_val=0, max_val=top,
        skip_runtime_bounds_check_because="the item lists are clamped to this range")
    return values


def free_values(nc, values):
    for value in values:
        for reg in value.val.handles:
            nc.free_register(reg)


def add_items(net, acc, added, blk, sums, cols):
    nc, v = net.nc, net.nc.vector
    blocks = item_values(nc, v, blk, NBU * P)
    for j in range(blk.shape[1]):
        wait(v, added)
        with Temporaries(nc, v):
            here = acc[:, bass.ds(blocks[j], cols)]
            added.up(v.tensor_tensor(here, here, sums(j), ALU.add))
    free_values(nc, blocks)


def attention_sum(net, acc):
    nc = net.nc
    v, s, pe, pool, sp = nc.vector, nc.scalar, nc.tensor, nc.gpsimd, nc.sync
    two = range(2)
    row_items = net.rows_d.rearrange("(n t p) r -> n p t r", t=SPAN, p=P)
    weight_items = net.weight_d.rearrange("(n t p) h -> n p t h", t=SPAN, p=P)
    with Mem(nc, "at") as t:
        rows = [t.sb(f"rows{r}", [P, GS, SPAN, ROW]) for r in range(4)]
        wts = [t.sb(f"wts{r}", [P, GS, SPAN, HEADS]) for r in range(4)]
        wtd = [t.sb(f"wtd{q}", [P, G, OUTJ]) for q in two]
        msg = [t.sb(f"msg{q}", [P, G, 2 * D]) for q in two]
        loc = [t.sb(f"loc{q}", [P, G]) for q in two]
        oh = [t.sb(f"oh{q}", [P, G, P]) for q in two]
        blk = [t.sb(f"blk{q}", [1, GS], I32) for q in two]
        til = [t.sb(f"til{r}", [1, GS], I32) for r in range(4)]
        ps = [t.ps(f"ps{q}", [P, GS, P]) for q in two]
        c = lambda name: Count(nc, "att_" + name)
        loaded = [c(f"loaded{r}") for r in range(4)]
        weighted, placed, summed, added, messaged, onehot, listed_t, listed_b = map(
            c, ("weighted", "placed", "summed", "added", "messaged", "onehot", "listed_t", "listed_b"))
        net.dve(v.memset(acc[:, :], 0.0))
        for cnt, eng, n in ((weighted, pool, 3), (messaged, v, 2), (onehot, v, 3), (summed, pe, 2),
                            (added, v, GS + 1)):
            cnt.credit(eng, n)

        def fetch(w0, r):
            wait(s, weighted, back=2)
            listed_t.up(s.copy(til[r][:, :], net.row_tsrc[:, bass.ds(w0, GS)]))
            wait(sp, listed_t)
            wait(sp, weighted, back=2)
            wait(sp, onehot, back=2)
            starts = item_values(nc, sp, til[r], T // SPAN - 1)
            with Temporaries(nc, sp):
                for j in range(GS):
                    for out, items in ((rows, row_items), (wts, weight_items)):
                        item = items[bass.ds(starts[j], 1), :, :, :].rearrange("n p t r -> (n p) t r")
                        loaded[r].up(sp.dma_start(out[r][:, j, :, :], item), 16)
            free_values(nc, starts)

        def prepare(w0, q, r):
            rq = rows[r][:, :, :, :].rearrange("p g t r -> p (g t) r")
            wait(pool, loaded[r])
            wait(pool, messaged, back=1)
            weighted.up(pool.tensor_tensor(
                wtd[q][:, :, :].rearrange("p g (h d) -> p g h d", h=HEADS),
                rq[:, :, 0:OUTJ].rearrange("p g (h d) -> p g h d", h=HEADS),
                wts[r][:, :, :, :].rearrange("p g t h -> p (g t) h").unsqueeze(3)
                .to_broadcast([P, G, HEADS, D]), ALU.mult))
            wait(v, loaded[r])
            wait(v, summed, back=1)
            placed.up(v.tensor_tensor(
                loc[q][:, :].rearrange("p (g t) -> p g t", t=SPAN), rows[r][:, :, :, OUTJ + HEADS],
                net.bsrc[:, bass.ds(w0, GS)].unsqueeze(2).to_broadcast([P, GS, SPAN]), ALU.subtract))
            wait(v, placed)
            onehot.up(v.tensor_tensor(oh[q][:, :, :], net.iota[:, None, :].to_broadcast([P, G, P]),
                                      loc[q][:, :].unsqueeze(2).to_broadcast([P, G, P]), ALU.is_equal))
            wait(v, weighted)
            messaged.up(v.tensor_tensor(msg[q][:, :, :], wtd[q][:, :, 0:2 * D], wtd[q][:, :, 2 * D:4 * D],
                                        ALU.add))

        for r in range(2):
            fetch(r * GS, r)
        prepare(0, 0, 0)
        per = {**{loaded[r]: 32 * GS for r in range(4)}, weighted: 4, placed: 4, summed: 4,
               added: 4 * GS, messaged: 4, onehot: 4, listed_t: 4, listed_b: 4}
        with Loop(nc, WS // (4 * GS), per) as it:
            for r in range(4):
                q = r % 2
                w0 = (it * 4 + r) * GS
                wait(pe, messaged)
                wait(pe, added, back=GS)
                for j in range(GS):
                    for k in range(SPAN):
                        n = j * SPAN + k
                        ins = pe.matmul(ps[q][:, j, :], oh[q][:, n, :], msg[q][:, n, :],
                                        start=k == 0, stop=k == SPAN - 1)
                summed.up(ins)
                fetch(w0 + 2 * GS, (r + 2) % 4)
                prepare(w0 + GS, 1 - q, (r + 1) % 4)
                wait(s, added, back=GS)
                listed_b.up(s.copy(blk[q][:, :], net.row_bsrc[:, bass.ds(w0, GS)]))
                wait(v, listed_b)
                wait(v, summed)
                add_items(net, acc, added, blk[q], lambda j: ps[q][:, j, :], 2 * D)
        wait(sp, loaded[1])
        wait(v, added)
        both = by_block(acc)
        net.dve(v.tensor_tensor(both[:, :, 0:D], both[:, :, 0:D], both[:, :, D:2 * D], ALU.add))


def gather_sum(net, tag, table, index, acc, cols, ones=False):
    nc = net.nc
    v, s, pe, pool = nc.vector, nc.scalar, nc.tensor, nc.gpsimd
    two = range(2)
    wide = cols + (1 if ones else 0)
    with Mem(nc, tag) as t:
        got = [t.sb(f"got{q}", [P, G, wide + wide % 2]) for q in two]
        idx = [t.sb(f"idx{q}", [P, G], U32) for q in two]
        oh = [t.sb(f"oh{q}", [P, G, P]) for q in two]
        blk = [t.sb(f"blk{q}", [1, G], I32) for q in two]
        ps = [t.ps(f"ps{q}", [P, G, P]) for q in two]
        c = lambda name: Count(nc, f"{tag}_{name}")
        gathered = [c(f"gathered{q}") for q in two]
        indexed, onehot, summed, added, listed = map(c, ("indexed", "onehot", "summed", "added", "listed"))
        net.dve(v.memset(acc[:, :], 0.0))
        if ones:
            for q in two:
                net.dve(v.memset(got[q][:, :, cols:wide], 1.0))
            net.after(pe, net.dve)
        for cnt, eng, n in ((summed, pe, 2), (added, v, G + 1)):
            cnt.credit(eng, n)

        def one_hots(w0, q):
            onehot.up(v.tensor_tensor(oh[q][:, :, :], net.iota[:, None, :].to_broadcast([P, G, P]),
                                      net.dloc[:, bass.ds(w0, G)].unsqueeze(2).to_broadcast([P, G, P]),
                                      ALU.is_equal))

        one_hots(0, 0)
        with Loop(nc, W // (2 * G), {gathered[0]: 16 * G, gathered[1]: 16 * G, indexed: 2, onehot: 2,
                                     summed: 2, added: 2 * G, listed: 2}) as it:
            for q in two:
                w0 = (it * 2 + q) * G
                wait(s, summed, back=1)
                indexed.up(s.copy(idx[q][:, :], index[:, bass.ds(w0, G)]))
                wait(s, added, back=G)
                listed.up(s.copy(blk[q][:, :], net.row_dst[:, bass.ds(w0, G)]))
                wait(pool, indexed)
                wait(pool, summed, back=1)
                for j in range(G):
                    gathered[q].up(pool.indirect_dma_start(
                        out=got[q][:, j, 0:cols], out_offset=None, in_=table,
                        in_offset=bass.IndirectOffsetOnAxis(ap=idx[q][:, j:j + 1], axis=0)), 16)
                wait(v, summed)
                wait(pe, onehot)
                one_hots(w0 + G, 1 - q)
                wait(pe, gathered[q])
                wait(pe, added, back=G)
                for j in range(G):
                    ins = pe.matmul(ps[q][:, j, 0:wide], oh[q][:, j, :], got[q][:, j, 0:wide], start=True,
                                    stop=True)
                summed.up(ins)
                wait(v, listed)
                wait(v, summed)
                add_items(net, acc, added, blk[q], lambda j: ps[q][:, j, 0:wide], wide)


def by_block(acc):
    return acc[:, :].rearrange("p (b s) -> p b s", s=P)


def relation_table(net, tag, h, w, table):
    nc = net.nc
    v, s, pe, sp = nc.vector, nc.scalar, nc.tensor, nc.sync
    two = range(2)
    wide = RELS * D
    part = wide // 3
    with Mem(nc, tag) as t:
        ws = t.sb("ws", [D, RELS, D])
        hs = [t.sb(f"hs{q}", [P, D]) for q in two]
        ht = [t.sb(f"ht{q}", [D, P]) for q in two]
        out = [t.sb(f"out{q}", [P, wide]) for q in two]
        tp = t.ps("tp", [D, P])
        ps = [t.ps(f"ps{q}", [P, wide]) for q in two]
        c = lambda name: Count(nc, f"{tag}_{name}")
        taken, turned, copied, done, emptied_s, emptied_v = map(
            c, ("taken", "turned", "copied", "done", "emptied_s", "emptied_v"))
        stored = [c(f"stored{q}") for q in two]
        net.load(ws[:, :, :], w.rearrange("r d f -> d r f"))
        net.after(pe, net.sp, net.dve)
        for cnt, eng, n in ((turned, pe, 2), (done, pe, 3), (emptied_s, s, 2), (emptied_v, v, 2)):
            cnt.credit(eng, n)
        for q in two:
            net.dve(v.memset(out[q][:, 0:1], 0.0))
            net.after(sp, net.dve)
            stored[q].up(sp.dma_start(net.spare_d[q], out[q][:, 0:1]), 16)

        def take(b, q):
            wait(v, turned, back=1)
            taken.up(v.tensor_copy(hs[q][:, :], h[:, bass.ds(b, 1), :].rearrange("p b d -> p (b d)")))

        def turn(q, ahead):
            wait(pe, taken)
            wait(pe, copied)
            turned.up(pe.transpose(tp[:, :], hs[q][:, :], net.ident[:, :]))
            wait(v, turned)
            wait(v, done, back=ahead)
            copied.up(v.tensor_copy(ht[q][:, :], tp[:, :]))

        copied.credit(v, 1)
        take(0, 0)
        turn(0, 1)
        with Loop(nc, NB // 2, {taken: 2, turned: 2, copied: 2, done: 2, emptied_s: 2, emptied_v: 2,
                                stored[0]: 16, stored[1]: 16}) as it:
            for q in two:
                b = it * 2 + q
                take(b + 1, 1 - q)
                wait(pe, copied)
                wait(pe, emptied_s, back=1)
                wait(pe, emptied_v, back=1)
                for k in range(3):
                    ins = pe.matmul(ps[q][:, k * part:(k + 1) * part], ht[q][:, :],
                                    ws[:, :, :].rearrange("d r f -> d (r f)")[:, k * part:(k + 1) * part],
                                    start=True, stop=True)
                    if k == 1:
                        turn(1 - q, 0)
                done.up(ins)
                wait(s, done)
                wait(s, stored[q])
                emptied_s.up(s.copy(out[q][:, 0:2 * part], ps[q][:, 0:2 * part]))
                wait(v, done)
                wait(v, stored[q])
                emptied_v.up(v.tensor_copy(out[q][:, 2 * part:wide], ps[q][:, 2 * part:wide]))
                wait(sp, emptied_s)
                wait(sp, emptied_v)
                stored[q].up(sp.dma_start(
                    table.rearrange("(b p) f -> p b f", p=P)[:, bass.ds(b, 1), :],
                    out[q][:, :].unsqueeze(1)), 16)
        for q in two:
            wait(sp, stored[q])


def relation_layer(net, tag, table, acc, h):
    v = net.nc.vector
    gather_sum(net, tag, table.rearrange("n (r f) -> (n r) f", f=D), net.grel, acc, D)
    net.dve(v.tensor_tensor(h[:, 0:NB, :], by_block(acc)[:, :, 0:D],
                            net.rdeg[:, :].unsqueeze(2).to_broadcast([P, NB, D]), ALU.mult))
    net.dve(v.tensor_scalar(h[:, 0:NB, :], h[:, 0:NB, :], 0.0, None, ALU.max))


def channel_tables(net, h, own, table):
    nc, a = net.nc, net.a
    v, s, pe, sp = nc.vector, nc.scalar, nc.tensor, nc.sync
    two = range(2)
    with Mem(nc, "ch") as t:
        ws = t.sb("ws", [D + 1, 5 * D])
        hs = [t.sb(f"hs{q}", [P, D + 1]) for q in two]
        nb = [t.sb(f"nb{q}", [P, 1]) for q in two]
        ht = [t.sb(f"ht{q}", [D + 1, P]) for q in two]
        out = [t.sb(f"out{q}", [P, 2 * D]) for q in two]
        tp = t.ps("tp", [D + 1, P])
        ps = [t.ps(f"ps{q}", [P, 5 * D]) for q in two]
        c = lambda name: Count(nc, f"ch_{name}")
        taken, turned, copied, done, kept, scaled, normed = map(
            c, ("taken", "turned", "copied", "done", "kept", "scaled", "normed"))
        stored = [c(f"stored{q}") for q in two]
        for i, name in enumerate(("self", "self_high", "id", "neigh", "neigh_high")):
            net.load(ws[0:D, i * D:(i + 1) * D], a["Wt_" + name])
            net.load(ws[D:D + 1, i * D:(i + 1) * D], a["b_" + name].rearrange("(a d) -> a d", a=1))
        for q in two:
            net.dve(v.memset(hs[q][:, D:D + 1], 1.0))
            net.dve(v.memset(out[q][:, 0:1], 0.0))
            net.after(sp, net.dve)
            stored[q].up(sp.dma_start(net.spare_d[q], out[q][:, 0:1]), 16)
        net.after(pe, net.sp, net.dve)
        for cnt, eng, n in ((turned, pe, 2), (done, pe, 3), (kept, s, 2), (scaled, v, 2), (copied, v, 1)):
            cnt.credit(eng, n)

        def take(b, q):
            wait(v, turned, back=1)
            taken.up(v.tensor_copy(hs[q][:, 0:D], h[:, bass.ds(b, 1), :].rearrange("p b d -> p (b d)")))

        def turn(q, ahead):
            wait(pe, taken)
            wait(pe, copied)
            turned.up(pe.transpose(tp[:, :], hs[q][:, :], net.ident[:, :]))
            wait(v, turned)
            wait(v, done, back=ahead)
            copied.up(v.tensor_copy(ht[q][:, :], tp[:, :]))

        take(0, 0)
        turn(0, 1)
        with Loop(nc, NB // 2, {taken: 2, turned: 2, copied: 2, done: 2, kept: 2, scaled: 2, normed: 2,
                                stored[0]: 16, stored[1]: 16}) as it:
            for q in two:
                b = it * 2 + q
                take(b + 1, 1 - q)
                wait(v, scaled, back=1)
                normed.up(v.tensor_copy(nb[q][:, :], net.norm[:, bass.ds(b, 1)]))
                wait(pe, copied)
                wait(pe, kept, back=1)
                wait(pe, scaled, back=1)
                done.up(pe.matmul(ps[q][:, :], ht[q][:, :], ws[:, :], start=True, stop=True))
                turn(1 - q, 1)
                wait(s, done)
                kept.up(s.activation(own[:, bass.ds(b, 1), :].rearrange("p b f -> p (b f)"),
                                     ps[q][:, 0:3 * D], ACT.Relu))
                wait(v, kept)
                wait(v, normed)
                wait(v, stored[q])
                scaled.up(v.tensor_scalar(out[q][:, :], ps[q][:, 3 * D:5 * D], 0.0, nb[q][:, 0:1], ALU.max,
                                          ALU.mult))
                wait(sp, scaled)
                stored[q].up(sp.dma_start(
                    table.rearrange("(b p) f -> p b f", p=P)[:, bass.ds(b, 1), :],
                    out[q][:, :].unsqueeze(1)), 16)
        for q in two:
            wait(sp, stored[q])


def channel_mix(net, acc, own):
    nc, a = net.nc, net.a
    v, s = nc.vector, nc.scalar
    with Mem(nc, "mix") as t:
        wa = t.sb("wa", [P, 3, D])
        w3 = t.sb("w3", [P, 3, 3])
        tmp = t.sb("tmp", [P, NB, D])
        lg = t.sb("lg", [P, NB, 3])
        at = t.sb("at", [P, NB, 3])
        pr = t.sb("pr", [P, NB, 3])
        mx = t.sb("mx", [P, NB])
        for i, name in enumerate(("low", "high", "mlp")):
            net.load(wa[:, i, :], a["att_" + name].partition_broadcast(P))
        net.load(w3[:, :, :], a["W_att"].partition_broadcast(P))
        net.after(v, net.sp)
        by_node = lambda x, n: x[:, :].unsqueeze(2).to_broadcast([P, NB, n])
        for i, op in ((0, ALU.add), (1, ALU.subtract)):
            o = own[:, :, i * D:(i + 1) * D]
            net.dve(v.tensor_tensor(tmp[:, :, :], by_block(acc)[:, :, i * D:(i + 1) * D],
                                    by_node(net.rdeg, D), ALU.mult))
            net.dve(v.tensor_tensor(o, o, tmp[:, :, :], op))
        for i in range(3):
            net.dve(v.tensor_tensor(tmp[:, :, :], own[:, :, i * D:(i + 1) * D],
                                    wa[:, i:i + 1, :].to_broadcast([P, NB, D]), ALU.mult))
            net.dve(v.tensor_reduce(lg[:, :, i], tmp[:, :, :], AX.X, ALU.add))
        net.after(s, net.dve)
        net.act(s.activation(lg[:, :, :], lg[:, :, :], ACT.Sigmoid))
        net.after(v, net.act)
        for j in range(3):
            net.dve(v.tensor_tensor(pr[:, :, :], lg[:, :, :], w3[:, j:j + 1, :].to_broadcast([P, NB, 3]),
                                    ALU.mult))
            net.dve(v.tensor_reduce(at[:, :, j], pr[:, :, :], AX.X, ALU.add))
        net.dve(v.tensor_scalar(at[:, :, :], at[:, :, :], 1.0 / 3.0, None, ALU.mult))
        net.dve(v.tensor_reduce(mx[:, :], at[:, :, :], AX.X, ALU.max))
        net.dve(v.tensor_tensor(at[:, :, :], at[:, :, :], by_node(mx, 3), ALU.subtract))
        net.after(s, net.dve)
        net.act(s.activation(at[:, :, :], at[:, :, :], ACT.Exp))
        net.after(v, net.act)
        net.dve(v.tensor_reduce(mx[:, :], at[:, :, :], AX.X, ALU.add))
        net.dve(v.reciprocal(mx[:, :], mx[:, :]))
        net.dve(v.tensor_scalar(mx[:, :], mx[:, :], 3.0, None, ALU.mult))
        net.dve(v.tensor_tensor(at[:, :, :], at[:, :, :], by_node(mx, 3), ALU.mult))
        for i in range(3):
            net.dve(v.tensor_tensor(tmp[:, :, :], own[:, :, i * D:(i + 1) * D],
                                    at[:, :, i:i + 1].to_broadcast([P, NB, D]), ALU.mult))
            net.dve(v.tensor_tensor(net.x[:, :, :], net.x[:, :, :], tmp[:, :, :], ALU.add))
        net.after(nc.sync, net.dve)
        net.load(node_view(net.out), net.x[:, :, :])


def build(nc, a, out):
    net = Net(nc, a)
    net.out = out
    dram = lambda name, shape: nc.dram_tensor(name, shape, F32).ap()
    net.lo_d = dram("lo_d", [EP + G * P])
    net.h0_d, h1_d = dram("h0_d", [NPAD, D]), dram("h1_d", [NPAD, D])
    net.rows_d = dram("rows_d", [EP + G * P, ROW])
    net.weight_d = dram("weight_d", [EP, HEADS])
    rel_d = [dram(f"rel{i}_d", [NPAD, RELS * D]) for i in range(2)]
    ch_d = dram("ch_d", [NPAD, 2 * D])
    net.spare_d = dram("spare_d", [2, P, 1])
    v = nc.vector
    with Mem(nc, "all", "right") as m:
        make_constants(net, m)
        with Mem(nc, "prep") as t:
            net.x = t.sb("x", [P, NB, D])
            net.load(net.x[:, :, :], node_view(a["x"]))
            net.after(v, net.sp)
            layer_norm(net, t, net.h0_d)
        with Mem(nc, "edge") as e:
            index_lists(net, m, e)
            histogram_src(net, e)
            b128, tiles = item_list(net, e, net.start_src, SPAN, WKS)
            both = e.sb("both", [P, 2, WKS], I32)
            net.dve(v.tensor_copy(both[:, 0, :], b128[:, :]))
            net.dve(v.tensor_copy(both[:, 1, :], tiles[:, :]))
            net.row_bsrc = to_rows(net, m, "row_bsrc", both[:, 0, :], I32, False)
            net.row_tsrc = to_rows(net, m, "row_tsrc", both[:, 1, :], I32, False)
            net.bsrc = to_rows(net, m, "bsrc", b128[:, :], F32, True)
            nc.all_engine_barrier()
            edge_pass(net, e)
        edge_softmax(net, m)
        with Mem(nc, "net") as t:
            net.x = t.sb("x", [P, NB, D])
            acc = t.sb("acc", [P, NB * P])
            bias = t.sb("bias", [P, D])
            net.norm, net.rdeg = t.sb("norm", [P, NB]), t.sb("rdeg", [P, NB])
            net.load(net.x[:, :, :], node_view(a["x"]))
            net.load(bias[:, :], a["bias"].partition_broadcast(P))
            net.after(v, net.sp)
            attention_sum(net, acc)
            net.dve(v.scalar_tensor_tensor(net.x[:, :, :], by_block(acc)[:, :, 0:D], 1.0 / HEADS,
                                           net.x[:, :, :], ALU.mult, ALU.add))
            net.dve(v.tensor_tensor(net.x[:, :, :], net.x[:, :, :],
                                    bias[:, None, :].to_broadcast([P, NB, D]), ALU.add))
            with Mem(nc, "l1") as n:
                layer_norm(net, n, h1_d)
            gather_sum(net, "l1s", h1_d, net.gsrc, acc, D, ones=True)
            net.dve(v.tensor_tensor(net.x[:, :, :], net.x[:, :, :], by_block(acc)[:, :, 0:D], ALU.add))
            net.dve(v.tensor_scalar(net.norm[:, :], by_block(acc)[:, :, D], 1.0, None, ALU.max))
            net.dve(v.reciprocal(net.rdeg[:, :], net.norm[:, :]))
            net.after(nc.scalar, net.dve)
            net.act(nc.scalar.activation(net.norm[:, :], net.norm[:, :], ACT.Sqrt))
            net.after(v, net.act)
            net.dve(v.reciprocal(net.norm[:, :], net.norm[:, :]))
            with Mem(nc, "l2") as n:
                h = layer_norm(net, n, None)
                for i in range(2):
                    relation_table(net, f"l2t{i}", h, a[f"W{i + 1}"], rel_d[i])
                    relation_layer(net, f"l2s{i}", rel_d[i], acc, h)
                net.dve(v.tensor_tensor(net.x[:, :, :], net.x[:, :, :], h[:, 0:NB, :], ALU.add))
            own = t.sb("own", [P, NB, 3 * D])
            with Mem(nc, "l3") as n:
                channel_tables(net, layer_norm(net, n, None), own, ch_d)
            gather_sum(net, "l3s", ch_d, net.gsrc, acc, 2 * D)
            channel_mix(net, acc, own)


def pad_to(a, n, fill=0):
    out = np.full((n,) + a.shape[1:], fill, a.dtype)
    out[:a.shape[0]] = a
    return out


def kernel(**inputs):
    from concourse.bass_utils import run_bass_kernel_spmd

    i = {k: np.asarray(v) for k, v in inputs.items()}
    arrays = {
        "x": pad_to(i["x"], NPAD), "src": pad_to(i["src"], EP + G * P, PAD_NODE), "dst": pad_to(i["dst"], EP, PAD_NODE),
        "rel": pad_to(i["edge_type_24"], EP),
        "edge_t": np.ascontiguousarray(pad_to(i["edge_attr_64"], EP + G * P).T),
        "W": i["L0_gnn_W"], "att": i["L0_gnn_att"][0], "bias": i["L0_gnn_bias"],
        "gamma": i["L0_gnn_bn_gamma"], "beta": i["L0_gnn_bn_beta"],
        "W1": i["L2_gnn_W1"], "W2": i["L2_gnn_W2"], "W_att": i["L3_gnn_W_att"],
    }
    for name in ("self", "self_high", "id", "neigh", "neigh_high"):
        arrays["Wt_" + name] = np.ascontiguousarray(i["L3_gnn_W_" + name].T)
        arrays["b_" + name] = i["L3_gnn_b_" + name]
    for name in ("low", "high", "mlp"):
        arrays["att_" + name] = i["L3_gnn_w_att_" + name][0]
    nc = bass.Bass("TRN2", target_bir_lowering=False, num_devices=1)
    args = {k: nc.dram_tensor(f"in_{k}", v.shape, mybir.dt.from_np(v.dtype), kind="ExternalInput").ap()
            for k, v in arrays.items()}
    out = nc.dram_tensor("out", (NPAD, D), F32, kind="ExternalOutput").ap()
    build(nc, args, out)
    res = run_bass_kernel_spmd(nc, [{f"in_{k}": v for k, v in arrays.items()}], core_ids=[0]).results[0]
    return res["out"][:N]
```
